# Optimizing a Trainium2 kernel written in Bass

```python
import numpy as np
import jax
import jax.numpy as jnp

def _softmax(x, axis=-1):
    return jax.nn.softmax(x, axis=axis)

def _gelu(x):
    return jax.nn.gelu(x, approximate=True)

def _silu(x):
    return jax.nn.silu(x)

def _sigmoid(x):
    return jax.nn.sigmoid(x)

def _layernorm(x, axis=-1, eps=1e-05):
    m = jnp.mean(x, axis=axis, keepdims=True)
    v = jnp.var(x, axis=axis, keepdims=True)
    return (x - m) / jnp.sqrt(v + eps)

def _scatter_add(tgt, idx, src, axis=0):
    return tgt.at[idx].add(src)

def _segment_sum(src, seg, n):
    return jax.ops.segment_sum(src, seg, n)
kernel_name = 'mk_xattn_seq_d4_seqx_r4_8c0454'

def setup_inputs(seed: int=0):
    np.random.seed(seed)
    _w = jnp.asarray

    def _rec_inputs():
        import jax
        import jax.numpy as jnp
        _rk = jax.random.key(seed)
        x = 7.22e-05 + 1 * jax.random.normal(jax.random.fold_in(_rk, 1), (32, 256, 256), jnp.float32)
        _lenS = 256 - jax.random.randint(jax.random.fold_in(_rk, 7), (32,), 0, max(1, 256 // 4) + 1, jnp.int32)
        _lenS2 = 120 - jax.random.randint(jax.random.fold_in(_rk, 8), (32,), 0, max(1, 120 // 4) + 1, jnp.int32)
        _ctx_1024P = jax.random.normal(jax.random.fold_in(_rk, 11), (32, 16, 256), jnp.float32)
        _ctx_1024c = jax.random.dirichlet(jax.random.fold_in(_rk, 511), 0.3 * jnp.ones((16,), jnp.float32), (32, 120))
        _ctx_1024t = jnp.einsum('bsk,bkd->bsd', _ctx_1024c, _ctx_1024P)
        _ctx_1024t = _ctx_1024t * jax.lax.rsqrt(jnp.mean(jnp.square(_ctx_1024t)) + 1e-12) * 0.953939
        ctx_1024 = -0.000514642 + 1.00011 * (_ctx_1024t + 0.3 * jax.random.normal(jax.random.fold_in(_rk, 611), (32, 120, 256), jnp.float32))
        _validS = jnp.arange(256)[None, :] < _lenS[:, None]
        _validS2 = jnp.arange(120)[None, :] < _lenS2[:, None]
        _causal = jnp.tril(jnp.ones((256, 256), dtype=bool))
        mask_SxS_ik1 = jnp.where(jnp.broadcast_to(_validS[0:1, :], (256, 256)), 1, 0).astype(jnp.int32)
        mask_BxSxS2_bk1 = jnp.broadcast_to(_validS2[:, None, :], (32, 256, 120))
        return (x, ctx_1024, mask_SxS_ik1, mask_BxSxS2_bk1)
    x, ctx_1024, mask_SxS_ik1, mask_BxSxS2_bk1 = _rec_inputs()

    def _L0_xattn_setup():
        import jax, jax.numpy as jnp
        import numpy as np
        import math
        B, T, C = (8, 256, 256)
        H = 16
        D = C // H
        TI = 64
        FF = 4 * C
        EPS = 1e-05

        def _ln(x, g, b):
            mu = jnp.mean(x, axis=-1, keepdims=True)
            var = jnp.mean(jnp.square(x - mu), axis=-1, keepdims=True)
            return (x - mu) * jax.lax.rsqrt(var + EPS) * g + b

        def _gelu_tanh(x):
            return jax.nn.gelu(x, approximate=True)

        def _heads(t):
            return t.reshape(t.shape[0], t.shape[1], H, D).transpose(0, 2, 1, 3)

        def _merge(t):
            return t.transpose(0, 2, 1, 3).reshape(t.shape[0], t.shape[2], C)
        key = jax.random.key(seed)
        ks = jax.random.split(key, 16)
        s = 0.02
        inp = {'x': jax.random.normal(ks[0], (B, T, C), jnp.float32), 'x_img_feats': jax.random.normal(ks[1], (B, TI, C), jnp.float32), 'ln1_g': jnp.ones((C,), jnp.float32), 'ln1_b': jnp.zeros((C,), jnp.float32), 'ln2_g': jnp.ones((C,), jnp.float32), 'ln2_b': jnp.zeros((C,), jnp.float32), 'W_attn': jax.random.normal(ks[2], (C, 3 * C), jnp.float32) * s, 'b_attn': jnp.zeros((3 * C,), jnp.float32), 'W_aproj': jax.random.normal(ks[3], (C, C), jnp.float32) * s, 'b_aproj': jnp.zeros((C,), jnp.float32), 'Wq': jax.random.normal(ks[4], (C, C), jnp.float32) * s, 'bq': jnp.zeros((C,), jnp.float32), 'Wk': jax.random.normal(ks[5], (C, C), jnp.float32) * s, 'bk': jnp.zeros((C,), jnp.float32), 'Wv': jax.random.normal(ks[6], (C, C), jnp.float32) * s, 'bv': jnp.zeros((C,), jnp.float32), 'Wcproj': jax.random.normal(ks[7], (C, C), jnp.float32) * s, 'bcproj': jnp.zeros((C,), jnp.float32), 'W_fc': jax.random.normal(ks[8], (C, FF), jnp.float32) * s, 'b_fc': jnp.zeros((FF,), jnp.float32), 'W_mproj': jax.random.normal(ks[9], (FF, C), jnp.float32) * s, 'b_mproj': jnp.zeros((C,), jnp.float32)}
        return inp
    _L0_xattn_all = _L0_xattn_setup()
    _L0_xattn_in = {k: v for k, v in _L0_xattn_all.items() if k in ('ln1_g', 'ln1_b', 'ln2_g', 'ln2_b', 'W_attn', 'b_attn', 'W_aproj', 'b_aproj', 'Wq', 'bq', 'Wk', 'bk', 'Wv', 'bv', 'Wcproj', 'bcproj', 'W_fc', 'b_fc', 'W_mproj', 'b_mproj')}
    del _L0_xattn_all

    def _L1_xattn_setup():
        import jax, jax.numpy as jnp
        import numpy as np
        D_MODEL = 256
        N_HEAD = 16
        D_FF = 1024
        EPS = 1e-05

        def _linear(x, w, b):
            return jnp.einsum('bli,io->blo', x, w) + b

        def _layernorm(x, g, b):
            mu = jnp.mean(x, -1, keepdims=True)
            var = jnp.mean(jnp.square(x - mu), -1, keepdims=True)
            return (x - mu) * jax.lax.rsqrt(var + EPS) * g + b

        def _attention(q, k, v, mask):
            B, Lq, D = q.shape
            H = N_HEAD
            hd = D // H
            qh = q.reshape(B, Lq, H, hd)
            kh = k.reshape(B, k.shape[1], H, hd)
            vh = v.reshape(B, v.shape[1], H, hd)
            scores = jnp.einsum('bqhd,bkhd->bhqk', qh, kh) / jnp.sqrt(jnp.float32(hd)).astype(q.dtype)
            if mask is not None:
                scores = jnp.where(mask[None, None] != 0, jnp.finfo(scores.dtype).min, scores)
            p = jax.nn.softmax(scores, axis=-1)
            out = jnp.einsum('bhqk,bkhd->bqhd', p, vh).reshape(B, Lq, D)
            return out
        key = jax.random.key(seed)
        ks = jax.random.split(key, 32)
        B, L, S, D, F = (2, 512, 512, D_MODEL, D_FF)
        std = 0.02
        inp = {'tgt': jax.random.normal(ks[0], (B, L, D), jnp.float32), 'memory': jax.random.normal(ks[1], (B, S, D), jnp.float32), 'tgt_mask': jnp.triu(jnp.ones((L, L), jnp.int32), k=1)}
        names = ['q', 'k', 'v', 'o', 'cq', 'ck', 'cv', 'co']
        for i, n in enumerate(names):
            inp[n + '_w'] = jax.random.normal(ks[2 + i], (D, D), jnp.float32) * std
            inp[n + '_b'] = jnp.zeros((D,), jnp.float32)
        inp['lin1_w'] = jax.random.normal(ks[12], (D, F), jnp.float32) * std
        inp['lin1_b'] = jnp.zeros((F,), jnp.float32)
        inp['lin2_w'] = jax.random.normal(ks[13], (F, D), jnp.float32) * std
        inp['lin2_b'] = jnp.zeros((D,), jnp.float32)
        for i, n in enumerate(['ln1', 'ln2', 'ln3']):
            inp[n + '_g'] = jnp.ones((D,), jnp.float32)
            inp[n + '_b'] = jnp.zeros((D,), jnp.float32)
        return inp
    _L1_xattn_all = _L1_xattn_setup()
    _L1_xattn_in = {k: v for k, v in _L1_xattn_all.items() if k in ('q_w', 'q_b', 'k_w', 'k_b', 'v_w', 'v_b', 'o_w', 'o_b', 'cq_w', 'cq_b', 'ck_w', 'ck_b', 'cv_w', 'cv_b', 'co_w', 'co_b', 'lin1_w', 'lin1_b', 'lin2_w', 'lin2_b', 'ln1_g', 'ln1_b', 'ln2_g', 'ln2_b', 'ln3_g', 'ln3_b')}
    del _L1_xattn_all

    def _L2_xattn_setup():
        import jax, jax.numpy as jnp
        import numpy as np
        B, S, D, H = (2, 512, 256, 16)
        HD = D // H
        EPS = 1e-05
        key = jax.random.key(seed)
        ks = jax.random.split(key, 9)
        q = jax.random.normal(ks[0], (B, S, D), dtype=jnp.float32)
        k = jax.random.normal(ks[1], (B, S, D), dtype=jnp.float32)
        v = jax.random.normal(ks[2], (B, S, D), dtype=jnp.float32)
        sc = 1.0 / np.sqrt(D)
        wq = jax.random.normal(ks[3], (D, D), dtype=jnp.float32) * sc
        wk = jax.random.normal(ks[4], (D, D), dtype=jnp.float32) * sc
        wv = jax.random.normal(ks[5], (D, D), dtype=jnp.float32) * sc
        wo = jax.random.normal(ks[6], (D, D), dtype=jnp.float32) * sc
        gamma = jnp.ones((D,), dtype=jnp.float32)
        beta = jnp.zeros((D,), dtype=jnp.float32)
        causal = ~jnp.tril(jnp.ones((S, S), dtype=bool))
        mask = jnp.broadcast_to(causal, (B, S, S))
        return {'q': q, 'k': k, 'v': v, 'wq': wq, 'wk': wk, 'wv': wv, 'wo': wo, 'gamma': gamma, 'beta': beta, 'mask': mask}
    _L2_xattn_all = _L2_xattn_setup()
    _L2_xattn_in = {k: v for k, v in _L2_xattn_all.items() if k in ('wq', 'wk', 'wv', 'wo', 'gamma', 'beta')}
    del _L2_xattn_all

    def _L3_xattn_setup():
        import jax, jax.numpy as jnp
        import numpy as np
        N_HEAD = 16
        D_MODEL = 256
        D_K = 64
        D_V = 64
        LN_EPS = 1e-06
        key = jax.random.key(seed)
        ks = jax.random.split(key, 8)
        B, S = (4, 512)
        q = jax.random.normal(ks[0], (B, S, D_MODEL), dtype=jnp.float32)
        k = jax.random.normal(ks[1], (B, S, D_MODEL), dtype=jnp.float32)
        v = jax.random.normal(ks[2], (B, S, D_MODEL), dtype=jnp.float32)
        sc = 1.0 / np.sqrt(D_MODEL)
        w_q = jax.random.normal(ks[3], (D_MODEL, N_HEAD * D_K), dtype=jnp.float32) * sc
        w_k = jax.random.normal(ks[4], (D_MODEL, N_HEAD * D_K), dtype=jnp.float32) * sc
        w_v = jax.random.normal(ks[5], (D_MODEL, N_HEAD * D_V), dtype=jnp.float32) * sc
        w_fc = jax.random.normal(ks[6], (N_HEAD * D_V, D_MODEL), dtype=jnp.float32) * sc
        ln_gamma = jnp.ones((D_MODEL,), dtype=jnp.float32)
        ln_beta = jnp.zeros((D_MODEL,), dtype=jnp.float32)
        return {'q': q, 'k': k, 'v': v, 'w_q': w_q, 'w_k': w_k, 'w_v': w_v, 'w_fc': w_fc, 'ln_gamma': ln_gamma, 'ln_beta': ln_beta}
    _L3_xattn_all = _L3_xattn_setup()
    _L3_xattn_in = {k: v for k, v in _L3_xattn_all.items() if k in ('w_q', 'w_k', 'w_v', 'w_fc', 'ln_gamma', 'ln_beta')}
    del _L3_xattn_all
    return {'x': x, 'ctx_1024': ctx_1024, 'mask_SxS_ik1': mask_SxS_ik1, 'mask_BxSxS2_bk1': mask_BxSxS2_bk1, 'L0_xattn_ln1_g': _L0_xattn_in['ln1_g'], 'L0_xattn_ln1_b': _L0_xattn_in['ln1_b'], 'L0_xattn_ln2_g': _L0_xattn_in['ln2_g'], 'L0_xattn_ln2_b': _L0_xattn_in['ln2_b'], 'L0_xattn_W_attn': _L0_xattn_in['W_attn'], 'L0_xattn_b_attn': _L0_xattn_in['b_attn'], 'L0_xattn_W_aproj': _L0_xattn_in['W_aproj'], 'L0_xattn_b_aproj': _L0_xattn_in['b_aproj'], 'L0_xattn_Wq': _L0_xattn_in['Wq'], 'L0_xattn_bq': _L0_xattn_in['bq'], 'L0_xattn_Wk': _L0_xattn_in['Wk'], 'L0_xattn_bk': _L0_xattn_in['bk'], 'L0_xattn_Wv': _L0_xattn_in['Wv'], 'L0_xattn_bv': _L0_xattn_in['bv'], 'L0_xattn_Wcproj': _L0_xattn_in['Wcproj'], 'L0_xattn_bcproj': _L0_xattn_in['bcproj'], 'L0_xattn_W_fc': _L0_xattn_in['W_fc'], 'L0_xattn_b_fc': _L0_xattn_in['b_fc'], 'L0_xattn_W_mproj': _L0_xattn_in['W_mproj'], 'L0_xattn_b_mproj': _L0_xattn_in['b_mproj'], 'L1_xattn_q_w': _L1_xattn_in['q_w'], 'L1_xattn_q_b': _L1_xattn_in['q_b'], 'L1_xattn_k_w': _L1_xattn_in['k_w'], 'L1_xattn_k_b': _L1_xattn_in['k_b'], 'L1_xattn_v_w': _L1_xattn_in['v_w'], 'L1_xattn_v_b': _L1_xattn_in['v_b'], 'L1_xattn_o_w': _L1_xattn_in['o_w'], 'L1_xattn_o_b': _L1_xattn_in['o_b'], 'L1_xattn_cq_w': _L1_xattn_in['cq_w'], 'L1_xattn_cq_b': _L1_xattn_in['cq_b'], 'L1_xattn_ck_w': _L1_xattn_in['ck_w'], 'L1_xattn_ck_b': _L1_xattn_in['ck_b'], 'L1_xattn_cv_w': _L1_xattn_in['cv_w'], 'L1_xattn_cv_b': _L1_xattn_in['cv_b'], 'L1_xattn_co_w': _L1_xattn_in['co_w'], 'L1_xattn_co_b': _L1_xattn_in['co_b'], 'L1_xattn_lin1_w': _L1_xattn_in['lin1_w'], 'L1_xattn_lin1_b': _L1_xattn_in['lin1_b'], 'L1_xattn_lin2_w': _L1_xattn_in['lin2_w'], 'L1_xattn_lin2_b': _L1_xattn_in['lin2_b'], 'L1_xattn_ln1_g': _L1_xattn_in['ln1_g'], 'L1_xattn_ln1_b': _L1_xattn_in['ln1_b'], 'L1_xattn_ln2_g': _L1_xattn_in['ln2_g'], 'L1_xattn_ln2_b': _L1_xattn_in['ln2_b'], 'L1_xattn_ln3_g': _L1_xattn_in['ln3_g'], 'L1_xattn_ln3_b': _L1_xattn_in['ln3_b'], 'L2_xattn_wq': _L2_xattn_in['wq'], 'L2_xattn_wk': _L2_xattn_in['wk'], 'L2_xattn_wv': _L2_xattn_in['wv'], 'L2_xattn_wo': _L2_xattn_in['wo'], 'L2_xattn_gamma': _L2_xattn_in['gamma'], 'L2_xattn_beta': _L2_xattn_in['beta'], 'L3_xattn_w_q': _L3_xattn_in['w_q'], 'L3_xattn_w_k': _L3_xattn_in['w_k'], 'L3_xattn_w_v': _L3_xattn_in['w_v'], 'L3_xattn_w_fc': _L3_xattn_in['w_fc'], 'L3_xattn_ln_gamma': _L3_xattn_in['ln_gamma'], 'L3_xattn_ln_beta': _L3_xattn_in['ln_beta']}

def reference(x, ctx_1024, mask_SxS_ik1, mask_BxSxS2_bk1, L0_xattn_ln1_g, L0_xattn_ln1_b, L0_xattn_ln2_g, L0_xattn_ln2_b, L0_xattn_W_attn, L0_xattn_b_attn, L0_xattn_W_aproj, L0_xattn_b_aproj, L0_xattn_Wq, L0_xattn_bq, L0_xattn_Wk, L0_xattn_bk, L0_xattn_Wv, L0_xattn_bv, L0_xattn_Wcproj, L0_xattn_bcproj, L0_xattn_W_fc, L0_xattn_b_fc, L0_xattn_W_mproj, L0_xattn_b_mproj, L1_xattn_q_w, L1_xattn_q_b, L1_xattn_k_w, L1_xattn_k_b, L1_xattn_v_w, L1_xattn_v_b, L1_xattn_o_w, L1_xattn_o_b, L1_xattn_cq_w, L1_xattn_cq_b, L1_xattn_ck_w, L1_xattn_ck_b, L1_xattn_cv_w, L1_xattn_cv_b, L1_xattn_co_w, L1_xattn_co_b, L1_xattn_lin1_w, L1_xattn_lin1_b, L1_xattn_lin2_w, L1_xattn_lin2_b, L1_xattn_ln1_g, L1_xattn_ln1_b, L1_xattn_ln2_g, L1_xattn_ln2_b, L1_xattn_ln3_g, L1_xattn_ln3_b, L2_xattn_wq, L2_xattn_wk, L2_xattn_wv, L2_xattn_wo, L2_xattn_gamma, L2_xattn_beta, L3_xattn_w_q, L3_xattn_w_k, L3_xattn_w_v, L3_xattn_w_fc, L3_xattn_ln_gamma, L3_xattn_ln_beta):
    import jax
    import jax.numpy as jnp

    def _L0_xattn_ref(x, x_img_feats, ln1_g, ln1_b, ln2_g, ln2_b, W_attn, b_attn, W_aproj, b_aproj, Wq, bq, Wk, bk, Wv, bv, Wcproj, bcproj, W_fc, b_fc, W_mproj, b_mproj):
        import jax, jax.numpy as jnp
        import numpy as np
        import math
        B, T, C = (8, 256, 256)
        H = 16
        D = C // H
        TI = 64
        FF = 4 * C
        EPS = 1e-05

        def _ln(x, g, b):
            mu = jnp.mean(x, axis=-1, keepdims=True)
            var = jnp.mean(jnp.square(x - mu), axis=-1, keepdims=True)
            return (x - mu) * jax.lax.rsqrt(var + EPS) * g + b

        def _gelu_tanh(x):
            return jax.nn.gelu(x, approximate=True)

        def _heads(t):
            return t.reshape(t.shape[0], t.shape[1], H, D).transpose(0, 2, 1, 3)

        def _merge(t):
            return t.transpose(0, 2, 1, 3).reshape(t.shape[0], t.shape[2], C)
        scale = 1.0 / math.sqrt(D)
        h = _ln(x, ln1_g, ln1_b)
        qkv = h @ W_attn + b_attn
        q, k, v = jnp.split(qkv, 3, axis=-1)
        q, k, v = (_heads(q), _heads(k), _heads(v))
        att = jnp.einsum('bhtd,bhsd->bhts', q, k) * scale
        causal = jnp.tril(jnp.ones((T, T), bool))
        att = jnp.where(causal[None, None], att, -jnp.inf)
        att = jax.nn.softmax(att, axis=-1)
        sa = _merge(jnp.einsum('bhts,bhsd->bhtd', att, v)) @ W_aproj + b_aproj
        x = x + sa
        ht = _ln(x, ln1_g, ln1_b)
        q = _heads(ht @ Wq + bq)
        k = _heads(x_img_feats @ Wk + bk)
        v = _heads(x_img_feats @ Wv + bv)
        catt = jax.nn.softmax(jnp.einsum('bhtd,bhsd->bhts', q, k) * scale, axis=-1)
        ca = _merge(jnp.einsum('bhts,bhsd->bhtd', catt, v)) @ Wcproj + bcproj
        x = x + ca
        h2 = _ln(x, ln2_g, ln2_b)
        x = x + _gelu_tanh(h2 @ W_fc + b_fc) @ W_mproj + b_mproj
        return x

    def _L1_xattn_ref(tgt, memory, tgt_mask, q_w, q_b, k_w, k_b, v_w, v_b, o_w, o_b, cq_w, cq_b, ck_w, ck_b, cv_w, cv_b, co_w, co_b, lin1_w, lin1_b, lin2_w, lin2_b, ln1_g, ln1_b, ln2_g, ln2_b, ln3_g, ln3_b):
        import jax, jax.numpy as jnp
        import numpy as np
        D_MODEL = 256
        N_HEAD = 16
        D_FF = 1024
        EPS = 1e-05

        def _linear(x, w, b):
            return jnp.einsum('bli,io->blo', x, w) + b

        def _layernorm(x, g, b):
            mu = jnp.mean(x, -1, keepdims=True)
            var = jnp.mean(jnp.square(x - mu), -1, keepdims=True)
            return (x - mu) * jax.lax.rsqrt(var + EPS) * g + b

        def _attention(q, k, v, mask):
            B, Lq, D = q.shape
            H = N_HEAD
            hd = D // H
            qh = q.reshape(B, Lq, H, hd)
            kh = k.reshape(B, k.shape[1], H, hd)
            vh = v.reshape(B, v.shape[1], H, hd)
            scores = jnp.einsum('bqhd,bkhd->bhqk', qh, kh) / jnp.sqrt(jnp.float32(hd)).astype(q.dtype)
            if mask is not None:
                scores = jnp.where(mask[None, None] != 0, jnp.finfo(scores.dtype).min, scores)
            p = jax.nn.softmax(scores, axis=-1)
            out = jnp.einsum('bhqk,bkhd->bqhd', p, vh).reshape(B, Lq, D)
            return out
        q = _linear(tgt, q_w, q_b)
        k = _linear(tgt, k_w, k_b)
        v = _linear(tgt, v_w, v_b)
        tgt2 = _linear(_attention(q, k, v, tgt_mask), o_w, o_b)
        x = _layernorm(tgt + tgt2, ln1_g, ln1_b)
        q = _linear(x, cq_w, cq_b)
        k = _linear(memory, ck_w, ck_b)
        v = _linear(memory, cv_w, cv_b)
        tgt2 = _linear(_attention(q, k, v, None), co_w, co_b)
        x = _layernorm(x + tgt2, ln2_g, ln2_b)
        tgt2 = _linear(jax.nn.relu(_linear(x, lin1_w, lin1_b)), lin2_w, lin2_b)
        x = _layernorm(x + tgt2, ln3_g, ln3_b)
        return x

    def _L2_xattn_ref(q, k, v, wq, wk, wv, wo, gamma, beta, mask):
        import jax, jax.numpy as jnp
        import numpy as np
        B, S, D, H = (2, 512, 256, 16)
        HD = D // H
        EPS = 1e-05
        Bq, Lq, _ = q.shape
        Lk = k.shape[1]
        qs = (q @ wq).reshape(Bq, Lq, H, HD).transpose(0, 2, 1, 3)
        ks_ = (k @ wk).reshape(Bq, Lk, H, HD).transpose(0, 2, 1, 3)
        vs = (v @ wv).reshape(Bq, Lk, H, HD).transpose(0, 2, 1, 3)
        scores = jnp.einsum('bhqd,bhkd->bhqk', qs, ks_) / jnp.sqrt(jnp.float32(HD))
        scores = jnp.where(mask[:, None, :, :], -jnp.inf, scores)
        attn_w = jax.nn.softmax(scores, axis=-1)
        attn = jnp.einsum('bhqk,bhkd->bhqd', attn_w, vs)
        attn = attn.transpose(0, 2, 1, 3).reshape(Bq, Lq, H * HD)
        out = attn @ wo + q
        mu = jnp.mean(out, axis=-1, keepdims=True)
        var = jnp.mean((out - mu) ** 2, axis=-1, keepdims=True)
        return (out - mu) / jnp.sqrt(var + EPS) * gamma + beta

    def _L3_xattn_ref(q, k, v, w_q, w_k, w_v, w_fc, ln_gamma, ln_beta):
        import jax, jax.numpy as jnp
        import numpy as np
        N_HEAD = 16
        D_MODEL = 256
        D_K = 64
        D_V = 64
        LN_EPS = 1e-06
        B, Sq, _ = q.shape
        Sk = k.shape[1]
        residual = q
        qh = (q @ w_q).reshape(B, Sq, N_HEAD, D_K).transpose(0, 2, 1, 3)
        kh = (k @ w_k).reshape(B, Sk, N_HEAD, D_K).transpose(0, 2, 1, 3)
        vh = (v @ w_v).reshape(B, Sk, N_HEAD, D_V).transpose(0, 2, 1, 3)
        scale = jnp.asarray(D_K ** 0.5, dtype=q.dtype)
        scores = jnp.einsum('bhqd,bhkd->bhqk', qh, kh) / scale
        attn = jax.nn.softmax(scores, axis=-1)
        ctx = jnp.einsum('bhqk,bhkd->bhqd', attn, vh)
        ctx = ctx.transpose(0, 2, 1, 3).reshape(B, Sq, N_HEAD * D_V)
        out = ctx @ w_fc + residual
        mean = out.mean(axis=-1, keepdims=True)
        var = out.var(axis=-1, keepdims=True)
        out = (out - mean) * jax.lax.rsqrt(var + LN_EPS) * ln_gamma + ln_beta
        return out
    x = _L0_xattn_ref(x, ctx_1024, L0_xattn_ln1_g, L0_xattn_ln1_b, L0_xattn_ln2_g, L0_xattn_ln2_b, L0_xattn_W_attn, L0_xattn_b_attn, L0_xattn_W_aproj, L0_xattn_b_aproj, L0_xattn_Wq, L0_xattn_bq, L0_xattn_Wk, L0_xattn_bk, L0_xattn_Wv, L0_xattn_bv, L0_xattn_Wcproj, L0_xattn_bcproj, L0_xattn_W_fc, L0_xattn_b_fc, L0_xattn_W_mproj, L0_xattn_b_mproj)
    x = _L1_xattn_ref(x, ctx_1024, mask_SxS_ik1, L1_xattn_q_w, L1_xattn_q_b, L1_xattn_k_w, L1_xattn_k_b, L1_xattn_v_w, L1_xattn_v_b, L1_xattn_o_w, L1_xattn_o_b, L1_xattn_cq_w, L1_xattn_cq_b, L1_xattn_ck_w, L1_xattn_ck_b, L1_xattn_cv_w, L1_xattn_cv_b, L1_xattn_co_w, L1_xattn_co_b, L1_xattn_lin1_w, L1_xattn_lin1_b, L1_xattn_lin2_w, L1_xattn_lin2_b, L1_xattn_ln1_g, L1_xattn_ln1_b, L1_xattn_ln2_g, L1_xattn_ln2_b, L1_xattn_ln3_g, L1_xattn_ln3_b)
    x = _L2_xattn_ref(x, ctx_1024, ctx_1024, L2_xattn_wq, L2_xattn_wk, L2_xattn_wv, L2_xattn_wo, L2_xattn_gamma, L2_xattn_beta, mask_BxSxS2_bk1)
    x = _L3_xattn_ref(x, ctx_1024, ctx_1024, L3_xattn_w_q, L3_xattn_w_k, L3_xattn_w_v, L3_xattn_w_fc, L3_xattn_ln_gamma, L3_xattn_ln_beta)
    return x

_drawn_inputs = setup_inputs


def setup_inputs(seed=0):
    import zlib

    import numpy as np

    out = dict(_drawn_inputs(seed))
    spreads = {'L0_xattn_ln1_g': (1.0, 0.6),
     'L0_xattn_ln1_b': (0.0, 0.8),
     'L0_xattn_ln2_g': (1.0, 0.6),
     'L0_xattn_ln2_b': (0.0, 0.8),
     'L0_xattn_b_attn': (0.0, 0.414),
     'L0_xattn_b_aproj': (0.0, 0.1),
     'L0_xattn_bq': (0.0, 2.0),
     'L0_xattn_bk': (0.0, 2.0),
     'L0_xattn_bv': (0.0, 0.388),
     'L0_xattn_bcproj': (0.0, 0.1),
     'L0_xattn_b_fc': (0.0, 0.363),
     'L0_xattn_b_mproj': (0.0, 0.1),
     'L1_xattn_q_b': (0.0, 0.8),
     'L1_xattn_k_b': (0.0, 2.0),
     'L1_xattn_v_b': (0.0, 0.445),
     'L1_xattn_o_b': (0.0, 0.1),
     'L1_xattn_cq_b': (0.0, 2.0),
     'L1_xattn_ck_b': (0.0, 2.0),
     'L1_xattn_cv_b': (0.0, 0.43),
     'L1_xattn_co_b': (0.0, 0.1),
     'L1_xattn_lin1_b': (0.0, 0.292),
     'L1_xattn_lin2_b': (0.0, 0.1),
     'L1_xattn_ln1_g': (1.0, 0.2),
     'L1_xattn_ln1_b': (0.0, 0.1),
     'L1_xattn_ln2_g': (1.0, 0.2),
     'L1_xattn_ln2_b': (0.0, 0.1),
     'L1_xattn_ln3_g': (1.0, 0.2),
     'L1_xattn_ln3_b': (0.0, 0.1),
     'L2_xattn_gamma': (1.0, 0.2),
     'L2_xattn_beta': (0.0, 0.1),
     'L3_xattn_ln_gamma': (1.0, 0.2),
     'L3_xattn_ln_beta': (0.0, 0.1)}
    factors = {'L0_xattn_W_attn': 4.584,
     'L0_xattn_Wq': 8.0,
     'L0_xattn_Wk': 8.0,
     'L1_xattn_q_w': 8.0,
     'L1_xattn_k_w': 8.0,
     'L1_xattn_v_w': 3.168,
     'L1_xattn_cq_w': 8.0,
     'L1_xattn_ck_w': 8.0}
    for name, (base, spread) in spreads.items():
        noise = np.random.default_rng([zlib.crc32(name.encode()), seed]).standard_normal(out[name].shape)
        drawn = base * np.exp(spread * noise) if base else spread * noise
        out[name] = jnp.asarray(drawn.astype(out[name].dtype))
    for name, factor in factors.items():
        out[name] = (out[name] * factor).astype(out[name].dtype)
    return out
```

```python
from contextlib import ExitStack

import concourse.bass as bass
from concourse import mybir

ALU = mybir.AluOpType
ACT = mybir.ActivationFunctionType
AX_X = mybir.AxisListType.X
F32 = mybir.dt.float32
BF16 = mybir.dt.bfloat16
U8 = mybir.dt.uint8
I32 = mybir.dt.int32

P = 128
NB, T, C = 32, 256, 256
S2 = 120
H = 16
D = C // H
D3 = 64
FF = 4 * C
QT = T // P
FT = C // P
PAIR = 2
TURNS = NB // PAIR
HG = 4
G = H // HG
FT3 = H * D3 // P
PARTS = 3
Q_SLOTS = (0, 0, 0, 1, 1, 2)
K_SLOTS = (0, 1, 2, 0, 1, 0)
SLOTS = len(Q_SLOTS)
KS = SLOTS * D
BIG = 2.0 ** 100
GELU_A = 0.044715
GELU_C = (2.0 / 3.141592653589793) ** 0.5


class Att:

    def __init__(self, key, kind, q, k, v, o, bias="", masked=False, d=D, res="xb", v_bias=None):
        self.key, self.kind, self.masked, self.d, self.res = key, kind, masked, d, res
        self.q, self.k, self.v, self.o = q, k, v, o
        self.v_bias = v_bias
        self.cross = kind == "cross"
        self.nk = S2 if self.cross else T
        self.scale = float(d) ** -0.5

    def max_jobs(self):
        jobs = []
        for t in range(QT):
            nk = P if self.kind == "causal" and t == 0 else self.nk
            n = 4 if nk <= P else 2
            for h in range(0, H, n):
                jobs.append((t, list(range(h, h + n)), nk))
        return jobs

    def exp_units(self):
        n = 2 if self.cross else 1
        return [list(range(h, h + n)) for h in range(0, H, n)]


def att_units(s, a):
    u = []
    if a.d == D:
        u += [("project_q", s, a.key, a, 0), ("project_k", s, a.key, a, 0), ("project_v", s, a.key, a, 0)]
    else:
        u += [("project_q3", s, a.key, a, j) for j in range(FT3 // 2)]
        u += [("project_k3", s, a.key, a, j) for j in range(FT3 // 4)]
        u += [("project_v3", s, a.key, a, j) for j in range(2)]
    u += [("scores_max", s, a.key, a, j) for j in range(len(a.max_jobs()))]
    u += [("negate_max", s, a.key, a, 0)]
    n = len(a.exp_units())
    for j in range(n + 2):
        if j < n:
            u.append(("scores_exp", s, a.key, a, j))
        if j >= 2:
            u.append(("probs_v", s, a.key, a, j - 2))
    if a.d == D:
        u += [("normalise", s, a.key, a, j) for j in range(G // 2)]
    else:
        u += [("normalise3", s, a.key, a, j) for j in range(FT3 // 2)]
    return u + [("project_out", s, a.key, a, 0)]


LENGTH = {
    "context": 400, "stats": 300, "norm": 900, "turn": 900, "project_q": 2100, "project_k": 2100,
    "project_v": 2100, "project_q3": 2100, "project_k3": 2000, "project_v3": 2000, "scores_max": 550,
    "negate_max": 300, "scores_exp": 700, "probs_v": 500, "normalise": 1000, "normalise3": 1000,
    "project_out": 4200, "ff_in": 2100, "ff_mid": 100, "ff_out": 8300, "store": 0, "mask": 400, "final": 300,
}


def weave(a, b, lag):
    out, ta, tb = [], 0, lag
    a, b = list(a), list(b)
    while a or b:
        if a and (not b or ta <= tb):
            out.append(a.pop(0))
            ta += LENGTH[out[-1][0]]
        else:
            out.append(b.pop(0))
            tb += LENGTH[out[-1][0]]
    return out


class Count:

    def __init__(self, handle, tags, step=1):
        self.sem, self.tags, self.step = handle, tags, step
        self.at = {t: i for i, t in enumerate(tags)}
        assert len(self.at) == len(tags)

    def after(self, turn, tag):
        return 1 + turn * (self.step * len(self.tags)) + (self.at[tag] + 1) * self.step

    def before(self, turn):
        return 1 + turn * (self.step * len(self.tags))


def step_signals(u, act):
    kind, s, key, a, j = u
    t = (kind, s, key, j)
    sig = {}
    if kind in ("context", "norm", "turn", "project_q", "project_k", "project_q3", "project_k3", "scores_exp", "ff_in"):
        sig["a"] = [t]
    if kind in ("project_v", "project_v3", "scores_max", "negate_max", "normalise", "normalise3", "project_out",
                "ff_out", "mask"):
        sig["d"] = [t]
    if kind == "probs_v":
        heads = a.exp_units()[j]
        per = 8 if a.d == D else 4
        if (heads[-1] + 1) % per == 0:
            sig["o"] = [(kind, s, key, heads[-1] // per)]
        if a.d != D and heads[-1] == H - 1:
            sig["den"] = [t]
    if kind == "stats":
        sig["moments"] = sig["rstd"] = [t]
    if kind == "norm":
        sig["xhat"] = [t]
    if kind in ("norm", "turn", "final") and a.get("xb"):
        sig["xb"] = [t]
    if kind == "final":
        sig["xhat"] = [t]
    if kind in ("project_q", "project_k"):
        sig["hi"] = sig["mid"] = sig["rest"] = sig["lo"] = [t]
    if kind == "negate_max":
        sig["negmax"] = [t]
    if kind == "mask":
        sig["mask"] = [t]
    if kind == "ff_mid" and act == "gelu":
        sig["tanh"] = [t]
        sig["ff"] = [t]
    if kind == "ff_in" and act == "gelu":
        sig["poly"] = [t]
    return sig


def run_pass(nc, name, streams, res, act):
    units = weave(streams[0], streams[1], res["lag"])
    order = {k: [] for k in ("a", "d", "o", "den", "moments", "rstd", "xhat", "xb", "hi", "mid", "rest", "lo", "negmax",
                             "mask", "tanh", "ff", "poly")}
    for u in units:
        for k, tags in step_signals(u, act).items():
            order[k] += tags
    width = 512
    with ExitStack() as ctx:
        def sb(n, shape, dt=F32):
            return ctx.enter_context(nc.sbuf_tensor(f"{name}_{n}", shape, dt))

        def two(n, shape, dt=F32):
            return [sb(f"{n}{s}", shape, dt) for s in range(PAIR)]

        def sem(n):
            return ctx.enter_context(nc.semaphore(f"{name}_{n}"))

        wide = res["wide"]
        x_in = two("x_in", [P, QT, C])
        c_in = two("c_in", [S2, C])
        xb = two("xb", [P, QT, C])
        xn = two("xn", [P, QT, C])
        xh = two("xh", [P, QT, C])
        ht = two("ht", [P, FT, T])
        ct = two("ct", [P, FT, S2])
        kstack = two("kstack", [P, H * T if not wide else H * 128], BF16)
        qstack = two("qstack", [P, 8 * T])
        parts = two("parts", [P, 2, PARTS, FT, T], BF16)
        ot_raw = two("ot_raw", [P, (FT3 if wide else G) * T])
        v_aug = two("v_aug", [P, QT, H, 32])
        probs = two("probs", [P, 3, width])
        mx = two("mx", [P, QT, H])
        nmf = two("nmf", [P, QT, H])
        nm_parts = two("nm_parts", [P, QT, PARTS, H], BF16)
        nm_t = two("nm_t", [P, T], BF16)
        moments = two("moments", [P, QT, 6])
        meanvar = two("meanvar", [P, QT, 2])
        veps = two("veps", [P, QT])
        rstd = two("rstd", [P, QT])
        recip = sb("recip", [P, width])
        if wide:
            ot_n3 = two("ot_n3", [P, FT3, T])
            kmask3 = two("kmask3", [P, H, S2])
            v3 = two("v3", [S2, H * D3])
            rden = two("rden", [H, T])
            m_in = two("m_in", [P, QT, S2], U8)
            m_rows = two("m_rows", [P, QT, S2], BF16)
            m_cols = two("m_cols", [S2, T], BF16)
        q32 = [ot_raw[s][:, 0:512].rearrange("p (f t) -> p f t", f=FT) for s in range(PAIR)]
        k32 = [ot_raw[s][:, 512:1024].rearrange("p (f t) -> p f t", f=FT) for s in range(PAIR)]
        otr = [ot_raw[s][:, 0:G * T].rearrange("p (g t) -> p g t", g=G) for s in range(PAIR)]
        ot_n = two("ot_n", [P, G, T])
        qs = [qstack[s][:, :].bitcast(BF16).rearrange("p (h t) -> p h t", h=H) for s in range(PAIR)]
        ks = [kstack[s][:, :].rearrange("p (h t) -> p h t", h=H) for s in range(PAIR)]
        ffh = [qstack[s][:, :].rearrange("p (f t) -> p f t", f=8) for s in range(PAIR)]
        q3 = ffh
        if not wide:
            g32 = [kstack[s][:, :].bitcast(F32).rearrange("p (c x f t) -> p c x f t", c=2, x=2, f=2) for s in range(PAIR)]

        na = 2 if wide else 3
        bank_a = [ctx.enter_context(nc.psum_tensor(f"{name}_bank_a{i}", [P, 512], F32)) for i in range(na)]
        bank_d = [ctx.enter_context(nc.psum_tensor(f"{name}_bank_d{i}", [P, 512], F32)) for i in range(2)]
        bank_o = [ctx.enter_context(nc.psum_tensor(f"{name}_bank_o{i}", [P, 512], F32)) for i in range(3)]
        bank_den = ctx.enter_context(nc.psum_tensor(f"{name}_bank_den", [P, 512], F32)) if wide else None
        rings = {"a": bank_a, "d": bank_d, "o": bank_o, "den": [bank_den]}

        def counts(n, key, step=1):
            return Count(sem(n), order[key], step)

        full = {r: counts(f"{r}_full", r) for r in rings}
        done = {r: counts(f"{r}_done", r) for r in rings}
        a_full, d_full, o_full, den_full = full.values()
        a_done, d_done, o_done, den_done = done.values()
        moments_ready = counts("moments_ready", "moments")
        rstd_ready = counts("rstd_ready", "rstd")
        xhat_ready = counts("xhat_ready", "xhat")
        xb_ready = counts("xb_ready", "xb")
        hi_ready = counts("hi_ready", "hi")
        rest_ready = counts("rest_ready", "rest")
        mid_ready = counts("mid_ready", "mid")
        lo_ready = counts("lo_ready", "lo")
        negmax_ready = counts("negmax_ready", "negmax")
        mask_ready = counts("mask_ready", "mask")
        tanh_ready = counts("tanh_ready", "tanh")
        poly_ready = counts("poly_ready", "poly")
        ff_ready = counts("ff_ready", "ff")
        stacks, spilled = {}, {}
        for s in range(PAIR):
            for w in ("project_q", "project_k"):
                tags = [(k, s2, key, j) for (k, s2, key, a, j) in units if k == w and s2 == s]
                if tags:
                    stacks[w, s] = Count(sem(f"stack_{w[-1]}{s}"), tags, 16 * SLOTS)
                    spilled[w, s] = Count(sem(f"spilled_{w[-1]}{s}"), tags, 16 * PARTS)
        loaded = [Count(sem(f"loaded{s}"), ["x"], 16 * res["loads"]) for s in range(PAIR)]
        stored = [Count(sem(f"stored{s}"), ["x"], 16) for s in range(PAIR)]
        setup_dma, setup_v, setup_g = sem("setup_dma"), sem("setup_v"), sem("setup_g")
        dve_step, pool_step, settled = sem("dve_step"), sem("pool_step"), sem("settled")
        n_dve, n_pool = res["dve_steps"], res["pool_steps"]

        last_readers = res["x_readers"]

        block = ctx.enter_context(nc.Block())

        class Seen:

            def __init__(self):
                self.last = {}

            def new(self, count, tag=None):
                at = -1 if tag is None else count.at[tag]
                if self.last.get(id(count), -2) >= at:
                    return False
                self.last[id(count)] = at
                return True

        def settle(eng):
            eng.sem_inc(settled, 1)

        def slot_of(r, tag):
            return rings[r][full[r].at[tag] % len(rings[r])]

        @block.sync
        def _(sp):
            w = Seen()

            def load(turn, s):
                sp.dma_start(x_in[s][:, :, :], res["x"](turn, s)).then_inc(loaded[s].sem, 16)
                sp.dma_start(c_in[s][:, :], res["ctx"](turn, s)).then_inc(loaded[s].sem, 16)
                if wide:
                    sp.dma_start(m_in[s][:, :, :], res["mask"](turn, s)).then_inc(loaded[s].sem, 16)

            every = [*full.values(), *done.values(), *stacks.values(), *spilled.values(), *loaded, *stored,
                     moments_ready, rstd_ready, xhat_ready, xb_ready, hi_ready, rest_ready, mid_ready, lo_ready,
                     negmax_ready, mask_ready, tanh_ready, poly_ready, ff_ready]
            for count in every:
                sp.sem_inc(count.sem, 1)
            n = 0
            with nc.allow_non_contiguous_dma(reason="biases and gains by feature, a few hundred words once"):
                for dst, src in res["weight_loads"]:
                    sp.dma_start(dst, src).then_inc(setup_dma, 16)
                    n += 1
            assert n == res["n_setup"], n
            for s in range(PAIR):
                load(0, s)

            def turn_body(turn, last):
                w.last = {}
                for kind, s, key, a, j in units:
                    tag = (kind, s, key, j)
                    if kind in ("project_q", "project_k"):
                        i = 0 if kind == "project_q" else 1
                        nt = a.nk if i else T
                        done_before = stacks[kind, s]
                        if done_before.at[tag]:
                            if w.new(done_before, done_before.tags[done_before.at[tag] - 1]):
                                sp.wait_ge(done_before.sem, done_before.after(turn, done_before.tags[done_before.at[tag] - 1]))
                                sp.sem_inc(settled, 1)
                        else:
                            if w.new(done_before):
                                sp.wait_ge(done_before.sem, done_before.before(turn))
                                sp.sem_inc(settled, 1)
                        for part, ready in enumerate((hi_ready, mid_ready, lo_ready)):
                            if w.new(ready, tag):
                                sp.wait_ge(ready.sem, ready.after(turn, tag))
                                sp.sem_inc(settled, 1)
                            sp.dma_start(res["scratch"][s, i, part, :, :, 0:nt].rearrange("f p t -> p f t"),
                                         parts[s][:, i, part, :, 0:nt]).then_inc(spilled[kind, s].sem, 16)
                    if kind in ("project_k", "project_v"):
                        i = 0 if kind == "project_k" else 1
                        what = ("project_q", "project_k")[i]
                        nt = a.nk if i else T
                        stack = (qs, ks)[i][s]
                        if w.new(spilled[what, s], (what, s, key, 0)):
                            sp.wait_ge(spilled[what, s].sem, spilled[what, s].after(turn, (what, s, key, 0)))
                            sp.sem_inc(settled, 1)
                        for n, part in enumerate((Q_SLOTS, K_SLOTS)[i]):
                            src = res["scratch"][s, i, part, :, :, 0:nt].rearrange("f (h d) t -> d (f h) t", d=D)
                            sp.dma_start(stack[n * D:(n + 1) * D, :, 0:nt], src).then_inc(stacks[what, s].sem, 16)
                    if (kind, key) == res["prefetch_at"] and not last:
                        for count, t in last_readers(s, dict(xhat=xhat_ready, xb=xb_ready, a=a_full, ad=a_done,
                                                             d=d_done, mask=mask_ready)):
                            if w.new(count, t):
                                sp.wait_ge(count.sem, count.after(turn, t))
                                sp.sem_inc(settled, 1)
                        load(turn + 1, s)
                    if kind == "store":
                        if res["final_ln"]:
                            sp.wait_ge(xb_ready.sem, xb_ready.after(turn, ("final", s, "ln3", 0)))
                        else:
                            sp.wait_ge(d_done.sem, d_done.after(turn, ("ff_out", s, "ff", 0)))
                        sp.sem_inc(settled, 1)
                        sp.dma_start(res["out"](turn, s), (xb if wide or res["final_ln"] else xn)[s][:, :, :])\
                          .then_inc(stored[s].sem, 16)

            with sp.Fori(0, TURNS - 1) as turn:
                turn_body(turn, False)
            turn_body(TURNS - 1, True)
            for s in range(PAIR):
                sp.wait_ge(stored[s].sem, stored[s].before(TURNS))

        @block.gpsimd
        def _(g):
            w = Seen()
            k = [0]

            def link(ins):
                k[0] += 1
                ins.then_inc(setup_g, 1)

            for t, v in res["zero"]:
                link(nc.gpsimd.memset(t, v))
            for s in range(PAIR):
                link(nc.gpsimd.memset(v_aug[s][:, :, :, :], 0.0))
                link(nc.gpsimd.memset(nm_t[s][:, :], 0.0))
                if wide:
                    link(nc.gpsimd.memset(kmask3[s][:, :, :], 0.0))
            g.wait_ge(setup_g, k[0])
            for s in range(PAIR):
                link(nc.gpsimd.memset(v_aug[s][:, :, :, D:D + 1], 1.0))
            g.wait_ge(setup_g, k[0])
            g.wait_ge(setup_dma, 16 * res["n_setup"])
            for dst, x, y in res["sums"]:
                link(nc.gpsimd.tensor_tensor(dst, x, y, ALU.add))
            g.wait_ge(setup_g, k[0])
            res["setup_total"] = k[0]
            chain = [0]

            def step(ins, turn):
                chain[0] += 1
                ins.then_inc(pool_step, 1)
                g.wait_ge(pool_step, turn * n_pool + chain[0])

            def body(turn):
                w.last = {}
                chain[0] = 0
                for kind, s, key, a, j in units:
                    tag = (kind, s, key, j)
                    if kind == "stats":
                        if w.new(moments_ready, tag):
                            g.wait_ge(moments_ready.sem, moments_ready.after(turn, tag))
                        settle(g)
                        step(nc.gpsimd.tensor_scalar(veps[s][:, :], meanvar[s][:, :, 1], a["eps"], None, ALU.add), turn)
                        nc.gpsimd.tensor_tensor(rstd[s][:, :], veps[s][:, :], res["half"][:, 0:QT],
                                                                  ALU.pow).then_inc(rstd_ready.sem, 1)
                    if kind in ("norm", "turn", "final") and a.get("xb"):
                        how, src, m1, m2 = a["xb"]
                        if res["final_ln"]:
                            if w.new(stored[s]):
                                g.wait_ge(stored[s].sem, stored[s].before(turn))
                        if how == "add":
                            if src == "x_in":
                                if w.new(loaded[s], "x"):
                                    g.wait_ge(loaded[s].sem, loaded[s].after(turn, "x"))
                                x = x_in[s]
                            else:
                                x = xn[s]
                                if w.new(d_done, a["sum_tag"]):
                                    g.wait_ge(d_done.sem, d_done.after(turn, a["sum_tag"]))
                            ins = nc.gpsimd.tensor_tensor(xb[s][:, :, :], x[:, :, :],
                                                          m2[:, None, :].broadcast_to((P, QT, C)), ALU.add)
                            ins.then_inc(xb_ready.sem, 1)
                        else:
                            if w.new(xhat_ready, tag):
                                g.wait_ge(xhat_ready.sem, xhat_ready.after(turn, tag))
                            settle(g)
                            step(nc.gpsimd.tensor_tensor(xb[s][:, :, :], xh[s][:, :, :],
                                                         m1[:, None, :].broadcast_to((P, QT, C)), ALU.mult), turn)
                            nc.gpsimd.tensor_tensor(xb[s][:, :, :], xb[s][:, :, :],
                                                                    m2[:, None, :].broadcast_to((P, QT, C)), ALU.add).then_inc(xb_ready.sem, 1)
                    if kind in ("project_q", "project_k"):
                        i = 0 if kind == "project_q" else 1
                        nt = a.nk if i else T
                        x32 = (q32, k32)[i][s][:, :, 0:nt]
                        if w.new(mid_ready, tag):
                            g.wait_ge(mid_ready.sem, mid_ready.after(turn, tag))
                        nc.gpsimd.tensor_tensor(parts[s][:, i, 2, :, 0:nt], x32,
                                                                parts[s][:, i, 1, :, 0:nt], ALU.subtract).then_inc(lo_ready.sem, 1)
                assert chain[0] == n_pool, ("pool", name, chain[0])

            with g.Fori(0, TURNS) as turn:
                body(turn)

        @block.scalar
        def _(act_e):
            w = Seen()
            act_e.wait_ge(setup_dma, 16 * res["n_setup"])
            act_e.wait_ge(setup_g, res["n_setup_g"])

            def affine(out, in_, scale, bias):
                return nc.scalar.activation(out, in_, ACT.Identity, scale=scale, bias=bias)

            def body(turn):
                w.last = {}
                for kind, s, key, a, j in units:
                    tag = (kind, s, key, j)
                    if tag in a_full.at:
                        if w.new(a_full, tag):
                            act_e.wait_ge(a_full.sem, a_full.after(turn, tag))
                        bank = slot_of("a", tag)
                    if kind == "context":
                        nc.scalar.activation(ct[s][:, :, :], bank[:, 0:FT * S2].rearrange(
                            "p (f t) -> p f t", f=FT), ACT.Copy).then_inc(a_done.sem, 1)
                    elif kind == "norm":
                        for f in range(FT):
                            ins = affine(ht[s][:, f, :], bank[:, f * T:(f + 1) * T], a["g"][:, f:f + 1], a["b"][:, f:f + 1])
                        ins.then_inc(a_done.sem, 1)
                    elif kind == "turn":
                        nc.scalar.activation(ht[s][:, :, :], bank[:, :].rearrange(
                            "p (f t) -> p f t", f=FT), ACT.Copy).then_inc(a_done.sem, 1)
                    elif kind in ("project_q", "project_k"):
                        i = 0 if kind == "project_q" else 1
                        nt = a.nk if i else T
                        bias = (a.q, a.k)[i][1]
                        src = bank[:, 0:FT * nt].rearrange("p (f t) -> p f t", f=FT)
                        dst = (q32, k32)[i][s]
                        if bias is None:
                            ins = nc.scalar.activation(dst[:, :, 0:nt], src, ACT.Copy)
                        else:
                            for f in range(FT):
                                ins = nc.scalar.activation(dst[:, f, 0:nt], src[:, f, :], ACT.Identity,
                                                           bias=bias[:, f:f + 1])
                        ins.then_inc(a_done.sem, 1)
                    elif kind == "project_q3":
                        nc.scalar.activation(q3[s][:, 2 * j:2 * j + 2, :], bank[:, :].rearrange(
                            "p (f t) -> p f t", f=2), ACT.Copy).then_inc(a_done.sem, 1)
                    elif kind == "project_k3":
                        for odd in range(2):
                            r = slice(64 * odd, 64 * odd + 64)
                            ins = nc.scalar.activation(kmask3[s][r, 8 * j + odd:8 * j + 8:2, :],
                                                       bank[r, 0:4 * S2].rearrange("p (f t) -> p f t", f=4), ACT.Copy)
                        ins.then_inc(a_done.sem, 1)
                    elif kind == "scores_exp":
                        if a.cross:
                            n, rows = 2 * T, S2
                        else:
                            n, rows = (T + P if a.kind == "causal" else 2 * T), P
                        nc.scalar.activation(probs[s][0:rows, j % 3, 0:n], bank[0:rows, 0:n], ACT.Exp,
                                                              scale=a.scale).then_inc(a_done.sem, 1)
                    elif kind == "probs_v":
                        heads = a.exp_units()[j]
                        per = 8 if a.d == D else 4
                        if (heads[-1] + 1) % per == 0:
                            n = heads[-1] // per
                            ot = (kind, s, key, n)
                            if w.new(o_full, ot):
                                act_e.wait_ge(o_full.sem, o_full.after(turn, ot))
                            nc.scalar.activation(ot_raw[s][:, 512 * n:512 * n + 512],
                                                                  slot_of("o", ot)[:, :], ACT.Copy).then_inc(o_done.sem, 1)
                    elif kind == "ff_in":
                        for f in range(2):
                            b = a["b"][:, 2 * j + f:2 * j + f + 1]
                            src = bank[:, f * T:(f + 1) * T]
                            if act == "relu":
                                ins = nc.scalar.activation(ffh[s][:, 2 * j + f, :], src, ACT.Relu, bias=b)
                            else:
                                if f == 0 and j >= 2:
                                    if w.new(ff_ready, ("ff_mid", s, key, j - 2)):
                                        act_e.wait_ge(ff_ready.sem, ff_ready.after(turn, ("ff_mid", s, key, j - 2)))
                                nc.scalar.activation(g32[s][:, j % 2, 0, f, :], src, ACT.Identity, bias=b)
                                ins = nc.scalar.activation(g32[s][:, j % 2, 1, f, :], src, ACT.Square, bias=b)
                        ins.then_inc(a_done.sem, 1)
                    elif kind == "ff_mid" and act == "gelu":
                        if w.new(poly_ready, ("ff_in", s, key, j)):
                            act_e.wait_ge(poly_ready.sem, poly_ready.after(turn, ("ff_in", s, key, j)))
                        nc.scalar.activation(g32[s][:, j % 2, 1, :, :], g32[s][:, j % 2, 1, :, :],
                                                               ACT.Tanh, scale=GELU_C).then_inc(tanh_ready.sem, 1)

            with act_e.Fori(0, TURNS) as turn:
                body(turn)

        @block.vector
        def _(dve):
            w = Seen()
            dve.wait_ge(setup_dma, 16 * res["n_setup"])
            dve.wait_ge(setup_g, res["n_setup_g"])
            v = nc.vector
            chain = [0]
            k = 0
            for ins in res["dve_setup"](v):
                k += 1
                ins.then_inc(setup_v, 1)
            assert k == res["n_setup_v"]
            dve.wait_ge(setup_v, k)

            def step(ins, turn):
                chain[0] += 1
                ins.then_inc(dve_step, 1)
                dve.wait_ge(dve_step, turn * n_dve + chain[0])

            def body(turn):
                w.last = {}
                chain[0] = 0
                last_use = None
                for kind, s, key, a, j in units:
                    tag = (kind, s, key, j)
                    if kind == "stats":
                        if a["src"] == "x_in":
                            if w.new(loaded[s], "x"):
                                dve.wait_ge(loaded[s].sem, loaded[s].after(turn, "x"))
                        x = x_in[s] if a["src"] == "x_in" else xn[s]
                        for t in range(QT):
                            ins = v.bn_stats(moments[s][:, t, :], x[:, t, :])
                        step(ins, turn)
                        settle(dve)
                        for t in range(QT):
                            ins = v.bn_aggr(meanvar[s][:, t, :], moments[s][:, t, :])
                        ins.then_inc(moments_ready.sem, 1)
                    elif kind in ("norm", "final"):
                        if w.new(moments_ready, ("stats", s, key, 0)):
                            dve.wait_ge(moments_ready.sem, moments_ready.after(turn, ("stats", s, key, 0)))
                        if w.new(rstd_ready, ("stats", s, key, 0)):
                            dve.wait_ge(rstd_ready.sem, rstd_ready.after(turn, ("stats", s, key, 0)))
                        x = x_in[s] if a["src"] == "x_in" else xn[s]
                        for t in range(QT):
                            ins = v.tensor_scalar(xh[s][:, t, :], x[:, t, :], meanvar[s][:, t, 0:1], rstd[s][:, t:t + 1],
                                                  ALU.subtract, ALU.mult)
                        ins.then_inc(xhat_ready.sem, 1)
                    elif kind == "mask":
                        if w.new(loaded[s], "x"):
                            dve.wait_ge(loaded[s].sem, loaded[s].after(turn, "x"))
                        v.tensor_scalar(m_rows[s][:, :, :], m_in[s][:, :, :], 0.0, -BIG,
                                                          ALU.not_equal, ALU.mult).then_inc(mask_ready.sem, 1)
                        if w.new(d_full, tag):
                            dve.wait_ge(d_full.sem, d_full.after(turn, tag))
                        v.tensor_copy(m_cols[s][:, :], slot_of("d", tag)[0:S2, 0:T // 2].bitcast(BF16)).then_inc(d_done.sem, 1)
                    elif kind in ("project_q", "project_k"):
                        i = 0 if kind == "project_q" else 1
                        nt = a.nk if i else T
                        x32 = (q32, k32)[i][s][:, :, 0:nt]
                        pt = [parts[s][:, i, n, :, 0:nt] for n in range(PARTS)]
                        if w.new(a_done, tag):
                            dve.wait_ge(a_done.sem, a_done.after(turn, tag))
                        v.tensor_copy(pt[0], x32).then_inc(hi_ready.sem, 1)
                        if w.new(hi_ready, tag):
                            dve.wait_ge(hi_ready.sem, hi_ready.after(turn, tag))
                        v.tensor_tensor(x32, x32, pt[0], ALU.subtract).then_inc(rest_ready.sem, 1)
                        if w.new(rest_ready, tag):
                            dve.wait_ge(rest_ready.sem, rest_ready.after(turn, tag))
                        v.tensor_copy(pt[1], x32).then_inc(mid_ready.sem, 1)
                    elif kind == "project_v":
                        if w.new(d_full, tag):
                            dve.wait_ge(d_full.sem, d_full.after(turn, tag))
                        bank = slot_of("d", tag)
                        kt, rows = (1, S2) if a.cross else (QT, P)
                        src = bank[0:rows, 0:kt * C].rearrange("p (k h d) -> p k h d", k=kt, d=D)
                        dst = v_aug[s][0:rows, 0:kt, :, 0:D]
                        if a.v_bias is None:
                            ins = v.tensor_copy(dst, src)
                        else:
                            for t in range(kt):
                                ins = v.tensor_tensor(dst[:, t], src[:, t],
                                                      a.v_bias[0:rows, :].rearrange("p (h d) -> p h d", d=D), ALU.add)
                        ins.then_inc(d_done.sem, 1)
                    elif kind == "project_v3":
                        if w.new(d_full, tag):
                            dve.wait_ge(d_full.sem, d_full.after(turn, tag))
                        v.tensor_copy(v3[s][:, 512 * j:512 * j + 512], slot_of("d", tag)[0:S2, :]).then_inc(d_done.sem, 1)
                    elif kind == "scores_max":
                        t, heads, nk = a.max_jobs()[j]
                        if w.new(d_full, tag):
                            dve.wait_ge(d_full.sem, d_full.after(turn, tag))
                        bank = slot_of("d", tag)
                        v.tensor_reduce(mx[s][:, t, heads[0]:heads[-1] + 1],
                                                         bank[:, 0:len(heads) * nk].rearrange("p (h k) -> p h k", k=nk),
                                                         AX_X, ALU.max).then_inc(d_done.sem, 1)
                    elif kind == "negate_max":
                        lim = 2.0 ** 90 if a.masked == "each" else 3.0e38
                        if w.new(d_done, ("scores_max", s, key, len(a.max_jobs()) - 1)):
                            dve.wait_ge(d_done.sem, d_done.after(turn, ("scores_max", s, key, len(a.max_jobs()) - 1)))
                        pt = nm_parts[s]
                        step(v.tensor_scalar(nmf[s][:, :, :], mx[s][:, :, :], -1.0, lim, ALU.mult, ALU.min), turn)
                        step(v.tensor_copy(pt[:, :, 0, :], nmf[s][:, :, :]), turn)
                        step(v.tensor_tensor(nmf[s][:, :, :], nmf[s][:, :, :], pt[:, :, 0, :], ALU.subtract), turn)
                        step(v.tensor_copy(pt[:, :, 1, :], nmf[s][:, :, :]), turn)
                        v.tensor_tensor(pt[:, :, 2, :], nmf[s][:, :, :], pt[:, :, 1, :], ALU.subtract).then_inc(negmax_ready.sem, 1)
                        if w.new(d_full, tag):
                            dve.wait_ge(d_full.sem, d_full.after(turn, tag))
                        v.tensor_copy(nm_t[s][0:PARTS * H, :],
                                                       slot_of("d", tag)[0:PARTS * H, 0:T // 2].bitcast(BF16)).then_inc(d_done.sem, 1)
                    elif kind == "probs_v":
                        if tag in den_full.at:
                            if w.new(den_full, tag):
                                dve.wait_ge(den_full.sem, den_full.after(turn, tag))
                            v.reciprocal(rden[s][:, :], bank_den[0:H, 0:T]).then_inc(den_done.sem, 1)
                    elif kind == "normalise":
                        if w.new(o_done, ("probs_v", s, key, j)):
                            dve.wait_ge(o_done.sem, o_done.after(turn, ("probs_v", s, key, j)))
                        if last_use:
                            if w.new(d_done, last_use):
                                dve.wait_ge(d_done.sem, d_done.after(turn, last_use))
                        last_use = tag
                        if w.new(d_full, tag):
                            dve.wait_ge(d_full.sem, d_full.after(turn, tag))
                        step(v.reciprocal(recip[:, :], slot_of("d", tag)[:, :]), turn)
                        v.tensor_tensor(ot_n[s][:, 2 * j:2 * j + 2, :], otr[s][:, 2 * j:2 * j + 2, :],
                                                         recip[:, :].rearrange("p (g t) -> p g t", g=2), ALU.mult).then_inc(d_done.sem, 1)
                    elif kind == "normalise3":
                        if w.new(o_done, ("probs_v", s, key, j)):
                            dve.wait_ge(o_done.sem, o_done.after(turn, ("probs_v", s, key, j)))
                        if w.new(d_full, tag):
                            dve.wait_ge(d_full.sem, d_full.after(turn, tag))
                        v.tensor_tensor(ot_n3[s][:, 2 * j:2 * j + 2, :],
                                                         ot_raw[s][:, 512 * j:512 * j + 512].rearrange("p (g t) -> p g t", g=2),
                                                         slot_of("d", tag)[:, :].rearrange("p (g t) -> p g t", g=2),
                                                         ALU.mult).then_inc(d_done.sem, 1)
                    elif kind in ("project_out", "ff_out"):
                        if w.new(d_full, tag):
                            dve.wait_ge(d_full.sem, d_full.after(turn, tag))
                        bank = slot_of("d", tag)[:, :].rearrange("p (t c) -> p t c", t=QT)
                        half = kind == "ff_out" and act == "gelu"
                        if kind == "project_out" and a.res == "x_in":
                            other = x_in[s]
                        else:
                            other = xb[s]
                            if w.new(xb_ready, res["xb_for"][s, kind, key]):
                                dve.wait_ge(xb_ready.sem, xb_ready.after(turn, res["xb_for"][s, kind, key]))
                        if not (wide or res["final_ln"]):
                            if w.new(stored[s]):
                                dve.wait_ge(stored[s].sem, stored[s].before(turn))
                        if half:
                            ins = v.scalar_tensor_tensor(xn[s][:, :, :], bank, 0.5, other[:, :, :], ALU.mult, ALU.add)
                        else:
                            ins = v.tensor_tensor(xn[s][:, :, :], bank, other[:, :, :], ALU.add)
                        ins.then_inc(d_done.sem, 1)
                        if w.new(d_done, tag):
                            dve.wait_ge(d_done.sem, d_done.after(turn, tag))
                    elif kind == "ff_in" and act == "gelu":
                        if w.new(a_done, tag):
                            dve.wait_ge(a_done.sem, a_done.after(turn, tag))
                        x, sq = g32[s][:, j % 2, 0], g32[s][:, j % 2, 1]
                        step(v.tensor_scalar(sq, sq, GELU_A, 1.0, ALU.mult, ALU.add), turn)
                        v.tensor_tensor(sq, sq, x, ALU.mult).then_inc(poly_ready.sem, 1)
                    elif kind == "ff_mid" and act == "gelu":
                        if w.new(tanh_ready, tag):
                            dve.wait_ge(tanh_ready.sem, tanh_ready.after(turn, tag))
                        v.scalar_tensor_tensor(ffh[s][:, 2 * j:2 * j + 2, :], g32[s][:, j % 2, 1], 1.0,
                                                               g32[s][:, j % 2, 0], ALU.add, ALU.mult).then_inc(ff_ready.sem, 1)
                assert chain[0] == n_dve, ("dve", name, chain[0])

            with dve.Fori(0, TURNS) as turn:
                body(turn)

        @block.tensor
        def _(pe):
            w = Seen()
            pe.wait_ge(setup_dma, 16 * res["n_setup"])
            pe.wait_ge(setup_g, res["n_setup_g"])
            pe.wait_ge(setup_v, res["n_setup_v"])
            ident, identb, sel, sel_den = res["ident"], res["identb"], res["sel"], res["sel_den"]

            def mm(out, lhsT, rhs, first):
                return nc.tensor.matmul(out, lhsT, rhs, start=first, stop=True, skip_group_check=True)

            def body(turn):
                w.last = {}

                def take(r, tag):
                    n = full[r].at[tag]
                    if n < len(rings[r]):
                        if w.new(done[r]):
                            pe.wait_ge(done[r].sem, done[r].before(turn))
                    else:
                        if w.new(done[r], full[r].tags[n - len(rings[r])]):
                            pe.wait_ge(done[r].sem, done[r].after(turn, full[r].tags[n - len(rings[r])]))
                    return slot_of(r, tag)

                for kind, s, key, a, j in units:
                    tag = (kind, s, key, j)
                    if kind == "context":
                        if w.new(loaded[s], "x"):
                            pe.wait_ge(loaded[s].sem, loaded[s].after(turn, "x"))
                        bank = take("a", tag)
                        for f in range(FT):
                            ins = nc.tensor.transpose(bank[:, f * S2:(f + 1) * S2], c_in[s][:, f * P:(f + 1) * P],
                                                      ident[0:S2, 0:S2])
                        ins.then_inc(a_full.sem, 1)
                    elif kind in ("norm", "turn"):
                        if kind == "norm":
                            if w.new(xhat_ready, tag):
                                pe.wait_ge(xhat_ready.sem, xhat_ready.after(turn, tag))
                            x = xh[s]
                        else:
                            if w.new(loaded[s], "x"):
                                pe.wait_ge(loaded[s].sem, loaded[s].after(turn, "x"))
                            x = x_in[s]
                        bank = take("a", tag)
                        for f in range(FT):
                            for t in range(QT):
                                ins = nc.tensor.transpose(bank[:, f * T + t * P:f * T + (t + 1) * P],
                                                          x[:, t, f * P:(f + 1) * P], ident[:, :])
                        ins.then_inc(a_full.sem, 1)
                    elif kind == "mask":
                        if w.new(mask_ready, tag):
                            pe.wait_ge(mask_ready.sem, mask_ready.after(turn, tag))
                        bank = take("d", tag)
                        for t in range(QT):
                            ins = nc.tensor.transpose(bank[0:S2, t * P // 2:(t + 1) * P // 2].bitcast(BF16),
                                                      m_rows[s][:, t, :], identb[:, :])
                        ins.then_inc(d_full.sem, 1)
                    elif kind in ("project_q", "project_k", "project_q3", "project_k3", "ff_in"):
                        if kind == "ff_in":
                            wt, x, xt, nt, n, fs = a["w"], ht[s], a["x_tag"], T, 2, (2 * j, 2 * j + 2)
                        elif kind in ("project_q", "project_q3"):
                            wt, x, xt, nt, n = a.q[0], ht[s], a.q[2], T, 2
                            fs = (2 * j, 2 * j + 2) if kind == "project_q3" else (0, FT)
                        else:
                            src = "c" if a.cross else "h"
                            wt, x, nt, xt = a.k[0], (ct if a.cross else ht)[s], a.nk, a.k[2]
                            fs = (4 * j, 4 * j + 4) if kind == "project_k3" else (0, FT)
                        if w.new(a_done, (xt[0], s) + xt[1:]):
                            pe.wait_ge(a_done.sem, a_done.after(turn, (xt[0], s) + xt[1:]))
                        bank = take("a", tag)
                        for m, f in enumerate(range(*fs)):
                            for c in range(FT):
                                ins = mm(bank[:, m * nt:(m + 1) * nt], wt[:, c, f * P:(f + 1) * P], x[:, c, 0:nt], c == 0)
                        ins.then_inc(a_full.sem, 1)
                    elif kind in ("project_v", "project_v3"):
                        xt = a.v[2]
                        if w.new(a_done, (xt[0], s) + xt[1:]):
                            pe.wait_ge(a_done.sem, a_done.after(turn, (xt[0], s) + xt[1:]))
                        bank = take("d", tag)
                        if kind == "project_v3":
                            for c in range(FT):
                                ins = mm(bank[0:S2, :], ct[s][:, c, :], a.v[0][:, c, 512 * j:512 * j + 512], c == 0)
                        else:
                            kt, rows = (1, S2) if a.cross else (QT, P)
                            x = (ct if a.cross else ht)[s]
                            for t in range(kt):
                                for c in range(FT):
                                    ins = mm(bank[0:rows, t * C:(t + 1) * C], x[:, c, t * rows:(t + 1) * rows],
                                             a.v[0][:, c, :], c == 0)
                        ins.then_inc(d_full.sem, 1)
                    elif kind == "scores_max":
                        t, heads, nk = a.max_jobs()[j]
                        if j == 0 and a.d == D:
                            if w.new(stacks["project_q", s], ("project_q", s, key, 0)):
                                pe.wait_ge(stacks["project_q", s].sem, stacks["project_q", s].after(turn, ("project_q", s, key, 0)))
                            if w.new(stacks["project_k", s], ("project_k", s, key, 0)):
                                pe.wait_ge(stacks["project_k", s].sem, stacks["project_k", s].after(turn, ("project_k", s, key, 0)))
                        elif j == 0:
                            if w.new(a_done, ("project_k3", s, key, FT3 // 4 - 1)):
                                pe.wait_ge(a_done.sem, a_done.after(turn, ("project_k3", s, key, FT3 // 4 - 1)))
                        bank = take("d", tag)
                        if a.d == D:
                            for n, h in enumerate(heads):
                                ins = mm(bank[:, n * nk:(n + 1) * nk], qs[s][0:KS, h, t * P:(t + 1) * P],
                                         ks[s][0:KS, h, 0:nk], n == 0)
                        else:
                            for n in range(0, len(heads), 2):
                                h = heads[n]
                                ins = mm(bank[:, n * nk:(n + 2) * nk], q3[s][:, h // 2, t * P:(t + 1) * P],
                                         kmask3[s][:, h:h + 2, :], n == 0)
                        n = len(heads)
                        whole = bank[:, 0:n * nk].rearrange("p (h k) -> p h k", k=nk)
                        if a.kind == "causal":
                            ins = mm(whole[:, :, nk - P:nk], identb[:, :],
                                     res["causal_rows"][:, None, :].broadcast_to((P, n, P)), False)
                        elif a.masked == "all":
                            ins = mm(whole, identb[:, :], res["mask_rows"][:, t, None, :].broadcast_to((P, n, nk)), False)
                        elif a.masked == "each":
                            if j == 0:
                                if w.new(mask_ready, ("mask", s, "mask", 0)):
                                    pe.wait_ge(mask_ready.sem, mask_ready.after(turn, ("mask", s, "mask", 0)))
                            ins = mm(whole, identb[:, :], m_rows[s][:, t, None, :].broadcast_to((P, n, nk)), False)
                        ins.then_inc(d_full.sem, 1)
                    elif kind == "negate_max":
                        if w.new(negmax_ready, tag):
                            pe.wait_ge(negmax_ready.sem, negmax_ready.after(turn, tag))
                        bank = take("d", tag)
                        settle(pe)
                        for t in range(QT):
                            ins = nc.tensor.transpose(bank[0:PARTS * H, t * P // 2:(t + 1) * P // 2].bitcast(BF16),
                                                      nm_parts[s][:, t, :, :].rearrange("p a h -> p (a h)"), identb[:, :])
                        ins.then_inc(d_full.sem, 1)
                    elif kind == "scores_exp":
                        if j == 0:
                            if w.new(d_done, ("negate_max", s, key, 0)):
                                pe.wait_ge(d_done.sem, d_done.after(turn, ("negate_max", s, key, 0)))
                            if a.masked == "each":
                                if w.new(d_done, ("mask", s, "mask", 0)):
                                    pe.wait_ge(d_done.sem, d_done.after(turn, ("mask", s, "mask", 0)))
                        bank = take("a", tag)
                        heads = a.exp_units()[j]
                        if a.cross:
                            for n, h in enumerate(heads):
                                out = bank[0:S2, n * T:(n + 1) * T]
                                if a.d == D:
                                    mm(out, ks[s][0:KS, h, 0:S2], qs[s][0:KS, h, :], n == 0)
                                else:
                                    mm(out, kmask3[s][:, h, :], q3[s][:, h // 2, :], n == 0)
                            for n, h in enumerate(heads):
                                ins = mm(bank[0:S2, n * T:(n + 1) * T], sel[:, h, 0:S2], nm_t[s][:, :], False)
                            if a.masked == "each":
                                ins = mm(bank[0:S2, :].rearrange("p (h t) -> p h t", h=2), identb[0:S2, 0:S2],
                                         m_cols[s][:, None, :].broadcast_to((S2, 2, T)), False)
                        else:
                            h = heads[0]
                            if a.kind == "causal":
                                mm(bank[:, 0:T], ks[s][0:KS, h, 0:P], qs[s][0:KS, h, :], True)
                                mm(bank[:, T:T + P], ks[s][0:KS, h, P:T], qs[s][0:KS, h, P:T], False)
                                mm(bank[:, 0:T], sel[:, h, :], nm_t[s][:, :], False)
                                mm(bank[:, T:T + P], sel[:, h, :], nm_t[s][:, P:T], False)
                                ins = mm(bank[:, :].rearrange("p (k t) -> p k t", k=2)[:, :, 0:P], identb[:, :],
                                         res["causal_cols"][:, None, :].broadcast_to((P, 2, P)), False)
                            else:
                                for t in range(QT):
                                    mm(bank[:, t * T:(t + 1) * T], ks[s][0:KS, h, t * P:(t + 1) * P], qs[s][0:KS, h, :], t == 0)
                                ins = mm(bank[:, :].rearrange("p (k t) -> p k t", k=2), sel[:, h, :],
                                         nm_t[s][:, None, :].broadcast_to((P, 2, T)), False)
                                if a.masked == "all":
                                    ins = mm(bank[:, :], identb[:, :], res["mask_cols"][:, :, :].rearrange("p k t -> p (k t)"),
                                             False)
                        ins.then_inc(a_full.sem, 1)
                    elif kind == "probs_v":
                        heads = a.exp_units()[j]
                        if w.new(a_done, ("scores_exp", s, key, j)):
                            pe.wait_ge(a_done.sem, a_done.after(turn, ("scores_exp", s, key, j)))
                        if j == 0:
                            vt = "project_v" if a.d == D else "project_v3"
                            if w.new(d_done, (vt, s, key, 0 if a.d == D else 1)):
                                pe.wait_ge(d_done.sem, d_done.after(turn, (vt, s, key, 0 if a.d == D else 1)))
                        for n, h in enumerate(heads):
                            pr = probs[s][:, j % 3, :]
                            if a.d == D:
                                ot = (kind, s, key, h // 8)
                                if h % 8 == 0:
                                    take("o", ot)
                                out = slot_of("o", ot)[32 * (h % HG):32 * (h % HG) + 32, :].rearrange(
                                    "p (g t) -> p g t", g=2)[:, (h // HG) % 2, :]
                                if a.cross:
                                    ins = mm(out, v_aug[s][0:S2, 0, h, :], pr[0:S2, n * T:(n + 1) * T], True)
                                elif a.kind == "causal":
                                    mm(out, v_aug[s][:, 0, h, :], pr[:, 0:T], True)
                                    ins = mm(out[:, P:T], v_aug[s][:, 1, h, :], pr[:, T:T + P], False)
                                else:
                                    for t in range(QT):
                                        ins = mm(out, v_aug[s][:, t, h, :], pr[:, t * T:(t + 1) * T], t == 0)
                                if h % 8 == 7:
                                    ins.then_inc(o_full.sem, 1)
                            else:
                                ot = (kind, s, key, h // 4)
                                if h % 4 == 0:
                                    take("o", ot)
                                if h == 0:
                                    take("den", (kind, s, key, H // 2 - 1))
                                mm(bank_den[0:32, 0:T], res["onehot"][0:S2, 31 - h:63 - h], pr[0:S2, n * T:(n + 1) * T],
                                   h == 0) if h < H - 1 else mm(bank_den[0:32, 0:T], res["onehot"][0:S2, 31 - h:63 - h],
                                          pr[0:S2, n * T:(n + 1) * T], False).then_inc(den_full.sem, 1)
                                half = (h // 2) % 2
                                out = slot_of("o", ot)[64 * (h % 2):64 * (h % 2) + 64, half * T:(half + 1) * T]
                                ins = mm(out, v3[s][:, h * D3:(h + 1) * D3], pr[0:S2, n * T:(n + 1) * T], True)
                                if h % 4 == 3:
                                    ins.then_inc(o_full.sem, 1)
                    elif kind == "normalise":
                        if w.new(o_done, ("probs_v", s, key, j)):
                            pe.wait_ge(o_done.sem, o_done.after(turn, ("probs_v", s, key, j)))
                        bank = take("d", tag)
                        mm(bank[:, :], sel_den[:, :], ot_raw[s][:, 512 * j:512 * j + 512], True).then_inc(d_full.sem, 1)
                    elif kind == "normalise3":
                        if j == 0:
                            if w.new(den_done, ("probs_v", s, key, H // 2 - 1)):
                                pe.wait_ge(den_done.sem, den_done.after(turn, ("probs_v", s, key, H // 2 - 1)))
                        bank = take("d", tag)
                        for n in range(2):
                            ins = mm(bank[:, n * T:(n + 1) * T], res["sel_pair"][:, 2 * j + n, :], rden[s][:, :], n == 0)
                        ins.then_inc(d_full.sem, 1)
                    elif kind in ("project_out", "ff_out"):
                        if kind == "ff_out":
                            wt, x, n = a["w"], ffh[s], 8
                            if act == "gelu":
                                if w.new(ff_ready, ("ff_mid", s, key, 3)):
                                    pe.wait_ge(ff_ready.sem, ff_ready.after(turn, ("ff_mid", s, key, 3)))
                            else:
                                if w.new(a_done, ("ff_in", s, key, 3)):
                                    pe.wait_ge(a_done.sem, a_done.after(turn, ("ff_in", s, key, 3)))
                        else:
                            wt, n = a.o, (G if a.d == D else FT3)
                            x = ot_n[s] if a.d == D else ot_n3[s]
                            if w.new(d_done, (("normalise", s, key, 1) if a.d == D else ("normalise3", s, key, 3))):
                                pe.wait_ge(d_done.sem, d_done.after(turn, (("normalise", s, key, 1) if a.d == D else ("normalise3", s, key, 3))))
                        bank = take("d", tag)
                        for t in range(QT):
                            for c in range(n):
                                ins = mm(bank[:, t * C:(t + 1) * C], x[:, c, t * P:(t + 1) * P], wt[:, c, :], c == 0)
                        ins.then_inc(d_full.sem, 1)

            with pe.Fori(0, TURNS) as turn:
                body(turn)


def build(nc, ins, out):
    x1 = nc.dram_tensor("between_0_1", (NB, T, C), F32).ap()
    x2 = nc.dram_tensor("between_1_2", (NB, T, C), F32).ap()
    scratch = nc.dram_tensor("parts", (PAIR, 2, PARTS, FT, P, T), BF16).ap()

    def rows(t, turn, s):
        v = t.rearrange("(i s) (q p) c -> i s p q c", s=PAIR, p=P)
        return v[turn, s]

    def context(turn, s):
        return ins["ctx_1024"].rearrange("(i s) t c -> i s t c", s=PAIR)[turn, s]

    def common(ctx, name, want):
        def sb(n, shape, dt=F32):
            return ctx.enter_context(nc.sbuf_tensor(f"{name}_{n}", shape, dt))
        r = {"scratch": scratch, "zero": [], "weight_loads": [], "sums": [], "sb": sb, "name": name}
        r["ident"] = sb("ident", [P, P])
        r["identb"] = sb("identb", [P, P], BF16)
        r["sel"] = sb("sel", [P, H, P], BF16)
        r["sel_den"] = sb("sel_den", [P, P])
        r["half"] = sb("half", [P, QT])
        r["zero"].append((r["half"][:, :], -0.5))
        return r

    def weight(r, n, src, width=None):
        k, m = src.shape
        t = r["sb"](n, [P, k // P, m])
        r["weight_loads"].append((t[:, :, :], src.rearrange("(c p) n -> p c n", p=P)))
        return t

    def padded(r, n, src):
        t = r["sb"](n, [P, G, C])
        v = src.rearrange("(g j d) n -> j d g n", j=HG, d=D)
        for j in range(HG):
            r["weight_loads"].append((t[32 * j:32 * j + D, :, :], v[j]))
        r["padded"].append(t)
        return t

    def column(r, n, src):
        k = src.shape[0] // P
        t = r["sb"](n, [P, k])
        r["weight_loads"].append((t[:, :], src.rearrange("(c p) -> p c", p=P)))
        return t

    def spread(r, n, src):
        t = r["sb"](n, [P, C])
        r["weight_loads"].append((t[:, :], src.partition_broadcast(P)))
        return t

    def prepare(r, name):
        with ExitStack() as c:
            zeroed = c.enter_context(nc.semaphore(f"{name}_zeroed"))
            made = c.enter_context(nc.semaphore(f"{name}_made"))
            block = c.enter_context(nc.Block())

            @block.gpsimd
            def _(g):
                n = 0
                for t in [r["ident"], r["identb"], r["sel"], r["sel_den"]] + r["padded"] + r["selectors"]:
                    nc.gpsimd.memset(t[tuple(slice(None) for _ in t.shape)], 0.0).then_inc(zeroed, 1)
                    n += 1
                g.wait_ge(zeroed, n)
                k = 0

                def select(v, op, fill, base, pattern, mult):
                    nonlocal k
                    nc.gpsimd.affine_select(out=v, in_=v, compare_op=op, fill=fill, base=base, pattern=pattern,
                                            channel_multiplier=mult).then_inc(made, 1)
                    k += 1
                    g.wait_ge(made, k)

                for t in (r["ident"], r["identb"]):
                    select(t[:, :], ALU.not_equal, 1.0, 0, [[-1, P]], 1)
                for part in range(PARTS):
                    select(r["sel"][:, :, :], ALU.not_equal, 1.0, -H * part, [[-1, H], [0, P]], 1)
                select(r["sel_den"][:, :].rearrange("p (j d) -> p j d", j=HG), ALU.not_equal, 1.0, -D,
                       [[-32, HG], [0, 32]], 1)
                if "causal_rows" in r:
                    select(r["causal_rows"][:, :], ALU.is_ge, -BIG, 0, [[-1, P]], 1)
                    select(r["causal_cols"][:, :], ALU.is_ge, -BIG, 0, [[1, P]], -1)
                if "onehot" in r:
                    nc.gpsimd.memset(r["onehot"][:, 31:32], 1.0).then_inc(made, 1)
                    k += 1
                    select(r["sel_pair"][:, :, :].rearrange("p a (b d) -> p a b d", b=2), ALU.not_equal, 1.0, 0,
                           [[-2, FT3], [-1, 2], [0, D3]], 1)
                g.wait_ge(made, k)

    def xb_tags(streams):
        last, found = {}, {}
        for s in range(PAIR):
            for kind, _, key, a, j in streams[s]:
                if kind in ("norm", "turn", "final") and a.get("xb"):
                    last[s] = (kind, s, key, j)
                if kind in ("project_out", "ff_out"):
                    found[s, kind, key] = last.get(s)
        return found

    with ExitStack() as ctx:
        r = common(ctx, "l0", None)
        r["padded"], sb = [], r["sb"]
        r["causal_rows"], r["causal_cols"] = sb("causal_rows", [P, P], BF16), sb("causal_cols", [P, P], BF16)
        r["selectors"] = [r["causal_rows"], r["causal_cols"]]
        i = {k[len("L0_xattn_"):]: v for k, v in ins.items() if k.startswith("L0_")}
        w_attn, w_q, w_k, w_v = (weight(r, n, i[m]) for n, m in (("w_attn", "W_attn"), ("wq", "Wq"), ("wk", "Wk"), ("wv", "Wv")))
        w_ao, w_co = padded(r, "w_ao", i["W_aproj"]), padded(r, "w_co", i["Wcproj"])
        w_fc, w_mp = weight(r, "w_fc", i["W_fc"]), weight(r, "w_mp", i["W_mproj"])
        b_attn = i["b_attn"]
        bq0, bk0 = column(r, "bq0", b_attn[0:C]), column(r, "bk0", b_attn[C:2 * C])
        bv0 = spread(r, "bv0", b_attn[2 * C:3 * C])
        bq, bk, bv = column(r, "bq", i["bq"]), column(r, "bk", i["bk"]), spread(r, "bv", i["bv"])
        b_ao, b_co, b_mp = (spread(r, n, i[m]) for n, m in (("b_ao", "b_aproj"), ("b_co", "bcproj"), ("b_mp", "b_mproj")))
        b_fc = column(r, "b_fc", i["b_fc"])
        g1, b1, g2, b2 = (column(r, n, i[n]) for n in ("ln1_g", "ln1_b", "ln2_g", "ln2_b"))
        prepare(r, "l0p")
        streams = []
        for s in range(PAIR):
            h0, h1, c = ("norm", "ln0", 0), ("norm", "ln1", 0), ("context", "ctx", 0)
            own = Att("own", "causal", (w_attn[:, :, 0:C], bq0, h0), (w_attn[:, :, C:2 * C], bk0, h0),
                      (w_attn[:, :, 2 * C:3 * C], None, h0), w_ao, v_bias=bv0)
            other = Att("other", "cross", (w_q, bq, h1), (w_k, bk, c), (w_v, None, c), w_co, v_bias=bv)
            n0 = dict(src="x_in", eps=1e-5, g=g1, b=b1, xb=("add", "x_in", None, b_ao))
            n1 = dict(src="xn", eps=1e-5, g=g1, b=b1, xb=("add", "xn", None, b_co), sum_tag=("project_out", s, "own", 0))
            n2 = dict(src="xn", eps=1e-5, g=g2, b=b2, xb=("add", "xn", None, b_mp), sum_tag=("project_out", s, "other", 0))
            u = [("context", s, "ctx", None, 0), ("stats", s, "ln0", n0, 0), ("norm", s, "ln0", n0, 0)]
            u += att_units(s, own) + [("stats", s, "ln1", n1, 0), ("norm", s, "ln1", n1, 0)]
            u += att_units(s, other) + [("stats", s, "ln2", n2, 0), ("norm", s, "ln2", n2, 0)]
            f = dict(w=w_fc, b=b_fc, x_tag=("norm", "ln2", 0))
            for j in range(5):
                if j < 4:
                    u.append(("ff_in", s, "ff", f, j))
                if j:
                    u.append(("ff_mid", s, "ff", f, j - 1))
            u += [("ff_out", s, "ff", dict(w=w_mp), 0), ("store", s, "x", None, 0)]
            streams.append(u)
        r.update(wide=False, lag=20000, loads=2, final_ln=False, x=lambda t, s: rows(ins["x"], t, s), ctx=context,
                 out=lambda t, s: rows(x1, t, s), prefetch_at=("project_v", "own"), n_setup=len(r["weight_loads"]),
                 x_readers=lambda s, c: [(c["xhat"], ("norm", s, "ln0", 0)), (c["xb"], ("norm", s, "ln0", 0)),
                                         (c["a"], ("context", s, "ctx", 0))],
                 dve_steps=38, pool_steps=6, n_setup_g=len(r["zero"]) + 3 * PAIR, n_setup_v=0, dve_setup=lambda v: [],
                 xb_for=xb_tags(streams))
        run_pass(nc, "l0", streams, r, "gelu")

    with ExitStack() as ctx:
        r = common(ctx, "l1", None)
        r["padded"], sb = [], r["sb"]
        r["selectors"] = []
        i = {k[len("L1_xattn_"):]: v for k, v in ins.items() if k.startswith("L1_")}
        wt = {n: weight(r, n, i[n + "_w"]) for n in ("q", "k", "v", "cq", "ck", "cv")}
        w_o, w_co = padded(r, "w_o", i["o_w"]), padded(r, "w_co", i["co_w"])
        w_1, w_2 = weight(r, "w_1", i["lin1_w"]), weight(r, "w_2", i["lin2_w"])
        col = {n: column(r, "c_" + n, i[n]) for n in ("q_b", "k_b", "cq_b", "ck_b", "lin1_b", "ln1_g", "ln1_b", "ln2_g", "ln2_b")}
        spr = {n: spread(r, "s_" + n, i[n]) for n in ("v_b", "cv_b", "o_b", "co_b", "lin2_b", "ln1_g", "ln1_b", "ln2_g",
                                                      "ln2_b", "ln3_g", "ln3_b")}
        r["sums"] = [(spr["ln1_b"][:, :], spr["ln1_b"][:, :], spr["co_b"][:, :]),
                     (spr["ln2_b"][:, :], spr["ln2_b"][:, :], spr["lin2_b"][:, :])]
        mask_i, mask_j = sb("mask_i", [P, QT, T], I32), sb("mask_j", [P, QT, T], I32)
        r["mask_rows"], r["mask_cols"] = sb("mask_rows", [P, QT, T], BF16), sb("mask_cols", [P, QT, T], BF16)
        m = ins["mask_SxS_ik1"]
        r["weight_loads"].append((mask_i[:, :, :], m.rearrange("(q p) k -> p q k", p=P)))
        r["weight_loads"].append((mask_j[:, :, :], ins["mask_by_key"].rearrange("(k p) q -> p k q", p=P)))
        prepare(r, "l1p")

        def masks(v):
            return [v.tensor_scalar(r["mask_rows"][:, :, :], mask_i[:, :, :], 0.0, -BIG, ALU.not_equal, ALU.mult),
                    v.tensor_scalar(r["mask_cols"][:, :, :], mask_j[:, :, :], 0.0, -BIG, ALU.not_equal, ALU.mult)]

        streams = []
        for s in range(PAIR):
            h0, h1, c = ("turn", "in", 0), ("norm", "ln1", 0), ("context", "ctx", 0)
            own = Att("own", "self", (wt["q"], col["q_b"], h0), (wt["k"], col["k_b"], h0), (wt["v"], None, h0), w_o,
                      masked="all", v_bias=spr["v_b"])
            other = Att("other", "cross", (wt["cq"], col["cq_b"], h1), (wt["ck"], col["ck_b"], c), (wt["cv"], None, c),
                        w_co, v_bias=spr["cv_b"])
            n1 = dict(src="xn", eps=1e-5, g=col["ln1_g"], b=col["ln1_b"], xb=("scale", None, spr["ln1_g"], spr["ln1_b"]))
            n2 = dict(src="xn", eps=1e-5, g=col["ln2_g"], b=col["ln2_b"], xb=("scale", None, spr["ln2_g"], spr["ln2_b"]))
            n3 = dict(src="xn", eps=1e-5, xb=("scale", None, spr["ln3_g"], spr["ln3_b"]))
            u = [("context", s, "ctx", None, 0), ("turn", s, "in", dict(xb=("add", "x_in", None, spr["o_b"])), 0)]
            u += att_units(s, own) + [("stats", s, "ln1", n1, 0), ("norm", s, "ln1", n1, 0)]
            u += att_units(s, other) + [("stats", s, "ln2", n2, 0), ("norm", s, "ln2", n2, 0)]
            u += [("ff_in", s, "ff", dict(w=w_1, b=col["lin1_b"], x_tag=("norm", "ln2", 0)), j) for j in range(4)]
            u += [("ff_out", s, "ff", dict(w=w_2), 0), ("stats", s, "ln3", n3, 0), ("final", s, "ln3", n3, 0),
                  ("store", s, "x", None, 0)]
            streams.append(u)
        r.update(wide=False, lag=20000, loads=2, final_ln=True, x=lambda t, s: rows(x1, t, s), ctx=context,
                 out=lambda t, s: rows(x2, t, s), prefetch_at=("project_v", "own"), n_setup=len(r["weight_loads"]),
                 x_readers=lambda s, c: [(c["xb"], ("turn", s, "in", 0)), (c["a"], ("turn", s, "in", 0)),
                                         (c["a"], ("context", s, "ctx", 0))],
                 dve_steps=30, pool_steps=12, n_setup_g=len(r["zero"]) + 3 * PAIR + 2, n_setup_v=2, dve_setup=masks,
                 xb_for=xb_tags(streams))
        run_pass(nc, "l1", streams, r, "relu")

    with ExitStack() as ctx:
        r = common(ctx, "l2", None)
        r["padded"], sb = [], r["sb"]
        r["onehot"], r["sel_pair"] = sb("onehot", [P, 63]), sb("sel_pair", [H, FT3, P])
        r["selectors"] = [r["onehot"], r["sel_pair"]]
        i = {k[3:]: v for k, v in ins.items() if k.startswith(("L2_", "L3_"))}
        w2 = {n: weight(r, "2" + n, ins["L2_xattn_w" + n]) for n in "qkv"}
        w2o = padded(r, "2o", ins["L2_xattn_wo"])
        w3 = {n: weight(r, "3" + n, ins["L3_xattn_w_" + n]) for n in ("q", "k", "v", "fc")}
        g2, b2 = column(r, "g2", ins["L2_xattn_gamma"]), column(r, "b2", ins["L2_xattn_beta"])
        g2s, b2s = spread(r, "g2s", ins["L2_xattn_gamma"]), spread(r, "b2s", ins["L2_xattn_beta"])
        g3s, b3s = spread(r, "g3s", ins["L3_xattn_ln_gamma"]), spread(r, "b3s", ins["L3_xattn_ln_beta"])
        prepare(r, "l2p")
        streams = []
        for s in range(PAIR):
            h0, h1, c = ("turn", "in", 0), ("norm", "ln2", 0), ("context", "ctx", 0)
            a2 = Att("two", "cross", (w2["q"], None, h0), (w2["k"], None, c), (w2["v"], None, c), w2o, masked="each",
                     res="x_in")
            a3 = Att("three", "cross", (w3["q"], None, h1), (w3["k"], None, c), (w3["v"], None, c), w3["fc"], d=D3)
            n2 = dict(src="xn", eps=1e-5, g=g2, b=b2, xb=("scale", None, g2s, b2s))
            n3 = dict(src="xn", eps=1e-6, xb=("scale", None, g3s, b3s))
            u = [("context", s, "ctx", None, 0), ("turn", s, "in", {}, 0), ("mask", s, "mask", None, 0)]
            u += att_units(s, a2) + [("stats", s, "ln2", n2, 0), ("norm", s, "ln2", n2, 0)]
            u += att_units(s, a3) + [("stats", s, "ln3", n3, 0), ("final", s, "ln3", n3, 0), ("store", s, "x", None, 0)]
            streams.append(u)
        mask = ins["mask_BxSxS2_bk1"].rearrange("(i s) (q p) k -> i s p q k", s=PAIR, p=P)
        r.update(wide=True, lag=12000, loads=3, final_ln=True, x=lambda t, s: rows(x2, t, s), ctx=context,
                 mask=lambda t, s: mask[t, s], out=lambda t, s: rows(out, t, s), prefetch_at=("norm", "ln2"),
                 n_setup=len(r["weight_loads"]),
                 x_readers=lambda s, c: [(c["d"], ("project_out", s, "two", 0)), (c["a"], ("turn", s, "in", 0)),
                                         (c["a"], ("context", s, "ctx", 0)), (c["mask"], ("mask", s, "mask", 0))],
                 dve_steps=24, pool_steps=8, n_setup_g=len(r["zero"]) + 4 * PAIR, n_setup_v=0, dve_setup=lambda v: [],
                 xb_for=xb_tags(streams))
        run_pass(nc, "l2", streams, r, None)


def kernel(**inputs):
    import numpy as _np
    import concourse.bacc as _bacc
    from concourse import mybir as _mybir
    from concourse.bass_utils import run_bass_kernel_spmd as _run

    nc = _bacc.Bacc("TRN2", target_bir_lowering=False, num_devices=1)
    arrays, aps = {}, {}
    inputs["mask_by_key"] = _np.asarray(inputs["mask_SxS_ik1"]).T
    for name, a in inputs.items():
        a = _np.ascontiguousarray(a)
        arrays[f"in_{name}"] = a
        aps[name] = nc.dram_tensor(f"in_{name}", a.shape, _mybir.dt.from_np(a.dtype), kind="ExternalInput").ap()
    out = nc.dram_tensor("out_0", (NB, T, C), F32, kind="ExternalOutput").ap()
    build(nc, aps, out)
    r = _run(nc, [arrays], core_ids=[0])
    return r.results[0]["out_0"]
```

```python
from contextlib import ExitStack

import concourse.bass as bass
from concourse import mybir

ALU = mybir.AluOpType
ACT = mybir.ActivationFunctionType
AX_X = mybir.AxisListType.X
F32 = mybir.dt.float32
BF16 = mybir.dt.bfloat16
U8 = mybir.dt.uint8
I32 = mybir.dt.int32

P = 128
NB, T, C = 32, 256, 256
S2 = 120
H = 16
D = C // H
D3 = 64
FF = 4 * C
QT = T // P
FT = C // P
PAIR = 2
TURNS = NB // PAIR
HG = 4
G = H // HG
FT3 = H * D3 // P
PARTS = 3
Q_SLOTS = (0, 0, 0, 1, 1, 2)
K_SLOTS = (0, 1, 2, 0, 1, 0)
SLOTS = len(Q_SLOTS)
KS = SLOTS * D
BIG = 2.0 ** 100
GELU_A = 0.044715
GELU_C = (2.0 / 3.141592653589793) ** 0.5


class Att:

    def __init__(self, key, kind, q, k, v, o, bias="", masked=False, d=D, res="xb", v_bias=None):
        self.key, self.kind, self.masked, self.d, self.res = key, kind, masked, d, res
        self.q, self.k, self.v, self.o = q, k, v, o
        self.v_bias = v_bias
        self.cross = kind == "cross"
        self.nk = S2 if self.cross else T
        self.scale = float(d) ** -0.5

    def max_jobs(self):
        jobs = []
        for t in range(QT):
            nk = P if self.kind == "causal" and t == 0 else self.nk
            n = 4 if nk <= P else 2
            for h in range(0, H, n):
                jobs.append((t, list(range(h, h + n)), nk))
        return jobs

    def exp_units(self):
        n = 2 if self.cross else 1
        return [list(range(h, h + n)) for h in range(0, H, n)]


def att_units(s, a):
    u = []
    if a.d == D:
        u += [("project_q", s, a.key, a, 0), ("project_k", s, a.key, a, 0), ("project_v", s, a.key, a, 0)]
    else:
        u += [("project_q3", s, a.key, a, j) for j in range(FT3 // 2)]
        u += [("project_k3", s, a.key, a, j) for j in range(FT3 // 4)]
        u += [("project_v3", s, a.key, a, j) for j in range(2)]
    u += [("scores_max", s, a.key, a, j) for j in range(len(a.max_jobs()))]
    u += [("negate_max", s, a.key, a, 0)]
    n = len(a.exp_units())
    for j in range(n + 2):
        if j < n:
            u.append(("scores_exp", s, a.key, a, j))
        if j >= 2:
            u.append(("probs_v", s, a.key, a, j - 2))
    if a.d == D:
        u += [("normalise", s, a.key, a, j) for j in range(G // 2)]
    else:
        u += [("normalise3", s, a.key, a, j) for j in range(FT3 // 2)]
    return u + [("project_out", s, a.key, a, 0)]


TIMES = {
    "context": (300, "act", 400, None), "turn": (700, "act", 600, 200), "stats": (0, "dve", 900, 1400),
    "norm": (700, "act", 800, 1000), "final": (0, "dve", 700, None), "store": (0, "dve", 0, None),
    "mask": (200, "dve", 500, None),
    "project_q": (1750, "act", 800, None), "project_k": (1500, "act", 800, None), "project_v": (1300, "dve", 600, 7500),
    "project_q3": (1750, "act", 500, None), "project_k3": (1700, "act", 900, None), "project_v3": (1750, "dve", 600, None),
    "scores_max": (500, "dve", 610, None), "negate_max": (200, "dve", 1300, 300),
    "scores_exp": (600, "act", 510, None), "probs_v": (350, "act", 0, None),
    "normalise": (850, "dve", 3900, None), "normalise3": (850, "dve", 610, None), "project_out": (3500, "dve", 700, 200),
    "ff_in": (1750, "act", 1000, None), "ff_mid": (0, "act", 500, None), "ff_out": (6900, "dve", 700, 200),
}


def weave(a, b):
    out, left, ready = [], [list(a), list(b)], [0, 0]
    pe = 0
    free = {"act": 0, "dve": 0}
    while left[0] or left[1]:
        s = min((s for s in range(PAIR) if left[s]), key=lambda s: (max(pe, ready[s]), -len(left[s])))
        step = left[s].pop(0)
        on_pe, engine, on_engine, then = TIMES[step[0][0]]
        pe = max(pe, ready[s]) + on_pe
        free[engine] = max(free[engine], pe) + on_engine
        pe = max(pe, free[engine] - 2 * on_engine)
        ready[s] = pe if then is None else free[engine] + then
        if step[0][0] in ("normalise", "normalise3", "ff_mid", "probs_v") and left[s] and \
                left[s][0][0][0] in ("project_out", "ff_out", "normalise", "normalise3"):
            ready[s] = free[engine] + 600
        out.append(step)
    return out


class Here:

    place, mode = 0, "middle"


class Count:

    def __init__(self, sem, signals, step=1):
        self.sem, self.step = sem, step
        self.tags = [tag for tag, _, _ in signals]
        self.at = {tag: i for i, tag in enumerate(self.tags)}
        self.place = {tag: place for tag, place, _ in signals}
        self.late = [late for _, _, late in signals]
        self.per_turn = step * len(signals)
        self.start = 1 + step * sum(self.late)
        assert len(self.at) == len(signals)

    def same_turn(self, tag):
        return self.place[tag] <= Here.place

    def after(self, turn, tag):
        i = self.at[tag] + 1
        if Here.mode == "first":
            return self.start + (self.step * (i - sum(self.late[:i])) if self.same_turn(tag) else 0)
        if Here.mode == "last" and self.same_turn(tag):
            return 1 + turn * self.per_turn + self.step * sum(self.late[:i])
        return turn * self.per_turn + (1 + self.step * i - (0 if self.same_turn(tag) else self.per_turn))

    def before(self, turn):
        return self.start if Here.mode == "first" else 1 + turn * self.per_turn


def step_signals(u, act):
    kind, s, key, a, j = u
    t = (kind, s, key, j)
    sig = {}
    if kind in ("context", "norm", "turn", "project_q", "project_k", "project_q3", "project_k3", "scores_exp", "ff_in"):
        sig["a"] = [t]
    if kind in ("project_v", "project_v3", "scores_max", "negate_max", "normalise", "normalise3", "project_out",
                "ff_out", "mask"):
        sig["d"] = [t]
    if kind == "probs_v":
        heads = a.exp_units()[j]
        per = 8 if a.d == D else 4
        if (heads[-1] + 1) % per == 0:
            sig["o"] = [(kind, s, key, heads[-1] // per)]
        if a.d != D and heads[-1] == H - 1:
            sig["den"] = [t]
    if kind == "stats":
        sig["moments"] = sig["rstd"] = [t]
    if kind == "norm":
        sig["xhat"] = [t]
    if kind in ("norm", "turn", "final") and a.get("xb"):
        sig["xb"] = [t]
    if kind == "final":
        sig["xhat"] = [t]
    if kind in ("project_q", "project_k"):
        sig["hi"] = sig["mid"] = sig["rest"] = sig["lo"] = [t]
    if kind == "negate_max":
        sig["negmax"] = [t]
    if kind == "store":
        sig["store"] = [t]
    links = {"stats": 1, "negate_max": 4, "normalise": 1, "ff_in": 1 if act == "gelu" else 0}.get(kind, 0)
    sig["dve_step"] = [t + (n,) for n in range(links)]
    scaled = kind in ("norm", "final") and a.get("xb") and a["xb"][0] == "scale"
    sig["pool_step"] = [t] if kind == "stats" or scaled else []
    if kind == "mask":
        sig["mask"] = [t]
    if kind == "ff_mid" and act == "gelu":
        sig["tanh"] = [t]
        sig["ff"] = [t]
    if kind == "ff_in" and act == "gelu":
        sig["poly"] = [t]
    return sig


def run_pass(nc, name, streams, res, act):
    late_from = res["late_from"]
    cut = [u[0] + u[2] for u in streams[1]].index(late_from)
    woven = weave([(u, False) for u in streams[0]],
                  [(u, True) for u in streams[1][cut:]] + [(u, False) for u in streams[1][:cut]])
    units = [u for u, _ in woven]
    late = [x for _, x in woven]

    def steps(mode):
        Here.mode = mode
        for Here.place, u in enumerate(units):
            if mode == "middle" or (mode == "last") == late[Here.place]:
                yield u

    order = {k: [] for k in ("store", "dve_step", "pool_step", "a", "d", "o", "den", "moments", "rstd", "xhat", "xb", "hi", "mid", "rest", "lo", "negmax",
                             "mask", "tanh", "ff", "poly")}
    for place, u in enumerate(units):
        for k, tags in step_signals(u, act).items():
            order[k] += [(tag, place, late[place]) for tag in tags]
    width = 512
    with ExitStack() as ctx:
        def sb(n, shape, dt=F32):
            return ctx.enter_context(nc.sbuf_tensor(f"{name}_{n}", shape, dt))

        def two(n, shape, dt=F32):
            return [sb(f"{n}{s}", shape, dt) for s in range(PAIR)]

        def sem(n):
            return ctx.enter_context(nc.semaphore(f"{name}_{n}"))

        wide = res["wide"]
        x_in = two("x_in", [P, QT, C])
        c_in = two("c_in", [S2, C])
        xb = two("xb", [P, QT, C])
        xn = two("xn", [P, QT, C])
        xh = two("xh", [P, QT, C])
        ht = two("ht", [P, FT, T])
        ct = two("ct", [P, FT, S2])
        kstack = two("kstack", [P, H * T if not wide else H * 128], BF16)
        qstack = two("qstack", [P, 8 * T])
        parts = two("parts", [P, 2, PARTS, FT, T], BF16)
        ot_raw = two("ot_raw", [P, (FT3 if wide else G) * T])
        v_aug = two("v_aug", [P, QT, H, 32])
        probs = two("probs", [P, 3, width])
        mx = two("mx", [P, QT, H])
        nmf = two("nmf", [P, QT, H])
        nm_parts = two("nm_parts", [P, QT, PARTS, H], BF16)
        nm_t = two("nm_t", [P, T], BF16)
        moments = two("moments", [P, QT, 6])
        meanvar = two("meanvar", [P, QT, 2])
        veps = two("veps", [P, QT])
        rstd = two("rstd", [P, QT])
        recip = sb("recip", [P, width])
        if wide:
            ot_n3 = two("ot_n3", [P, FT3, T])
            kmask3 = two("kmask3", [P, H, S2])
            v3 = two("v3", [S2, H * D3])
            rden = two("rden", [H, T])
            m_in = two("m_in", [P, QT, S2], U8)
            m_rows = two("m_rows", [P, QT, S2], BF16)
            m_cols = two("m_cols", [S2, T], BF16)
        q32 = [ot_raw[s][:, 0:512].rearrange("p (f t) -> p f t", f=FT) for s in range(PAIR)]
        k32 = [ot_raw[s][:, 512:1024].rearrange("p (f t) -> p f t", f=FT) for s in range(PAIR)]
        otr = [ot_raw[s][:, 0:G * T].rearrange("p (g t) -> p g t", g=G) for s in range(PAIR)]
        ot_n = two("ot_n", [P, G, T])
        qs = [qstack[s][:, :].bitcast(BF16).rearrange("p (h t) -> p h t", h=H) for s in range(PAIR)]
        ks = [kstack[s][:, :].rearrange("p (h t) -> p h t", h=H) for s in range(PAIR)]
        ffh = [qstack[s][:, :].rearrange("p (f t) -> p f t", f=8) for s in range(PAIR)]
        q3 = ffh
        if not wide:
            g32 = [kstack[s][:, :].bitcast(F32).rearrange("p (c x f t) -> p c x f t", c=2, x=2, f=2) for s in range(PAIR)]

        na = 2 if wide else 3
        bank_a = [ctx.enter_context(nc.psum_tensor(f"{name}_bank_a{i}", [P, 512], F32)) for i in range(na)]
        bank_d = [ctx.enter_context(nc.psum_tensor(f"{name}_bank_d{i}", [P, 512], F32)) for i in range(2)]
        bank_o = [ctx.enter_context(nc.psum_tensor(f"{name}_bank_o{i}", [P, 512], F32)) for i in range(3)]
        bank_den = ctx.enter_context(nc.psum_tensor(f"{name}_bank_den", [P, 512], F32)) if wide else None
        rings = {"a": bank_a, "d": bank_d, "o": bank_o, "den": [bank_den]}

        def counts(n, key, step=1):
            return Count(sem(n), order[key], step)

        full = {r: counts(f"{r}_full", r) for r in rings}
        done = {r: counts(f"{r}_done", r) for r in rings}
        a_full, d_full, o_full, den_full = full.values()
        a_done, d_done, o_done, den_done = done.values()
        moments_ready = counts("moments_ready", "moments")
        rstd_ready = counts("rstd_ready", "rstd")
        xhat_ready = counts("xhat_ready", "xhat")
        xb_ready = counts("xb_ready", "xb")
        hi_ready = counts("hi_ready", "hi")
        rest_ready = counts("rest_ready", "rest")
        mid_ready = counts("mid_ready", "mid")
        lo_ready = counts("lo_ready", "lo")
        negmax_ready = counts("negmax_ready", "negmax")
        mask_ready = counts("mask_ready", "mask")
        tanh_ready = counts("tanh_ready", "tanh")
        poly_ready = counts("poly_ready", "poly")
        ff_ready = counts("ff_ready", "ff")
        stacks, spilled = {}, {}
        for s in range(PAIR):
            for w in ("project_q", "project_k"):
                stacks[w, s] = Count(sem(f"stack_{w[-1]}{s}"), [x for x in order["hi"] if x[0][:2] == (w, s)], 16 * SLOTS)
                spilled[w, s] = Count(sem(f"spilled_{w[-1]}{s}"), [x for x in order["hi"] if x[0][:2] == (w, s)], 16 * PARTS)
        loaded, per_load = [sem(f"loaded{s}") for s in range(PAIR)], 16 * res["loads"]
        stored = [Count(sem(f"stored{s}"), [x for x in order["store"] if x[0][1] == s], 16) for s in range(PAIR)]
        setup_dma, setup_v, setup_g, settled = sem("setup_dma"), sem("setup_v"), sem("setup_g"), sem("settled")
        dve_step, pool_step = counts("dve_step", "dve_step"), counts("pool_step", "pool_step")

        last_readers = res["x_readers"]

        block = ctx.enter_context(nc.Block())

        class Seen:

            def __init__(self):
                self.last = {}

            def new(self, count, tag=None):
                if tag is not None and Here.mode == "first" and not count.same_turn(tag):
                    return False
                at = -1 if tag is None else count.at[tag] - (0 if count.same_turn(tag) else len(count.tags))
                if self.last.get(id(count), -1 << 20) >= at:
                    return False
                self.last[id(count)] = at
                return True

        def settle(eng):
            eng.sem_inc(settled, 1)

        def slot_of(r, tag):
            return rings[r][full[r].at[tag] % len(rings[r])]

        @block.sync
        def _(sp):
            w = Seen()

            def load(turn, s):
                sp.dma_start(x_in[s][:, :, :], res["x"](turn, s)).then_inc(loaded[s], 16)
                sp.dma_start(c_in[s][:, :], res["ctx"](turn, s)).then_inc(loaded[s], 16)
                if wide:
                    sp.dma_start(m_in[s][:, :, :], res["mask"](turn, s)).then_inc(loaded[s], 16)

            every = [*full.values(), *done.values(), *stacks.values(), *spilled.values(), *stored, dve_step, pool_step,
                     moments_ready, rstd_ready, xhat_ready, xb_ready, hi_ready, rest_ready, mid_ready, lo_ready,
                     negmax_ready, mask_ready, tanh_ready, poly_ready, ff_ready]
            for count in every:
                sp.sem_inc(count.sem, count.start)
            n = 0
            with nc.allow_non_contiguous_dma(reason="biases and gains by feature, a few hundred words once"):
                for dst, src in res["weight_loads"]:
                    sp.dma_start(dst, src).then_inc(setup_dma, 16)
                    n += 1
            assert n == res["n_setup"], n
            for s in range(PAIR):
                load(0, s)

            def body(turn, mode, prefetch=True):
                w.last = {}
                for kind, s, key, a, j in steps(mode):
                    tag = (kind, s, key, j)
                    if kind in ("project_q", "project_k"):
                        i = 0 if kind == "project_q" else 1
                        nt = a.nk if i else T
                        done_before = stacks[kind, s]
                        if done_before.at[tag]:
                            if w.new(done_before, done_before.tags[done_before.at[tag] - 1]):
                                sp.wait_ge(done_before.sem, done_before.after(turn, done_before.tags[done_before.at[tag] - 1]))
                                sp.sem_inc(settled, 1)
                        else:
                            if w.new(done_before):
                                sp.wait_ge(done_before.sem, done_before.before(turn))
                                sp.sem_inc(settled, 1)
                        for part, ready in enumerate((hi_ready, mid_ready, lo_ready)):
                            if w.new(ready, tag):
                                sp.wait_ge(ready.sem, ready.after(turn, tag))
                                sp.sem_inc(settled, 1)
                            sp.dma_start(res["scratch"][s, i, part, :, :, 0:nt].rearrange("f p t -> p f t"),
                                         parts[s][:, i, part, :, 0:nt]).then_inc(spilled[kind, s].sem, 16)
                    if kind in ("project_k", "project_v"):
                        i = 0 if kind == "project_k" else 1
                        what = ("project_q", "project_k")[i]
                        nt = a.nk if i else T
                        stack = (qs, ks)[i][s]
                        if w.new(spilled[what, s], (what, s, key, 0)):
                            sp.wait_ge(spilled[what, s].sem, spilled[what, s].after(turn, (what, s, key, 0)))
                            sp.sem_inc(settled, 1)
                        for n, part in enumerate((Q_SLOTS, K_SLOTS)[i]):
                            src = res["scratch"][s, i, part, :, :, 0:nt].rearrange("f (h d) t -> d (f h) t", d=D)
                            sp.dma_start(stack[n * D:(n + 1) * D, :, 0:nt], src).then_inc(stacks[what, s].sem, 16)
                    if (kind, key) == res["prefetch_at"] and prefetch:
                        for count, t in last_readers(s, dict(xhat=xhat_ready, xb=xb_ready, a=a_full, ad=a_done,
                                                             d=d_done, mask=mask_ready)):
                            if w.new(count, t):
                                sp.wait_ge(count.sem, count.after(turn, t))
                                sp.sem_inc(settled, 1)
                        load(turn + 1, s)
                    if kind == "store":
                        if res["final_ln"]:
                            sp.wait_ge(xb_ready.sem, xb_ready.after(turn, ("final", s, "ln3", 0)))
                        else:
                            sp.wait_ge(d_done.sem, d_done.after(turn, ("ff_out", s, "ff", 0)))
                        sp.sem_inc(settled, 1)
                        sp.dma_start(res["out"](turn - 1 if late[Here.place] else turn, s), (xb if wide or res["final_ln"] else xn)[s][:, :, :])\
                          .then_inc(stored[s].sem, 16)

            body(0, "first")
            with sp.Fori(1, TURNS - 1) as turn:
                body(turn, "middle")
            body(TURNS - 1, "middle", prefetch=False)
            body(TURNS, "last")
            for s in range(PAIR):
                sp.wait_ge(stored[s].sem, 1 + TURNS * stored[s].per_turn + stored[s].step * sum(stored[s].late))

        @block.gpsimd
        def _(g):
            w = Seen()
            k = [0]

            def link(ins):
                k[0] += 1
                ins.then_inc(setup_g, 1)

            for t, v in res["zero"]:
                link(nc.gpsimd.memset(t, v))
            for s in range(PAIR):
                link(nc.gpsimd.memset(v_aug[s][:, :, :, :], 0.0))
                link(nc.gpsimd.memset(nm_t[s][:, :], 0.0))
                if wide:
                    link(nc.gpsimd.memset(kmask3[s][:, :, :], 0.0))
            g.wait_ge(setup_g, k[0])
            for s in range(PAIR):
                link(nc.gpsimd.memset(v_aug[s][:, :, :, D:D + 1], 1.0))
            g.wait_ge(setup_g, k[0])
            g.wait_ge(setup_dma, 16 * res["n_setup"])
            for dst, x, y in res["sums"]:
                link(nc.gpsimd.tensor_tensor(dst, x, y, ALU.add))
            g.wait_ge(setup_g, k[0])
            res["setup_total"] = k[0]

            def body(turn, mode):
                w.last = {}
                for kind, s, key, a, j in steps(mode):
                    tag = (kind, s, key, j)
                    if kind == "stats":
                        if w.new(moments_ready, tag):
                            g.wait_ge(moments_ready.sem, moments_ready.after(turn, tag))
                        settle(g)
                        nc.gpsimd.tensor_scalar(veps[s][:, :], meanvar[s][:, :, 1], a["eps"], None,
                                                ALU.add).then_inc(pool_step.sem, 1)
                        g.wait_ge(pool_step.sem, pool_step.after(turn, tag))
                        nc.gpsimd.tensor_tensor(rstd[s][:, :], veps[s][:, :], res["half"][:, 0:QT],
                                                                  ALU.pow).then_inc(rstd_ready.sem, 1)
                    if kind in ("norm", "turn", "final") and a.get("xb"):
                        how, src, m1, m2 = a["xb"]
                        if res["final_ln"]:
                            if w.new(stored[s], stored[s].tags[0]):
                                g.wait_ge(stored[s].sem, stored[s].after(turn, stored[s].tags[0]))
                        if how == "add":
                            if src == "x_in":
                                g.wait_ge(loaded[s], per_load * turn + per_load)
                                x = x_in[s]
                            else:
                                x = xn[s]
                                if w.new(d_done, a["sum_tag"]):
                                    g.wait_ge(d_done.sem, d_done.after(turn, a["sum_tag"]))
                            ins = nc.gpsimd.tensor_tensor(xb[s][:, :, :], x[:, :, :],
                                                          m2[:, None, :].broadcast_to((P, QT, C)), ALU.add)
                            ins.then_inc(xb_ready.sem, 1)
                        else:
                            if w.new(xhat_ready, tag):
                                g.wait_ge(xhat_ready.sem, xhat_ready.after(turn, tag))
                            settle(g)
                            nc.gpsimd.tensor_tensor(xb[s][:, :, :], xh[s][:, :, :],
                                                    m1[:, None, :].broadcast_to((P, QT, C)), ALU.mult)\
                              .then_inc(pool_step.sem, 1)
                            g.wait_ge(pool_step.sem, pool_step.after(turn, tag))
                            nc.gpsimd.tensor_tensor(xb[s][:, :, :], xb[s][:, :, :],
                                                                    m2[:, None, :].broadcast_to((P, QT, C)), ALU.add).then_inc(xb_ready.sem, 1)
                    if kind in ("project_q", "project_k"):
                        i = 0 if kind == "project_q" else 1
                        nt = a.nk if i else T
                        x32 = (q32, k32)[i][s][:, :, 0:nt]
                        if w.new(mid_ready, tag):
                            g.wait_ge(mid_ready.sem, mid_ready.after(turn, tag))
                        nc.gpsimd.tensor_tensor(parts[s][:, i, 2, :, 0:nt], x32,
                                                                parts[s][:, i, 1, :, 0:nt], ALU.subtract).then_inc(lo_ready.sem, 1)

            body(0, "first")
            with g.Fori(1, TURNS) as turn:
                body(turn, "middle")
            body(TURNS, "last")

        @block.scalar
        def _(act_e):
            w = Seen()
            act_e.wait_ge(setup_dma, 16 * res["n_setup"])
            act_e.wait_ge(setup_g, res["n_setup_g"])

            def affine(out, in_, scale, bias):
                return nc.scalar.activation(out, in_, ACT.Identity, scale=scale, bias=bias)

            def body(turn, mode):
                w.last = {}
                for kind, s, key, a, j in steps(mode):
                    tag = (kind, s, key, j)
                    if tag in a_full.at:
                        if w.new(a_full, tag):
                            act_e.wait_ge(a_full.sem, a_full.after(turn, tag))
                        bank = slot_of("a", tag)
                    if kind == "context":
                        nc.scalar.activation(ct[s][:, :, :], bank[:, 0:FT * S2].rearrange(
                            "p (f t) -> p f t", f=FT), ACT.Copy).then_inc(a_done.sem, 1)
                    elif kind == "norm":
                        for f in range(FT):
                            ins = affine(ht[s][:, f, :], bank[:, f * T:(f + 1) * T], a["g"][:, f:f + 1], a["b"][:, f:f + 1])
                        ins.then_inc(a_done.sem, 1)
                    elif kind == "turn":
                        nc.scalar.activation(ht[s][:, :, :], bank[:, :].rearrange(
                            "p (f t) -> p f t", f=FT), ACT.Copy).then_inc(a_done.sem, 1)
                    elif kind in ("project_q", "project_k"):
                        i = 0 if kind == "project_q" else 1
                        nt = a.nk if i else T
                        bias = (a.q, a.k)[i][1]
                        src = bank[:, 0:FT * nt].rearrange("p (f t) -> p f t", f=FT)
                        dst = (q32, k32)[i][s]
                        if bias is None:
                            ins = nc.scalar.activation(dst[:, :, 0:nt], src, ACT.Copy)
                        else:
                            for f in range(FT):
                                ins = nc.scalar.activation(dst[:, f, 0:nt], src[:, f, :], ACT.Identity,
                                                           bias=bias[:, f:f + 1])
                        ins.then_inc(a_done.sem, 1)
                    elif kind == "project_q3":
                        nc.scalar.activation(q3[s][:, 2 * j:2 * j + 2, :], bank[:, :].rearrange(
                            "p (f t) -> p f t", f=2), ACT.Copy).then_inc(a_done.sem, 1)
                    elif kind == "project_k3":
                        for odd in range(2):
                            r = slice(64 * odd, 64 * odd + 64)
                            ins = nc.scalar.activation(kmask3[s][r, 8 * j + odd:8 * j + 8:2, :],
                                                       bank[r, 0:4 * S2].rearrange("p (f t) -> p f t", f=4), ACT.Copy)
                        ins.then_inc(a_done.sem, 1)
                    elif kind == "scores_exp":
                        if a.cross:
                            n, rows = 2 * T, S2
                        else:
                            n, rows = (T + P if a.kind == "causal" else 2 * T), P
                        nc.scalar.activation(probs[s][0:rows, j % 3, 0:n], bank[0:rows, 0:n], ACT.Exp,
                                                              scale=a.scale).then_inc(a_done.sem, 1)
                    elif kind == "probs_v":
                        heads = a.exp_units()[j]
                        per = 8 if a.d == D else 4
                        if (heads[-1] + 1) % per == 0:
                            n = heads[-1] // per
                            ot = (kind, s, key, n)
                            if w.new(o_full, ot):
                                act_e.wait_ge(o_full.sem, o_full.after(turn, ot))
                            nc.scalar.activation(ot_raw[s][:, 512 * n:512 * n + 512],
                                                                  slot_of("o", ot)[:, :], ACT.Copy).then_inc(o_done.sem, 1)
                    elif kind == "ff_in":
                        for f in range(2):
                            b = a["b"][:, 2 * j + f:2 * j + f + 1]
                            src = bank[:, f * T:(f + 1) * T]
                            if act == "relu":
                                ins = nc.scalar.activation(ffh[s][:, 2 * j + f, :], src, ACT.Relu, bias=b)
                            else:
                                if f == 0 and j >= 2:
                                    if w.new(ff_ready, ("ff_mid", s, key, j - 2)):
                                        act_e.wait_ge(ff_ready.sem, ff_ready.after(turn, ("ff_mid", s, key, j - 2)))
                                nc.scalar.activation(g32[s][:, j % 2, 0, f, :], src, ACT.Identity, bias=b)
                                ins = nc.scalar.activation(g32[s][:, j % 2, 1, f, :], src, ACT.Square, bias=b)
                        ins.then_inc(a_done.sem, 1)
                    elif kind == "ff_mid" and act == "gelu":
                        if w.new(poly_ready, ("ff_in", s, key, j)):
                            act_e.wait_ge(poly_ready.sem, poly_ready.after(turn, ("ff_in", s, key, j)))
                        nc.scalar.activation(g32[s][:, j % 2, 1, :, :], g32[s][:, j % 2, 1, :, :],
                                                               ACT.Tanh, scale=GELU_C).then_inc(tanh_ready.sem, 1)

            body(0, "first")
            with act_e.Fori(1, TURNS) as turn:
                body(turn, "middle")
            body(TURNS, "last")

        @block.vector
        def _(dve):
            w = Seen()
            dve.wait_ge(setup_dma, 16 * res["n_setup"])
            dve.wait_ge(setup_g, res["n_setup_g"])
            v = nc.vector
            k = 0
            for ins in res["dve_setup"](v):
                k += 1
                ins.then_inc(setup_v, 1)
            assert k == res["n_setup_v"]
            dve.wait_ge(setup_v, k)

            sums = [u for u in units if u[0] == "normalise"]
            recip_before = {(u[0],) + u[1:3] + (u[4],): (p[0],) + p[1:3] + (p[4],)
                            for p, u in zip(sums[-1:] + sums[:-1], sums)}

            def body(turn, mode):
                w.last = {}
                for kind, s, key, a, j in steps(mode):
                    tag = (kind, s, key, j)
                    if kind == "stats":
                        if a["src"] == "x_in":
                            dve.wait_ge(loaded[s], per_load * turn + per_load)
                        x = x_in[s] if a["src"] == "x_in" else xn[s]
                        for t in range(QT):
                            ins = v.bn_stats(moments[s][:, t, :], x[:, t, :])
                        ins.then_inc(dve_step.sem, 1)
                        dve.wait_ge(dve_step.sem, dve_step.after(turn, tag + (0,)))
                        settle(dve)
                        for t in range(QT):
                            ins = v.bn_aggr(meanvar[s][:, t, :], moments[s][:, t, :])
                        ins.then_inc(moments_ready.sem, 1)
                    elif kind in ("norm", "final"):
                        if w.new(moments_ready, ("stats", s, key, 0)):
                            dve.wait_ge(moments_ready.sem, moments_ready.after(turn, ("stats", s, key, 0)))
                        if w.new(rstd_ready, ("stats", s, key, 0)):
                            dve.wait_ge(rstd_ready.sem, rstd_ready.after(turn, ("stats", s, key, 0)))
                        x = x_in[s] if a["src"] == "x_in" else xn[s]
                        for t in range(QT):
                            ins = v.tensor_scalar(xh[s][:, t, :], x[:, t, :], meanvar[s][:, t, 0:1], rstd[s][:, t:t + 1],
                                                  ALU.subtract, ALU.mult)
                        ins.then_inc(xhat_ready.sem, 1)
                    elif kind == "mask":
                        dve.wait_ge(loaded[s], per_load * turn + per_load)
                        v.tensor_scalar(m_rows[s][:, :, :], m_in[s][:, :, :], 0.0, -BIG,
                                                          ALU.not_equal, ALU.mult).then_inc(mask_ready.sem, 1)
                        if w.new(d_full, tag):
                            dve.wait_ge(d_full.sem, d_full.after(turn, tag))
                        v.tensor_copy(m_cols[s][:, :], slot_of("d", tag)[0:S2, 0:T // 2].bitcast(BF16)).then_inc(d_done.sem, 1)
                    elif kind in ("project_q", "project_k"):
                        i = 0 if kind == "project_q" else 1
                        nt = a.nk if i else T
                        x32 = (q32, k32)[i][s][:, :, 0:nt]
                        pt = [parts[s][:, i, n, :, 0:nt] for n in range(PARTS)]
                        if w.new(a_done, tag):
                            dve.wait_ge(a_done.sem, a_done.after(turn, tag))
                        v.tensor_copy(pt[0], x32).then_inc(hi_ready.sem, 1)
                        if w.new(hi_ready, tag):
                            dve.wait_ge(hi_ready.sem, hi_ready.after(turn, tag))
                        v.tensor_tensor(x32, x32, pt[0], ALU.subtract).then_inc(rest_ready.sem, 1)
                        if w.new(rest_ready, tag):
                            dve.wait_ge(rest_ready.sem, rest_ready.after(turn, tag))
                        v.tensor_copy(pt[1], x32).then_inc(mid_ready.sem, 1)
                    elif kind == "project_v":
                        if w.new(d_full, tag):
                            dve.wait_ge(d_full.sem, d_full.after(turn, tag))
                        bank = slot_of("d", tag)
                        kt, rows = (1, S2) if a.cross else (QT, P)
                        src = bank[0:rows, 0:kt * C].rearrange("p (k h d) -> p k h d", k=kt, d=D)
                        dst = v_aug[s][0:rows, 0:kt, :, 0:D]
                        if a.v_bias is None:
                            ins = v.tensor_copy(dst, src)
                        else:
                            for t in range(kt):
                                ins = v.tensor_tensor(dst[:, t], src[:, t],
                                                      a.v_bias[0:rows, :].rearrange("p (h d) -> p h d", d=D), ALU.add)
                        ins.then_inc(d_done.sem, 1)
                    elif kind == "project_v3":
                        if w.new(d_full, tag):
                            dve.wait_ge(d_full.sem, d_full.after(turn, tag))
                        v.tensor_copy(v3[s][:, 512 * j:512 * j + 512], slot_of("d", tag)[0:S2, :]).then_inc(d_done.sem, 1)
                    elif kind == "scores_max":
                        t, heads, nk = a.max_jobs()[j]
                        if w.new(d_full, tag):
                            dve.wait_ge(d_full.sem, d_full.after(turn, tag))
                        bank = slot_of("d", tag)
                        v.tensor_reduce(mx[s][:, t, heads[0]:heads[-1] + 1],
                                                         bank[:, 0:len(heads) * nk].rearrange("p (h k) -> p h k", k=nk),
                                                         AX_X, ALU.max).then_inc(d_done.sem, 1)
                    elif kind == "negate_max":
                        lim = 2.0 ** 90 if a.masked == "each" else 3.0e38
                        if w.new(d_done, ("scores_max", s, key, len(a.max_jobs()) - 1)):
                            dve.wait_ge(d_done.sem, d_done.after(turn, ("scores_max", s, key, len(a.max_jobs()) - 1)))
                        pt = nm_parts[s]
                        v.tensor_scalar(nmf[s][:, :, :], mx[s][:, :, :], -1.0, lim, ALU.mult, ALU.min).then_inc(dve_step.sem, 1)
                        dve.wait_ge(dve_step.sem, dve_step.after(turn, tag + (0,)))
                        v.tensor_copy(pt[:, :, 0, :], nmf[s][:, :, :]).then_inc(dve_step.sem, 1)
                        dve.wait_ge(dve_step.sem, dve_step.after(turn, tag + (1,)))
                        v.tensor_tensor(nmf[s][:, :, :], nmf[s][:, :, :], pt[:, :, 0, :], ALU.subtract).then_inc(dve_step.sem, 1)
                        dve.wait_ge(dve_step.sem, dve_step.after(turn, tag + (2,)))
                        v.tensor_copy(pt[:, :, 1, :], nmf[s][:, :, :]).then_inc(dve_step.sem, 1)
                        dve.wait_ge(dve_step.sem, dve_step.after(turn, tag + (3,)))
                        v.tensor_tensor(pt[:, :, 2, :], nmf[s][:, :, :], pt[:, :, 1, :], ALU.subtract).then_inc(negmax_ready.sem, 1)
                        if w.new(d_full, tag):
                            dve.wait_ge(d_full.sem, d_full.after(turn, tag))
                        v.tensor_copy(nm_t[s][0:PARTS * H, :],
                                                       slot_of("d", tag)[0:PARTS * H, 0:T // 2].bitcast(BF16)).then_inc(d_done.sem, 1)
                    elif kind == "probs_v":
                        if tag in den_full.at:
                            if w.new(den_full, tag):
                                dve.wait_ge(den_full.sem, den_full.after(turn, tag))
                            v.reciprocal(rden[s][:, :], bank_den[0:H, 0:T]).then_inc(den_done.sem, 1)
                    elif kind == "normalise":
                        if w.new(o_done, ("probs_v", s, key, j)):
                            dve.wait_ge(o_done.sem, o_done.after(turn, ("probs_v", s, key, j)))
                        if w.new(d_done, recip_before[tag]):
                            dve.wait_ge(d_done.sem, d_done.after(turn, recip_before[tag]))
                        if w.new(d_full, tag):
                            dve.wait_ge(d_full.sem, d_full.after(turn, tag))
                        v.reciprocal(recip[:, :], slot_of("d", tag)[:, :]).then_inc(dve_step.sem, 1)
                        dve.wait_ge(dve_step.sem, dve_step.after(turn, tag + (0,)))
                        v.tensor_tensor(ot_n[s][:, 2 * j:2 * j + 2, :], otr[s][:, 2 * j:2 * j + 2, :],
                                                         recip[:, :].rearrange("p (g t) -> p g t", g=2), ALU.mult).then_inc(d_done.sem, 1)
                    elif kind == "normalise3":
                        if w.new(o_done, ("probs_v", s, key, j)):
                            dve.wait_ge(o_done.sem, o_done.after(turn, ("probs_v", s, key, j)))
                        if w.new(d_full, tag):
                            dve.wait_ge(d_full.sem, d_full.after(turn, tag))
                        v.tensor_tensor(ot_n3[s][:, 2 * j:2 * j + 2, :],
                                                         ot_raw[s][:, 512 * j:512 * j + 512].rearrange("p (g t) -> p g t", g=2),
                                                         slot_of("d", tag)[:, :].rearrange("p (g t) -> p g t", g=2),
                                                         ALU.mult).then_inc(d_done.sem, 1)
                    elif kind in ("project_out", "ff_out"):
                        if w.new(d_full, tag):
                            dve.wait_ge(d_full.sem, d_full.after(turn, tag))
                        bank = slot_of("d", tag)[:, :].rearrange("p (t c) -> p t c", t=QT)
                        half = kind == "ff_out" and act == "gelu"
                        if kind == "project_out" and a.res == "x_in":
                            other = x_in[s]
                        else:
                            other = xb[s]
                            if w.new(xb_ready, res["xb_for"][s, kind, key]):
                                dve.wait_ge(xb_ready.sem, xb_ready.after(turn, res["xb_for"][s, kind, key]))
                        if not (wide or res["final_ln"]):
                            if w.new(stored[s], stored[s].tags[0]):
                                dve.wait_ge(stored[s].sem, stored[s].after(turn, stored[s].tags[0]))
                        if half:
                            ins = v.scalar_tensor_tensor(xn[s][:, :, :], bank, 0.5, other[:, :, :], ALU.mult, ALU.add)
                        else:
                            ins = v.tensor_tensor(xn[s][:, :, :], bank, other[:, :, :], ALU.add)
                        ins.then_inc(d_done.sem, 1)
                        if w.new(d_done, tag):
                            dve.wait_ge(d_done.sem, d_done.after(turn, tag))
                    elif kind == "ff_in" and act == "gelu":
                        if w.new(a_done, tag):
                            dve.wait_ge(a_done.sem, a_done.after(turn, tag))
                        x, sq = g32[s][:, j % 2, 0], g32[s][:, j % 2, 1]
                        v.tensor_scalar(sq, sq, GELU_A, 1.0, ALU.mult, ALU.add).then_inc(dve_step.sem, 1)
                        dve.wait_ge(dve_step.sem, dve_step.after(turn, tag + (0,)))
                        v.tensor_tensor(sq, sq, x, ALU.mult).then_inc(poly_ready.sem, 1)
                    elif kind == "ff_mid" and act == "gelu":
                        if w.new(tanh_ready, tag):
                            dve.wait_ge(tanh_ready.sem, tanh_ready.after(turn, tag))
                        v.scalar_tensor_tensor(ffh[s][:, 2 * j:2 * j + 2, :], g32[s][:, j % 2, 1], 1.0,
                                                               g32[s][:, j % 2, 0], ALU.add, ALU.mult).then_inc(ff_ready.sem, 1)

            body(0, "first")
            with dve.Fori(1, TURNS) as turn:
                body(turn, "middle")
            body(TURNS, "last")

        @block.tensor
        def _(pe):
            w = Seen()
            pe.wait_ge(setup_dma, 16 * res["n_setup"])
            pe.wait_ge(setup_g, res["n_setup_g"])
            pe.wait_ge(setup_v, res["n_setup_v"])
            ident, identb, sel, sel_den = res["ident"], res["identb"], res["sel"], res["sel_den"]

            def mm(out, lhsT, rhs, first):
                return nc.tensor.matmul(out, lhsT, rhs, start=first, stop=True, skip_group_check=True)

            def body(turn, mode):
                w.last = {}

                def take(r, tag):
                    n = full[r].at[tag]
                    if n < len(rings[r]):
                        if w.new(done[r]):
                            pe.wait_ge(done[r].sem, done[r].before(turn))
                    else:
                        if w.new(done[r], full[r].tags[n - len(rings[r])]):
                            pe.wait_ge(done[r].sem, done[r].after(turn, full[r].tags[n - len(rings[r])]))
                    return slot_of(r, tag)

                for kind, s, key, a, j in steps(mode):
                    tag = (kind, s, key, j)
                    if kind == "context":
                        pe.wait_ge(loaded[s], per_load * turn + per_load)
                        bank = take("a", tag)
                        for f in range(FT):
                            ins = nc.tensor.transpose(bank[:, f * S2:(f + 1) * S2], c_in[s][:, f * P:(f + 1) * P],
                                                      ident[0:S2, 0:S2])
                        ins.then_inc(a_full.sem, 1)
                    elif kind in ("norm", "turn"):
                        if kind == "norm":
                            if w.new(xhat_ready, tag):
                                pe.wait_ge(xhat_ready.sem, xhat_ready.after(turn, tag))
                            x = xh[s]
                        else:
                            pe.wait_ge(loaded[s], per_load * turn + per_load)
                            x = x_in[s]
                        bank = take("a", tag)
                        for f in range(FT):
                            for t in range(QT):
                                ins = nc.tensor.transpose(bank[:, f * T + t * P:f * T + (t + 1) * P],
                                                          x[:, t, f * P:(f + 1) * P], ident[:, :])
                        ins.then_inc(a_full.sem, 1)
                    elif kind == "mask":
                        if w.new(mask_ready, tag):
                            pe.wait_ge(mask_ready.sem, mask_ready.after(turn, tag))
                        bank = take("d", tag)
                        for t in range(QT):
                            ins = nc.tensor.transpose(bank[0:S2, t * P // 2:(t + 1) * P // 2].bitcast(BF16),
                                                      m_rows[s][:, t, :], identb[:, :])
                        ins.then_inc(d_full.sem, 1)
                    elif kind in ("project_q", "project_k", "project_q3", "project_k3", "ff_in"):
                        if kind == "ff_in":
                            wt, x, xt, nt, n, fs = a["w"], ht[s], a["x_tag"], T, 2, (2 * j, 2 * j + 2)
                        elif kind in ("project_q", "project_q3"):
                            wt, x, xt, nt, n = a.q[0], ht[s], a.q[2], T, 2
                            fs = (2 * j, 2 * j + 2) if kind == "project_q3" else (0, FT)
                        else:
                            src = "c" if a.cross else "h"
                            wt, x, nt, xt = a.k[0], (ct if a.cross else ht)[s], a.nk, a.k[2]
                            fs = (4 * j, 4 * j + 4) if kind == "project_k3" else (0, FT)
                        if w.new(a_done, (xt[0], s) + xt[1:]):
                            pe.wait_ge(a_done.sem, a_done.after(turn, (xt[0], s) + xt[1:]))
                        bank = take("a", tag)
                        for m, f in enumerate(range(*fs)):
                            for c in range(FT):
                                ins = mm(bank[:, m * nt:(m + 1) * nt], wt[:, c, f * P:(f + 1) * P], x[:, c, 0:nt], c == 0)
                        ins.then_inc(a_full.sem, 1)
                    elif kind in ("project_v", "project_v3"):
                        xt = a.v[2]
                        if w.new(a_done, (xt[0], s) + xt[1:]):
                            pe.wait_ge(a_done.sem, a_done.after(turn, (xt[0], s) + xt[1:]))
                        bank = take("d", tag)
                        if kind == "project_v3":
                            for c in range(FT):
                                ins = mm(bank[0:S2, :], ct[s][:, c, :], a.v[0][:, c, 512 * j:512 * j + 512], c == 0)
                        else:
                            kt, rows = (1, S2) if a.cross else (QT, P)
                            x = (ct if a.cross else ht)[s]
                            for t in range(kt):
                                for c in range(FT):
                                    ins = mm(bank[0:rows, t * C:(t + 1) * C], x[:, c, t * rows:(t + 1) * rows],
                                             a.v[0][:, c, :], c == 0)
                        ins.then_inc(d_full.sem, 1)
                    elif kind == "scores_max":
                        t, heads, nk = a.max_jobs()[j]
                        if j == 0 and a.d == D:
                            if w.new(stacks["project_q", s], ("project_q", s, key, 0)):
                                pe.wait_ge(stacks["project_q", s].sem, stacks["project_q", s].after(turn, ("project_q", s, key, 0)))
                            if w.new(stacks["project_k", s], ("project_k", s, key, 0)):
                                pe.wait_ge(stacks["project_k", s].sem, stacks["project_k", s].after(turn, ("project_k", s, key, 0)))
                        elif j == 0:
                            if w.new(a_done, ("project_k3", s, key, FT3 // 4 - 1)):
                                pe.wait_ge(a_done.sem, a_done.after(turn, ("project_k3", s, key, FT3 // 4 - 1)))
                        bank = take("d", tag)
                        if a.d == D:
                            for n, h in enumerate(heads):
                                ins = mm(bank[:, n * nk:(n + 1) * nk], qs[s][0:KS, h, t * P:(t + 1) * P],
                                         ks[s][0:KS, h, 0:nk], n == 0)
                        else:
                            for n in range(0, len(heads), 2):
                                h = heads[n]
                                ins = mm(bank[:, n * nk:(n + 2) * nk], q3[s][:, h // 2, t * P:(t + 1) * P],
                                         kmask3[s][:, h:h + 2, :], n == 0)
                        n = len(heads)
                        whole = bank[:, 0:n * nk].rearrange("p (h k) -> p h k", k=nk)
                        if a.kind == "causal":
                            ins = mm(whole[:, :, nk - P:nk], identb[:, :],
                                     res["causal_rows"][:, None, :].broadcast_to((P, n, P)), False)
                        elif a.masked == "all":
                            ins = mm(whole, identb[:, :], res["mask_rows"][:, t, None, :].broadcast_to((P, n, nk)), False)
                        elif a.masked == "each":
                            if j == 0:
                                if w.new(mask_ready, ("mask", s, "mask", 0)):
                                    pe.wait_ge(mask_ready.sem, mask_ready.after(turn, ("mask", s, "mask", 0)))
                            ins = mm(whole, identb[:, :], m_rows[s][:, t, None, :].broadcast_to((P, n, nk)), False)
                        ins.then_inc(d_full.sem, 1)
                    elif kind == "negate_max":
                        if w.new(negmax_ready, tag):
                            pe.wait_ge(negmax_ready.sem, negmax_ready.after(turn, tag))
                        bank = take("d", tag)
                        settle(pe)
                        for t in range(QT):
                            ins = nc.tensor.transpose(bank[0:PARTS * H, t * P // 2:(t + 1) * P // 2].bitcast(BF16),
                                                      nm_parts[s][:, t, :, :].rearrange("p a h -> p (a h)"), identb[:, :])
                        ins.then_inc(d_full.sem, 1)
                    elif kind == "scores_exp":
                        if j == 0:
                            if w.new(d_done, ("negate_max", s, key, 0)):
                                pe.wait_ge(d_done.sem, d_done.after(turn, ("negate_max", s, key, 0)))
                            if a.masked == "each":
                                if w.new(d_done, ("mask", s, "mask", 0)):
                                    pe.wait_ge(d_done.sem, d_done.after(turn, ("mask", s, "mask", 0)))
                        bank = take("a", tag)
                        heads = a.exp_units()[j]
                        if a.cross:
                            for n, h in enumerate(heads):
                                out = bank[0:S2, n * T:(n + 1) * T]
                                if a.d == D:
                                    mm(out, ks[s][0:KS, h, 0:S2], qs[s][0:KS, h, :], n == 0)
                                else:
                                    mm(out, kmask3[s][:, h, :], q3[s][:, h // 2, :], n == 0)
                            for n, h in enumerate(heads):
                                ins = mm(bank[0:S2, n * T:(n + 1) * T], sel[:, h, 0:S2], nm_t[s][:, :], False)
                            if a.masked == "each":
                                ins = mm(bank[0:S2, :].rearrange("p (h t) -> p h t", h=2), identb[0:S2, 0:S2],
                                         m_cols[s][:, None, :].broadcast_to((S2, 2, T)), False)
                        else:
                            h = heads[0]
                            if a.kind == "causal":
                                mm(bank[:, 0:T], ks[s][0:KS, h, 0:P], qs[s][0:KS, h, :], True)
                                mm(bank[:, T:T + P], ks[s][0:KS, h, P:T], qs[s][0:KS, h, P:T], False)
                                mm(bank[:, 0:T], sel[:, h, :], nm_t[s][:, :], False)
                                mm(bank[:, T:T + P], sel[:, h, :], nm_t[s][:, P:T], False)
                                ins = mm(bank[:, :].rearrange("p (k t) -> p k t", k=2)[:, :, 0:P], identb[:, :],
                                         res["causal_cols"][:, None, :].broadcast_to((P, 2, P)), False)
                            else:
                                for t in range(QT):
                                    mm(bank[:, t * T:(t + 1) * T], ks[s][0:KS, h, t * P:(t + 1) * P], qs[s][0:KS, h, :], t == 0)
                                ins = mm(bank[:, :].rearrange("p (k t) -> p k t", k=2), sel[:, h, :],
                                         nm_t[s][:, None, :].broadcast_to((P, 2, T)), False)
                                if a.masked == "all":
                                    ins = mm(bank[:, :], identb[:, :], res["mask_cols"][:, :, :].rearrange("p k t -> p (k t)"),
                                             False)
                        ins.then_inc(a_full.sem, 1)
                    elif kind == "probs_v":
                        heads = a.exp_units()[j]
                        if w.new(a_done, ("scores_exp", s, key, j)):
                            pe.wait_ge(a_done.sem, a_done.after(turn, ("scores_exp", s, key, j)))
                        if j == 0:
                            vt = "project_v" if a.d == D else "project_v3"
                            if w.new(d_done, (vt, s, key, 0 if a.d == D else 1)):
                                pe.wait_ge(d_done.sem, d_done.after(turn, (vt, s, key, 0 if a.d == D else 1)))
                        for n, h in enumerate(heads):
                            pr = probs[s][:, j % 3, :]
                            if a.d == D:
                                ot = (kind, s, key, h // 8)
                                if h % 8 == 0:
                                    take("o", ot)
                                out = slot_of("o", ot)[32 * (h % HG):32 * (h % HG) + 32, :].rearrange(
                                    "p (g t) -> p g t", g=2)[:, (h // HG) % 2, :]
                                if a.cross:
                                    ins = mm(out, v_aug[s][0:S2, 0, h, :], pr[0:S2, n * T:(n + 1) * T], True)
                                elif a.kind == "causal":
                                    mm(out, v_aug[s][:, 0, h, :], pr[:, 0:T], True)
                                    ins = mm(out[:, P:T], v_aug[s][:, 1, h, :], pr[:, T:T + P], False)
                                else:
                                    for t in range(QT):
                                        ins = mm(out, v_aug[s][:, t, h, :], pr[:, t * T:(t + 1) * T], t == 0)
                                if h % 8 == 7:
                                    ins.then_inc(o_full.sem, 1)
                            else:
                                ot = (kind, s, key, h // 4)
                                if h % 4 == 0:
                                    take("o", ot)
                                if h == 0:
                                    take("den", (kind, s, key, H // 2 - 1))
                                mm(bank_den[0:32, 0:T], res["onehot"][0:S2, 31 - h:63 - h], pr[0:S2, n * T:(n + 1) * T],
                                   h == 0) if h < H - 1 else mm(bank_den[0:32, 0:T], res["onehot"][0:S2, 31 - h:63 - h],
                                          pr[0:S2, n * T:(n + 1) * T], False).then_inc(den_full.sem, 1)
                                half = (h // 2) % 2
                                out = slot_of("o", ot)[64 * (h % 2):64 * (h % 2) + 64, half * T:(half + 1) * T]
                                ins = mm(out, v3[s][:, h * D3:(h + 1) * D3], pr[0:S2, n * T:(n + 1) * T], True)
                                if h % 4 == 3:
                                    ins.then_inc(o_full.sem, 1)
                    elif kind == "normalise":
                        if w.new(o_done, ("probs_v", s, key, j)):
                            pe.wait_ge(o_done.sem, o_done.after(turn, ("probs_v", s, key, j)))
                        bank = take("d", tag)
                        mm(bank[:, :], sel_den[:, :], ot_raw[s][:, 512 * j:512 * j + 512], True).then_inc(d_full.sem, 1)
                    elif kind == "normalise3":
                        if j == 0:
                            if w.new(den_done, ("probs_v", s, key, H // 2 - 1)):
                                pe.wait_ge(den_done.sem, den_done.after(turn, ("probs_v", s, key, H // 2 - 1)))
                        bank = take("d", tag)
                        for n in range(2):
                            ins = mm(bank[:, n * T:(n + 1) * T], res["sel_pair"][:, 2 * j + n, :], rden[s][:, :], n == 0)
                        ins.then_inc(d_full.sem, 1)
                    elif kind in ("project_out", "ff_out"):
                        if kind == "ff_out":
                            wt, x, n = a["w"], ffh[s], 8
                            if act == "gelu":
                                if w.new(ff_ready, ("ff_mid", s, key, 3)):
                                    pe.wait_ge(ff_ready.sem, ff_ready.after(turn, ("ff_mid", s, key, 3)))
                            else:
                                if w.new(a_done, ("ff_in", s, key, 3)):
                                    pe.wait_ge(a_done.sem, a_done.after(turn, ("ff_in", s, key, 3)))
                        else:
                            wt, n = a.o, (G if a.d == D else FT3)
                            x = ot_n[s] if a.d == D else ot_n3[s]
                            if w.new(d_done, (("normalise", s, key, 1) if a.d == D else ("normalise3", s, key, 3))):
                                pe.wait_ge(d_done.sem, d_done.after(turn, (("normalise", s, key, 1) if a.d == D else ("normalise3", s, key, 3))))
                        bank = take("d", tag)
                        for t in range(QT):
                            for c in range(n):
                                ins = mm(bank[:, t * C:(t + 1) * C], x[:, c, t * P:(t + 1) * P], wt[:, c, :], c == 0)
                        ins.then_inc(d_full.sem, 1)

            body(0, "first")
            with pe.Fori(1, TURNS) as turn:
                body(turn, "middle")
            body(TURNS, "last")


def build(nc, ins, out):
    x1 = nc.dram_tensor("between_0_1", (NB, T, C), F32).ap()
    x2 = nc.dram_tensor("between_1_2", (NB, T, C), F32).ap()
    scratch = nc.dram_tensor("parts", (PAIR, 2, PARTS, FT, P, T), BF16).ap()

    def rows(t, turn, s):
        v = t.rearrange("(i s) (q p) c -> i s p q c", s=PAIR, p=P)
        return v[turn, s]

    def context(turn, s):
        return ins["ctx_1024"].rearrange("(i s) t c -> i s t c", s=PAIR)[turn, s]

    def common(ctx, name, want):
        def sb(n, shape, dt=F32):
            return ctx.enter_context(nc.sbuf_tensor(f"{name}_{n}", shape, dt))
        r = {"scratch": scratch, "zero": [], "weight_loads": [], "sums": [], "sb": sb, "name": name}
        r["ident"] = sb("ident", [P, P])
        r["identb"] = sb("identb", [P, P], BF16)
        r["sel"] = sb("sel", [P, H, P], BF16)
        r["sel_den"] = sb("sel_den", [P, P])
        r["half"] = sb("half", [P, QT])
        r["zero"].append((r["half"][:, :], -0.5))
        return r

    def weight(r, n, src, width=None):
        k, m = src.shape
        t = r["sb"](n, [P, k // P, m])
        r["weight_loads"].append((t[:, :, :], src.rearrange("(c p) n -> p c n", p=P)))
        return t

    def padded(r, n, src):
        t = r["sb"](n, [P, G, C])
        v = src.rearrange("(g j d) n -> j d g n", j=HG, d=D)
        for j in range(HG):
            r["weight_loads"].append((t[32 * j:32 * j + D, :, :], v[j]))
        r["padded"].append(t)
        return t

    def column(r, n, src):
        k = src.shape[0] // P
        t = r["sb"](n, [P, k])
        r["weight_loads"].append((t[:, :], src.rearrange("(c p) -> p c", p=P)))
        return t

    def spread(r, n, src):
        t = r["sb"](n, [P, C])
        r["weight_loads"].append((t[:, :], src.partition_broadcast(P)))
        return t

    def prepare(r, name):
        with ExitStack() as c:
            zeroed = c.enter_context(nc.semaphore(f"{name}_zeroed"))
            made = c.enter_context(nc.semaphore(f"{name}_made"))
            block = c.enter_context(nc.Block())

            @block.gpsimd
            def _(g):
                n = 0
                for t in [r["ident"], r["identb"], r["sel"], r["sel_den"]] + r["padded"] + r["selectors"]:
                    nc.gpsimd.memset(t[tuple(slice(None) for _ in t.shape)], 0.0).then_inc(zeroed, 1)
                    n += 1
                g.wait_ge(zeroed, n)
                k = 0

                def select(v, op, fill, base, pattern, mult):
                    nonlocal k
                    nc.gpsimd.affine_select(out=v, in_=v, compare_op=op, fill=fill, base=base, pattern=pattern,
                                            channel_multiplier=mult).then_inc(made, 1)
                    k += 1
                    g.wait_ge(made, k)

                for t in (r["ident"], r["identb"]):
                    select(t[:, :], ALU.not_equal, 1.0, 0, [[-1, P]], 1)
                for part in range(PARTS):
                    select(r["sel"][:, :, :], ALU.not_equal, 1.0, -H * part, [[-1, H], [0, P]], 1)
                select(r["sel_den"][:, :].rearrange("p (j d) -> p j d", j=HG), ALU.not_equal, 1.0, -D,
                       [[-32, HG], [0, 32]], 1)
                if "causal_rows" in r:
                    select(r["causal_rows"][:, :], ALU.is_ge, -BIG, 0, [[-1, P]], 1)
                    select(r["causal_cols"][:, :], ALU.is_ge, -BIG, 0, [[1, P]], -1)
                if "onehot" in r:
                    nc.gpsimd.memset(r["onehot"][:, 31:32], 1.0).then_inc(made, 1)
                    k += 1
                    select(r["sel_pair"][:, :, :].rearrange("p a (b d) -> p a b d", b=2), ALU.not_equal, 1.0, 0,
                           [[-2, FT3], [-1, 2], [0, D3]], 1)
                g.wait_ge(made, k)

    def xb_tags(streams):
        last, found = {}, {}
        for s in range(PAIR):
            for kind, _, key, a, j in streams[s]:
                if kind in ("norm", "turn", "final") and a.get("xb"):
                    last[s] = (kind, s, key, j)
                if kind in ("project_out", "ff_out"):
                    found[s, kind, key] = last.get(s)
        return found

    with ExitStack() as ctx:
        r = common(ctx, "l0", None)
        r["padded"], sb = [], r["sb"]
        r["causal_rows"], r["causal_cols"] = sb("causal_rows", [P, P], BF16), sb("causal_cols", [P, P], BF16)
        r["selectors"] = [r["causal_rows"], r["causal_cols"]]
        i = {k[len("L0_xattn_"):]: v for k, v in ins.items() if k.startswith("L0_")}
        w_attn, w_q, w_k, w_v = (weight(r, n, i[m]) for n, m in (("w_attn", "W_attn"), ("wq", "Wq"), ("wk", "Wk"), ("wv", "Wv")))
        w_ao, w_co = padded(r, "w_ao", i["W_aproj"]), padded(r, "w_co", i["Wcproj"])
        w_fc, w_mp = weight(r, "w_fc", i["W_fc"]), weight(r, "w_mp", i["W_mproj"])
        b_attn = i["b_attn"]
        bq0, bk0 = column(r, "bq0", b_attn[0:C]), column(r, "bk0", b_attn[C:2 * C])
        bv0 = spread(r, "bv0", b_attn[2 * C:3 * C])
        bq, bk, bv = column(r, "bq", i["bq"]), column(r, "bk", i["bk"]), spread(r, "bv", i["bv"])
        b_ao, b_co, b_mp = (spread(r, n, i[m]) for n, m in (("b_ao", "b_aproj"), ("b_co", "bcproj"), ("b_mp", "b_mproj")))
        b_fc = column(r, "b_fc", i["b_fc"])
        g1, b1, g2, b2 = (column(r, n, i[n]) for n in ("ln1_g", "ln1_b", "ln2_g", "ln2_b"))
        prepare(r, "l0p")
        streams = []
        for s in range(PAIR):
            h0, h1, c = ("norm", "ln0", 0), ("norm", "ln1", 0), ("context", "ctx", 0)
            own = Att("own", "causal", (w_attn[:, :, 0:C], bq0, h0), (w_attn[:, :, C:2 * C], bk0, h0),
                      (w_attn[:, :, 2 * C:3 * C], None, h0), w_ao, v_bias=bv0)
            other = Att("other", "cross", (w_q, bq, h1), (w_k, bk, c), (w_v, None, c), w_co, v_bias=bv)
            n0 = dict(src="x_in", eps=1e-5, g=g1, b=b1, xb=("add", "x_in", None, b_ao))
            n1 = dict(src="xn", eps=1e-5, g=g1, b=b1, xb=("add", "xn", None, b_co), sum_tag=("project_out", s, "own", 0))
            n2 = dict(src="xn", eps=1e-5, g=g2, b=b2, xb=("add", "xn", None, b_mp), sum_tag=("project_out", s, "other", 0))
            u = [("context", s, "ctx", None, 0), ("stats", s, "ln0", n0, 0), ("norm", s, "ln0", n0, 0)]
            u += att_units(s, own) + [("stats", s, "ln1", n1, 0), ("norm", s, "ln1", n1, 0)]
            u += att_units(s, other) + [("stats", s, "ln2", n2, 0), ("norm", s, "ln2", n2, 0)]
            f = dict(w=w_fc, b=b_fc, x_tag=("norm", "ln2", 0))
            for j in range(5):
                if j < 4:
                    u.append(("ff_in", s, "ff", f, j))
                if j:
                    u.append(("ff_mid", s, "ff", f, j - 1))
            u += [("ff_out", s, "ff", dict(w=w_mp), 0), ("store", s, "x", None, 0)]
            streams.append(u)
        r.update(wide=False, loads=2, final_ln=False, x=lambda t, s: rows(ins["x"], t, s), ctx=context,
                 out=lambda t, s: rows(x1, t, s), prefetch_at=("project_v", "own"), n_setup=len(r["weight_loads"]),
                 x_readers=lambda s, c: [(c["xhat"], ("norm", s, "ln0", 0)), (c["xb"], ("norm", s, "ln0", 0)),
                                         (c["a"], ("context", s, "ctx", 0))],
                 n_setup_g=len(r["zero"]) + 3 * PAIR, n_setup_v=0, dve_setup=lambda v: [],
                 xb_for=xb_tags(streams), late_from="statsln1")
        run_pass(nc, "l0", streams, r, "gelu")

    with ExitStack() as ctx:
        r = common(ctx, "l1", None)
        r["padded"], sb = [], r["sb"]
        r["selectors"] = []
        i = {k[len("L1_xattn_"):]: v for k, v in ins.items() if k.startswith("L1_")}
        wt = {n: weight(r, n, i[n + "_w"]) for n in ("q", "k", "v", "cq", "ck", "cv")}
        w_o, w_co = padded(r, "w_o", i["o_w"]), padded(r, "w_co", i["co_w"])
        w_1, w_2 = weight(r, "w_1", i["lin1_w"]), weight(r, "w_2", i["lin2_w"])
        col = {n: column(r, "c_" + n, i[n]) for n in ("q_b", "k_b", "cq_b", "ck_b", "lin1_b", "ln1_g", "ln1_b", "ln2_g", "ln2_b")}
        spr = {n: spread(r, "s_" + n, i[n]) for n in ("v_b", "cv_b", "o_b", "co_b", "lin2_b", "ln1_g", "ln1_b", "ln2_g",
                                                      "ln2_b", "ln3_g", "ln3_b")}
        r["sums"] = [(spr["ln1_b"][:, :], spr["ln1_b"][:, :], spr["co_b"][:, :]),
                     (spr["ln2_b"][:, :], spr["ln2_b"][:, :], spr["lin2_b"][:, :])]
        mask_i, mask_j = sb("mask_i", [P, QT, T], I32), sb("mask_j", [P, QT, T], I32)
        r["mask_rows"], r["mask_cols"] = sb("mask_rows", [P, QT, T], BF16), sb("mask_cols", [P, QT, T], BF16)
        m = ins["mask_SxS_ik1"]
        r["weight_loads"].append((mask_i[:, :, :], m.rearrange("(q p) k -> p q k", p=P)))
        r["weight_loads"].append((mask_j[:, :, :], ins["mask_by_key"].rearrange("(k p) q -> p k q", p=P)))
        prepare(r, "l1p")

        def masks(v):
            return [v.tensor_scalar(r["mask_rows"][:, :, :], mask_i[:, :, :], 0.0, -BIG, ALU.not_equal, ALU.mult),
                    v.tensor_scalar(r["mask_cols"][:, :, :], mask_j[:, :, :], 0.0, -BIG, ALU.not_equal, ALU.mult)]

        streams = []
        for s in range(PAIR):
            h0, h1, c = ("turn", "in", 0), ("norm", "ln1", 0), ("context", "ctx", 0)
            own = Att("own", "self", (wt["q"], col["q_b"], h0), (wt["k"], col["k_b"], h0), (wt["v"], None, h0), w_o,
                      masked="all", v_bias=spr["v_b"])
            other = Att("other", "cross", (wt["cq"], col["cq_b"], h1), (wt["ck"], col["ck_b"], c), (wt["cv"], None, c),
                        w_co, v_bias=spr["cv_b"])
            n1 = dict(src="xn", eps=1e-5, g=col["ln1_g"], b=col["ln1_b"], xb=("scale", None, spr["ln1_g"], spr["ln1_b"]))
            n2 = dict(src="xn", eps=1e-5, g=col["ln2_g"], b=col["ln2_b"], xb=("scale", None, spr["ln2_g"], spr["ln2_b"]))
            n3 = dict(src="xn", eps=1e-5, xb=("scale", None, spr["ln3_g"], spr["ln3_b"]))
            u = [("context", s, "ctx", None, 0), ("turn", s, "in", dict(xb=("add", "x_in", None, spr["o_b"])), 0)]
            u += att_units(s, own) + [("stats", s, "ln1", n1, 0), ("norm", s, "ln1", n1, 0)]
            u += att_units(s, other) + [("stats", s, "ln2", n2, 0), ("norm", s, "ln2", n2, 0)]
            u += [("ff_in", s, "ff", dict(w=w_1, b=col["lin1_b"], x_tag=("norm", "ln2", 0)), j) for j in range(4)]
            u += [("ff_out", s, "ff", dict(w=w_2), 0), ("stats", s, "ln3", n3, 0), ("final", s, "ln3", n3, 0),
                  ("store", s, "x", None, 0)]
            streams.append(u)
        r.update(wide=False, loads=2, final_ln=True, x=lambda t, s: rows(x1, t, s), ctx=context,
                 out=lambda t, s: rows(x2, t, s), prefetch_at=("project_v", "own"), n_setup=len(r["weight_loads"]),
                 x_readers=lambda s, c: [(c["xb"], ("turn", s, "in", 0)), (c["a"], ("turn", s, "in", 0)),
                                         (c["a"], ("context", s, "ctx", 0))],
                 n_setup_g=len(r["zero"]) + 3 * PAIR + 2, n_setup_v=2, dve_setup=masks,
                 xb_for=xb_tags(streams), late_from="statsln1")
        run_pass(nc, "l1", streams, r, "relu")

    with ExitStack() as ctx:
        r = common(ctx, "l2", None)
        r["padded"], sb = [], r["sb"]
        r["onehot"], r["sel_pair"] = sb("onehot", [P, 63]), sb("sel_pair", [H, FT3, P])
        r["selectors"] = [r["onehot"], r["sel_pair"]]
        i = {k[3:]: v for k, v in ins.items() if k.startswith(("L2_", "L3_"))}
        w2 = {n: weight(r, "2" + n, ins["L2_xattn_w" + n]) for n in "qkv"}
        w2o = padded(r, "2o", ins["L2_xattn_wo"])
        w3 = {n: weight(r, "3" + n, ins["L3_xattn_w_" + n]) for n in ("q", "k", "v", "fc")}
        g2, b2 = column(r, "g2", ins["L2_xattn_gamma"]), column(r, "b2", ins["L2_xattn_beta"])
        g2s, b2s = spread(r, "g2s", ins["L2_xattn_gamma"]), spread(r, "b2s", ins["L2_xattn_beta"])
        g3s, b3s = spread(r, "g3s", ins["L3_xattn_ln_gamma"]), spread(r, "b3s", ins["L3_xattn_ln_beta"])
        prepare(r, "l2p")
        streams = []
        for s in range(PAIR):
            h0, h1, c = ("turn", "in", 0), ("norm", "ln2", 0), ("context", "ctx", 0)
            a2 = Att("two", "cross", (w2["q"], None, h0), (w2["k"], None, c), (w2["v"], None, c), w2o, masked="each",
                     res="x_in")
            a3 = Att("three", "cross", (w3["q"], None, h1), (w3["k"], None, c), (w3["v"], None, c), w3["fc"], d=D3)
            n2 = dict(src="xn", eps=1e-5, g=g2, b=b2, xb=("scale", None, g2s, b2s))
            n3 = dict(src="xn", eps=1e-6, xb=("scale", None, g3s, b3s))
            u = [("context", s, "ctx", None, 0), ("turn", s, "in", {}, 0), ("mask", s, "mask", None, 0)]
            u += att_units(s, a2) + [("stats", s, "ln2", n2, 0), ("norm", s, "ln2", n2, 0)]
            u += att_units(s, a3) + [("stats", s, "ln3", n3, 0), ("final", s, "ln3", n3, 0), ("store", s, "x", None, 0)]
            streams.append(u)
        mask = ins["mask_BxSxS2_bk1"].rearrange("(i s) (q p) k -> i s p q k", s=PAIR, p=P)
        r.update(wide=True, loads=3, final_ln=True, x=lambda t, s: rows(x2, t, s), ctx=context,
                 mask=lambda t, s: mask[t, s], out=lambda t, s: rows(out, t, s), prefetch_at=("project_out", "two"),
                 n_setup=len(r["weight_loads"]),
                 x_readers=lambda s, c: [(c["d"], ("project_out", s, "two", 0)), (c["a"], ("turn", s, "in", 0)),
                                         (c["a"], ("context", s, "ctx", 0)), (c["mask"], ("mask", s, "mask", 0))],
                 n_setup_g=len(r["zero"]) + 4 * PAIR, n_setup_v=0, dve_setup=lambda v: [],
                 xb_for=xb_tags(streams), late_from="statsln2")
        run_pass(nc, "l2", streams, r, None)


def kernel(**inputs):
    import numpy as _np
    import concourse.bacc as _bacc
    from concourse import mybir as _mybir
    from concourse.bass_utils import run_bass_kernel_spmd as _run

    nc = _bacc.Bacc("TRN2", target_bir_lowering=False, num_devices=1)
    arrays, aps = {}, {}
    inputs["mask_by_key"] = _np.asarray(inputs["mask_SxS_ik1"]).T
    for name, a in inputs.items():
        a = _np.ascontiguousarray(a)
        arrays[f"in_{name}"] = a
        aps[name] = nc.dram_tensor(f"in_{name}", a.shape, _mybir.dt.from_np(a.dtype), kind="ExternalInput").ap()
    out = nc.dram_tensor("out_0", (NB, T, C), F32, kind="ExternalOutput").ap()
    build(nc, aps, out)
    r = _run(nc, [arrays], core_ids=[0])
    return r.results[0]["out_0"]
```

```python
from contextlib import ExitStack

import concourse.bass as bass
from concourse import mybir

ALU = mybir.AluOpType
ACT = mybir.ActivationFunctionType
AX_X = mybir.AxisListType.X
F32 = mybir.dt.float32
BF16 = mybir.dt.bfloat16
U8 = mybir.dt.uint8
I32 = mybir.dt.int32

P = 128
NB, T, C = 32, 256, 256
S2 = 120
H = 16
D = C // H
D3 = 64
FF = 4 * C
QT = T // P
FT = C // P
PAIR = 2
TURNS = NB // PAIR
HG = 4
G = H // HG
FT3 = H * D3 // P
PARTS = 3
Q_SLOTS = (0, 0, 0, 1, 2, 1)
K_SLOTS = (2, 1, 0, 0, 0, 1)
SLOTS = len(Q_SLOTS)
KS = SLOTS * D
BIG = 2.0 ** 100
GELU_A = 0.044715
GELU_C = (2.0 / 3.141592653589793) ** 0.5


def slots_of(part, slots):
    at = [n for n, x in enumerate(slots) if x == part]
    return slice(at[0], at[-1] + 1, at[1] - at[0] if len(at) > 1 else 1)


def stack_place(h):
    return h % (H // FT) * FT + h // (H // FT)


class Att:

    def __init__(self, key, kind, q, k, v, o, bias="", masked=False, d=D, res="xb", v_bias=None, after=None, slots=6):
        self.key, self.kind, self.masked, self.d, self.res = key, kind, masked, d, res
        self.q, self.k, self.v, self.o = q, k, v, o
        self.v_bias, self.slots = v_bias, slots
        self.after = after
        self.cross = kind == "cross"
        self.nk = S2 if self.cross else T
        self.scale = float(d) ** -0.5

    def max_jobs(self):
        jobs = []
        for t in range(QT):
            nk = P if self.kind == "causal" and t == 0 else self.nk
            n = 4 if nk <= P else 2
            for h in range(0, H, n):
                jobs.append((t, list(range(h, h + n)), nk))
        return jobs

    def exp_units(self):
        n = 2 if self.cross else 1
        return [list(range(h, h + n)) for h in range(0, H, n)]

    def sum_units(self):
        n = len(self.exp_units())
        k = 1 if self.d != D else n * HG // H
        return [list(range(j, j + k)) for j in range(0, n, k)]


def att_units(s, a, following=None):
    nxt = following
    u = []
    if a.d == D:
        u += [("project_q", s, a.key, a, 0)]
        if a.after is None:
            u += [("project_k", s, a.key, a, 0), ("project_v", s, a.key, a, 0)]
    else:
        u += [("project_q3", s, a.key, a, j) for j in range(FT3 // 2)]
    if nxt and nxt.d != D:
        u += [("project_k3", s, nxt.key, nxt, j) for j in range(FT3 // 4)]
        u += [("project_v3", s, nxt.key, nxt, j) for j in range(2)]
    u += [("scores_max", s, a.key, a, j) for j in range(len(a.max_jobs()))]
    u += [("negate_max", s, a.key, a, 0)]
    n = len(a.exp_units())
    behind = min(2, a.slots - len(a.sum_units()[0]))
    for j in range(n + behind):
        if j < n:
            u.append(("scores_exp", s, a.key, a, j))
        u += [("probs_v", s, a.key, a, i) for i, taken in enumerate(a.sum_units()) if taken[-1] == j - behind]
    if a.d == D:
        u += [("denominators", s, a.key, a, 0)]
        u += [("normalise", s, a.key, a, j) for j in range(G // 2)]
    else:
        u += [("normalise3", s, a.key, a, j) for j in range(FT3 // 2)]
    if nxt and nxt.d == D:
        return u + [("project_k", s, nxt.key, nxt, 0), ("project_out", s, a.key, a, 0), ("project_v", s, nxt.key, nxt, 0)]
    return u + [("project_out", s, a.key, a, 0)]


WEIGHTS = {
    "l0": {
        "context": (340, "act", 370, 0, 0), "stats": (0, "dve", 1040, 1560, 0), "norm": (1800, "act", 700, 0, 0),
        "store": (0, "dve", 0, None, 0), "project_q": (1400, "act", 750, 11700, 0),
        "project_k": (1300, "act", 560, 12350, 0), "project_v": (910, "dve", 690, 0, 0),
        "scores_max": (300, "dve", 700, 0, 0), "negate_max": (180, "dve", 580, 3200, 1560),
        "scores_exp": (550, "act", 340, 0, 0), "probs_v": (440, "act", 0, 0, 0),
        "denominators": (880, "dve", 1490, 170, 1800), "normalise": (680, "dve", 790, 0, 0),
        "project_out": (2800, "dve", 560, 0, 100), "ff_in": (1490, "act", 1150, 0, 0),
        "ff_mid": (0, "act", 500, 800, 0), "ff_out": (5950, "dve", 600, 0, 0),
    },
    "l1": {
        "context": (430, "act", 320, 0, 0), "stats": (0, "dve", 1170, 840, 0), "norm": (2340, "act", 1040, 0, 0),
        "store": (0, "dve", 0, None, 0), "project_q": (1750, "act", 1040, 10350, 0),
        "project_k": (1430, "act", 1300, 13650, 0), "project_v": (1300, "dve", 600, 0, 0),
        "scores_max": (560, "dve", 610, 0, 0), "negate_max": (140, "dve", 500, 4400, 1300),
        "scores_exp": (380, "act", 590, 0, 0), "probs_v": (350, "act", 0, 0, 0),
        "denominators": (880, "dve", 1190, 200, 1080), "normalise": (600, "dve", 700, 0, 0),
        "project_out": (3280, "dve", 700, 0, 100), "ff_in": (2010, "act", 850, 0, 0),
        "ff_out": (7700, "dve", 800, 0, 0), "turn": (910, "act", 510, 0, 0), "final": (0, "dve", 700, None, 0),
    },
    "l2": {
        "context": (380, "act", 460, 0, 0), "stats": (0, "dve", 900, 840, 0), "norm": (1800, "act", 1250, 0, 0),
        "store": (0, "dve", 0, None, 0), "project_q": (1400, "act", 680, 9560, 0),
        "project_k": (1100, "act", 560, 11880, 0), "project_v": (1300, "dve", 780, 0, 0),
        "scores_max": (450, "dve", 770, 0, 0), "negate_max": (200, "dve", 500, 2720, 780),
        "scores_exp": (440, "act", 510, 0, 0), "probs_v": (190, "act", 0, 0, 0),
        "denominators": (630, "dve", 1700, 200, 720), "normalise": (850, "dve", 870, 0, 0),
        "project_out": (2700, "dve", 800, 0, 100), "turn": (700, "act", 780, 0, 0), "final": (0, "dve", 630, None, 0),
        "mask": (200, "dve", 500, 0, 0), "project_q3": (1220, "act", 500, 0, 0),
        "project_k3": (1700, "act", 1040, 0, 0), "project_v3": (1220, "dve", 420, 0, 0),
        "normalise3": (850, "dve", 610, 0, 4050),
    },
}
TAKES = {
    "norm": ("stats",), "final": ("stats",), "stats": ("project_out", "ff_out"), "project_q": ("norm", "turn"),
    "project_q3": ("norm",), "ff_in": ("norm",), "scores_max": ("project_q", "project_k", "project_q3", "project_k3"),
    "negate_max": ("scores_max",), "scores_exp": ("negate_max",), "probs_v": ("project_v",),
    "denominators": ("scores_exp",), "normalise": ("denominators",), "normalise3": ("scores_exp",),
    "project_out": ("normalise", "normalise3"), "ff_mid": ("ff_in",), "ff_out": ("ff_mid",),
}


def weave(a, b, times):
    out, left = [], [list(a), list(b)]
    usable = [{}, {}]
    pe, free, banks = 0, {"act": 0, "dve": 0}, {"act": [0, 0, 0], "dve": [0, 0]}

    def start(s):
        (kind, _, key, _, j), _ = left[s][0]
        at = max([usable[s].get(x, 0) for x in TAKES.get(kind, ())] + [0]) + times[kind][4]
        if kind == "probs_v":
            at = max(at, usable[s].get(("scores_exp", left[s][0][0][3].sum_units()[j][-1]), 0))
        if times[kind][0]:
            at = max(at, pe, banks[times[kind][1]][0] if kind != "probs_v" else 0)
        return at

    while left[0] or left[1]:
        s = min((s for s in range(PAIR) if left[s]), key=lambda s: (start(s), -len(left[s])))
        at = start(s)
        step = left[s].pop(0)
        kind, j = step[0][0], step[0][4]
        on_pe, engine, on_engine, then, _ = times[kind]
        if on_pe:
            pe = at + on_pe
        free[engine] = max(free[engine], at + on_pe) + on_engine
        if on_pe and kind != "probs_v":
            banks[engine] = banks[engine][1:] + [free[engine]]
        if then is not None:
            usable[s][kind] = free[engine] + then
            usable[s][kind, j] = free[engine] + then
        out.append(step)
    return out


class Here:

    place, mode = 0, "middle"


class Count:

    def __init__(self, sem, signals, step=1):
        self.sem, self.step = sem, step
        self.tags = [tag for tag, _, _ in signals]
        self.at = {tag: i for i, tag in enumerate(self.tags)}
        self.place = {tag: place for tag, place, _ in signals}
        self.late = [late for _, _, late in signals]
        self.per_turn = step * len(signals)
        self.start = 1 + step * sum(self.late)
        assert len(self.at) == len(signals)

    def same_turn(self, tag):
        return self.place[tag] <= Here.place

    def after(self, turn, tag):
        i = self.at[tag] + 1
        if Here.mode == "first":
            return self.start + (self.step * (i - sum(self.late[:i])) if self.same_turn(tag) else 0)
        if Here.mode == "last" and self.same_turn(tag):
            return 1 + turn * self.per_turn + self.step * sum(self.late[:i])
        return turn * self.per_turn + (1 + self.step * i - (0 if self.same_turn(tag) else self.per_turn))

    def before(self, turn):
        return self.start if Here.mode == "first" else 1 + turn * self.per_turn


def step_signals(u, act):
    kind, s, key, a, j = u
    t = (kind, s, key, j)
    sig = {}
    if kind in ("context", "norm", "turn", "project_q", "project_k", "project_q3", "project_k3", "scores_exp", "ff_in"):
        sig["a"] = [t]
    if kind in ("project_v", "project_v3", "scores_max", "negate_max", "denominators", "normalise", "normalise3", "project_out",
                "ff_out", "mask"):
        sig["d"] = [t]
    if kind == "probs_v":
        heads = a.exp_units()[a.sum_units()[j][-1]]
        per = 8 if a.d == D else 4
        if (heads[-1] + 1) % per == 0:
            sig["o"] = [(kind, s, key, heads[-1] // per)]
        if a.d != D and heads[-1] == H - 1:
            sig[f"den{s}"] = [t]
    if kind == "stats":
        sig["moments"] = sig["rstd"] = [t]
    if kind == "norm":
        sig["xhat"] = [t]
    if kind in ("norm", "turn", "final") and a.get("xb"):
        sig["xb"] = [t]
    if kind == "final":
        sig["xhat"] = [t]
    if kind in ("project_q", "project_k"):
        sig["hi"] = sig["mid"] = sig["rest"] = sig["lo"] = [t]
    if kind == "negate_max":
        sig["negmax"] = [t]
        if a.d == D:
            sig["nmrows"] = [t]
    if kind == "project_k" and act == "gelu" and not a.cross:
        sig["ones"] = [t]
    if kind == "store":
        sig["store"] = [t]
    links = {"stats": 1, "negate_max": 4, "ff_in": 1 if act == "gelu" else 0}.get(kind, 0)
    sig["dve_step"] = [t + (n,) for n in range(links)]
    scaled = kind in ("norm", "final") and a.get("xb") and a["xb"][0] == "scale"
    sig["pool_step"] = [t] if kind == "stats" or scaled else []
    if kind == "mask":
        sig["mask"] = [t]
    if kind == "ff_mid" and act == "gelu":
        sig["tanh"] = [t]
        sig["ff"] = [t]
    if kind == "ff_in" and act == "gelu":
        sig["poly"] = [t]
    return sig


def run_pass(nc, name, streams, res, act):
    late_from = res["late_from"]
    cut = [u[0] + u[2] for u in streams[1]].index(late_from)
    woven = weave([(u, False) for u in streams[0]],
                  [(u, True) for u in streams[1][cut:]] + [(u, False) for u in streams[1][:cut]], WEIGHTS[name])
    units = [u for u, _ in woven]
    late = [x for _, x in woven]

    def steps(mode):
        Here.mode = mode
        for Here.place, u in enumerate(units):
            if mode == "middle" or (mode == "last") == late[Here.place]:
                yield u

    order = {k: [] for k in ("store", "dve_step", "pool_step", "a", "d", "o", "den0", "den1", "moments", "rstd", "xhat", "xb", "hi", "mid", "rest", "lo", "negmax", "nmrows", "ones",
                             "mask", "tanh", "ff", "poly")}
    for place, u in enumerate(units):
        for k, tags in step_signals(u, act).items():
            order[k] += [(tag, place, late[place]) for tag in tags]
    with ExitStack() as ctx:
        def sb(n, shape, dt=F32):
            return ctx.enter_context(nc.sbuf_tensor(f"{name}_{n}", shape, dt))

        def two(n, shape, dt=F32):
            return [sb(f"{n}{s}", shape, dt) for s in range(PAIR)]

        def sem(n):
            return ctx.enter_context(nc.semaphore(f"{name}_{n}"))

        wide = res["wide"]
        x_in = two("x_in", [P, QT, C])
        c_in = two("c_in", [S2, C])
        xb = two("xb", [P, QT, C])
        xn = two("xn", [P, QT, C])
        xh = two("xh", [P, QT, C])
        ht = two("ht", [P, FT, T])
        ct = two("ct", [P, FT, S2])
        kstack = two("kstack", [P, H * T if not wide else H * 128], BF16)
        qstack = two("qstack", [P, 8 * T])
        parts = two("parts", [P, 2, PARTS, FT * T], BF16)
        ot_raw = two("ot_raw", [P, (FT3 if wide else G) * T])
        v_aug = two("v_aug", [P, QT, H, 32])
        slots = 3 if wide else 6
        probs = two("probs", [P, slots, 512])
        mx = two("mx", [P, QT, H])
        nmf = two("nmf", [P, QT, H])
        nm_parts = two("nm_parts", [P, QT, PARTS, H], BF16)
        nm_t = two("nm_t", [P, T], BF16)
        moments = two("moments", [P, QT, 6])
        meanvar = two("meanvar", [P, QT, 2])
        veps = two("veps", [P, QT])
        rstd = two("rstd", [P, QT])
        rden = two("rden", [P, T])
        if wide:
            ot_n3 = two("ot_n3", [P, FT3, T])
            kmask3 = two("kmask3", [P, H, S2])
            v3 = two("v3", [S2, H * D3])
            m_in = two("m_in", [P, QT, S2], U8)
            m_rows = two("m_rows", [P, QT, S2], BF16)
            m_cols = two("m_cols", [S2, T], BF16)
        q32 = [ot_raw[s][:, 0:512].rearrange("p (f t) -> p f t", f=FT) for s in range(PAIR)]
        k32 = [ot_raw[s][:, 512:1024].rearrange("p (f t) -> p f t", f=FT) for s in range(PAIR)]
        otr = [ot_raw[s][:, 0:G * T].rearrange("p (g t) -> p g t", g=G) for s in range(PAIR)]
        ot_n = two("ot_n", [P, G, T])
        qs = [qstack[s][:, :].bitcast(BF16).rearrange("p (h t) -> p h t", h=H) for s in range(PAIR)]
        ks = [{nk: kstack[s][:, 0:H * nk].rearrange("p (h t) -> p h t", h=H) for nk in ([S2] if wide else [S2, T])}
              for s in range(PAIR)]

        def part_cols(s, i, part, nt):
            return parts[s][:, i, part, 0:FT * nt].rearrange("p (f t) -> p f t", f=FT)

        ffh = [qstack[s][:, :].rearrange("p (f t) -> p f t", f=8) for s in range(PAIR)]
        q3 = ffh
        if not wide:
            g32 = [kstack[s][:, :].bitcast(F32).rearrange("p (c x f t) -> p c x f t", c=2, x=2, f=2) for s in range(PAIR)]

        na, nd, no = (2, 2, 3) if wide else (3, 3, 2)
        bank_a = [ctx.enter_context(nc.psum_tensor(f"{name}_bank_a{i}", [P, 512], F32)) for i in range(na)]
        bank_d = [ctx.enter_context(nc.psum_tensor(f"{name}_bank_d{i}", [P, 512], F32)) for i in range(nd)]
        bank_o = [ctx.enter_context(nc.psum_tensor(f"{name}_bank_o{i}", [P, 512], F32)) for i in range(no)]
        bank_den = ctx.enter_context(nc.psum_tensor(f"{name}_bank_den", [P, 512], F32)) if wide else None
        den_bank = [bank_den[64 * s:64 * s + 32, 0:T] if wide else None for s in range(PAIR)]
        rings = {"a": bank_a, "d": bank_d, "o": bank_o, "den0": den_bank[0:1], "den1": den_bank[1:2]}

        def counts(n, key, step=1):
            return Count(sem(n), order[key], step)

        full = {r: counts(f"{r}_full", r) for r in rings}
        done = {r: counts(f"{r}_done", r) for r in rings}
        a_full, d_full, o_full, *den_full = full.values()
        a_done, d_done, o_done, *den_done = done.values()
        moments_ready = counts("moments_ready", "moments")
        rstd_ready = counts("rstd_ready", "rstd")
        xhat_ready = counts("xhat_ready", "xhat")
        xb_ready = counts("xb_ready", "xb")
        hi_ready = counts("hi_ready", "hi")
        rest_ready = counts("rest_ready", "rest")
        mid_ready = counts("mid_ready", "mid")
        lo_ready = counts("lo_ready", "lo")
        negmax_ready = counts("negmax_ready", "negmax")
        mask_ready = counts("mask_ready", "mask")
        tanh_ready = counts("tanh_ready", "tanh")
        poly_ready = counts("poly_ready", "poly")
        ff_ready = counts("ff_ready", "ff")
        stacks, spilled = {}, {}
        for s in range(PAIR):
            for w in ("project_q", "project_k"):
                stacks[w, s] = Count(sem(f"stack_{w[-1]}{s}"), [x for x in order["hi"] if x[0][:2] == (w, s)], 16)
                spilled[w, s] = Count(sem(f"spilled_{w[-1]}{s}"), [x for x in order["hi"] if x[0][:2] == (w, s)], 16 * PARTS)
        loaded, per_load = [sem(f"loaded{s}") for s in range(PAIR)], 16 * res["loads"]
        stored = [Count(sem(f"stored{s}"), [x for x in order["store"] if x[0][1] == s], 16) for s in range(PAIR)]
        nm_rows = [Count(sem(f"nm_rows{s}"), [x for x in order["nmrows"] if x[0][1] == s], 16) for s in range(PAIR)]
        ones_rows = [Count(sem(f"ones_rows{s}"), [x for x in order["ones"] if x[0][1] == s], 16) for s in range(PAIR)]
        setup_dma, setup_v, setup_g, settled = sem("setup_dma"), sem("setup_v"), sem("setup_g"), sem("settled")
        setup_ones = sem("setup_ones")
        dve_step, pool_step = counts("dve_step", "dve_step"), counts("pool_step", "pool_step")

        last_readers = res["x_readers"]

        block = ctx.enter_context(nc.Block())

        class Seen:

            def __init__(self):
                self.last = {}

            def new(self, count, tag=None):
                if tag is not None and Here.mode == "first" and not count.same_turn(tag):
                    return False
                at = -1 if tag is None else count.at[tag] - (0 if count.same_turn(tag) else len(count.tags))
                if self.last.get(id(count), -1 << 20) >= at:
                    return False
                self.last[id(count)] = at
                return True

        def settle(eng):
            eng.sem_inc(settled, 1)

        def slot_of(r, tag):
            return rings[r][full[r].at[tag] % len(rings[r])]

        @block.sync
        def _(sp):
            w = Seen()

            def load(turn, s):
                sp.dma_start(x_in[s][:, :, :], res["x"](turn, s)).then_inc(loaded[s], 16)
                sp.dma_start(c_in[s][:, :], res["ctx"](turn, s)).then_inc(loaded[s], 16)
                if wide:
                    sp.dma_start(m_in[s][:, :, :], res["mask"](turn, s)).then_inc(loaded[s], 16)

            every = [*full.values(), *done.values(), *stacks.values(), *spilled.values(), *stored, *nm_rows, *ones_rows, dve_step, pool_step,
                     moments_ready, rstd_ready, xhat_ready, xb_ready, hi_ready, rest_ready, mid_ready, lo_ready,
                     negmax_ready, mask_ready, tanh_ready, poly_ready, ff_ready]
            for count in every:
                sp.sem_inc(count.sem, count.start)
            n = 0
            with nc.allow_non_contiguous_dma(reason="biases and gains by feature, a few hundred words once"):
                for dst, src in res["weight_loads"]:
                    sp.dma_start(dst, src).then_inc(setup_dma, 16)
                    n += 1
            assert n == res["n_setup"], n
            for s in range(PAIR):
                load(0, s)
            if act == "gelu":
                sp.wait_ge(setup_g, res["n_setup_g"])
                sp.dma_start(res["ones"], kstack[0][KS:KS + PARTS, :]).then_inc(setup_ones, 16)
                sp.wait_ge(setup_ones, 16)

            def body(turn, mode, prefetch=True):
                w.last = {}
                for kind, s, key, a, j in steps(mode):
                    tag = (kind, s, key, j)
                    if kind in ("project_q", "project_k"):
                        i = 0 if kind == "project_q" else 1
                        nt = a.nk if i else T
                        done_before = stacks[kind, s]
                        if done_before.at[tag]:
                            if w.new(done_before, done_before.tags[done_before.at[tag] - 1]):
                                sp.wait_ge(done_before.sem, done_before.after(turn, done_before.tags[done_before.at[tag] - 1]))
                                sp.sem_inc(settled, 1)
                        else:
                            if w.new(done_before):
                                sp.wait_ge(done_before.sem, done_before.before(turn))
                                sp.sem_inc(settled, 1)
                        for part, ready in enumerate((hi_ready, mid_ready, lo_ready)):
                            if w.new(ready, tag):
                                sp.wait_ge(ready.sem, ready.after(turn, tag))
                                sp.sem_inc(settled, 1)
                            where = slots_of(part, (Q_SLOTS, K_SLOTS)[i])
                            dst = res["scratch"][s, i, where, :, 0:FT * nt].rearrange("n p t -> p n t")
                            sp.dma_start(dst, parts[s][:, i, part, None, 0:FT * nt].broadcast_to(dst.shape))\
                              .then_inc(spilled[kind, s].sem, 16)
                    if kind == "project_v" or (kind == "project_k" and not a.after) or (kind == "project_q" and a.after):
                        i = 1 if kind == "project_v" else 0
                        what = ("project_q", "project_k")[i]
                        nt = a.nk if i else T
                        stack = (qstack[s][:, :].bitcast(BF16), kstack[s][:, :])[i]
                        if w.new(spilled[what, s], (what, s, key, 0)):
                            sp.wait_ge(spilled[what, s].sem, spilled[what, s].after(turn, (what, s, key, 0)))
                            sp.sem_inc(settled, 1)
                        runs = res["scratch"][s, i, :, :, 0:FT * nt].rearrange("n (d h) t -> (n d) h t", d=D)
                        sp.dma_start(stack[0:KS, 0:H * nt].rearrange("p (h t) -> p h t", h=H // FT), runs)\
                          .then_inc(stacks[what, s].sem, 16)
                        if (what, s, key, 0) in ones_rows[s].at:
                            sp.dma_start(kstack[s][KS:KS + PARTS, :], res["ones"]).then_inc(ones_rows[s].sem, 16)
                    if kind == "negate_max" and a.d == D:
                        if w.new(d_done, tag):
                            sp.wait_ge(d_done.sem, d_done.after(turn, tag))
                            sp.sem_inc(settled, 1)
                        sp.dma_start(qstack[s][:, :].bitcast(BF16)[KS:KS + PARTS, :], nm_t[s][0:PARTS * H, :])\
                          .then_inc(nm_rows[s].sem, 16)
                    if (kind, key) == res["prefetch_at"] and prefetch:
                        for count, t in last_readers(s, dict(xhat=xhat_ready, xb=xb_ready, a=a_full, ad=a_done,
                                                             d=d_done, mask=mask_ready)):
                            if w.new(count, t):
                                sp.wait_ge(count.sem, count.after(turn, t))
                                sp.sem_inc(settled, 1)
                        load(turn + 1, s)
                    if kind == "store":
                        if res["final_ln"]:
                            sp.wait_ge(xb_ready.sem, xb_ready.after(turn, ("final", s, "ln3", 0)))
                        else:
                            sp.wait_ge(d_done.sem, d_done.after(turn, ("ff_out", s, "ff", 0)))
                        sp.sem_inc(settled, 1)
                        sp.dma_start(res["out"](turn - 1 if late[Here.place] else turn, s), (xb if wide or res["final_ln"] else xn)[s][:, :, :])\
                          .then_inc(stored[s].sem, 16)

            body(0, "first")
            with sp.Fori(1, TURNS - 1) as turn:
                body(turn, "middle")
            body(TURNS - 1, "middle", prefetch=False)
            body(TURNS, "last")
            for s in range(PAIR):
                sp.wait_ge(stored[s].sem, 1 + TURNS * stored[s].per_turn + stored[s].step * sum(stored[s].late))

        @block.gpsimd
        def _(g):
            w = Seen()
            k = [0]

            def link(ins):
                k[0] += 1
                ins.then_inc(setup_g, 1)

            for t, v in res["zero"]:
                link(nc.gpsimd.memset(t, v))
            for s in range(PAIR):
                link(nc.gpsimd.memset(v_aug[s][:, :, :, :], 0.0))
                link(nc.gpsimd.memset(nm_t[s][:, :], 0.0))
                if wide:
                    link(nc.gpsimd.memset(kmask3[s][:, :, :], 0.0))
            g.wait_ge(setup_g, k[0])
            for s in range(PAIR):
                link(nc.gpsimd.memset(v_aug[s][:, :, :, D:D + 1], 1.0))
                g.wait_ge(setup_g, k[0])
                link(nc.gpsimd.memset(kstack[s][KS:KS + PARTS, :], 1.0))
                g.wait_ge(setup_g, k[0])
            g.wait_ge(setup_dma, 16 * res["n_setup"])
            for dst, x, y in res["sums"]:
                link(nc.gpsimd.tensor_tensor(dst, x, y, ALU.add))
            g.wait_ge(setup_g, k[0])
            res["setup_total"] = k[0]

            def body(turn, mode):
                w.last = {}
                for kind, s, key, a, j in steps(mode):
                    tag = (kind, s, key, j)
                    if kind == "stats":
                        if w.new(moments_ready, tag):
                            g.wait_ge(moments_ready.sem, moments_ready.after(turn, tag))
                        settle(g)
                        nc.gpsimd.tensor_scalar(veps[s][:, :], meanvar[s][:, :, 1], a["eps"], None,
                                                ALU.add).then_inc(pool_step.sem, 1)
                        g.wait_ge(pool_step.sem, pool_step.after(turn, tag))
                        nc.gpsimd.tensor_tensor(rstd[s][:, :], veps[s][:, :], res["half"][:, 0:QT],
                                                                  ALU.pow).then_inc(rstd_ready.sem, 1)
                    if kind in ("norm", "turn", "final") and a.get("xb"):
                        how, src, m1, m2 = a["xb"]
                        if res["final_ln"]:
                            if w.new(stored[s], stored[s].tags[0]):
                                g.wait_ge(stored[s].sem, stored[s].after(turn, stored[s].tags[0]))
                        if how == "add":
                            if src == "x_in":
                                g.wait_ge(loaded[s], per_load * turn + per_load)
                                x = x_in[s]
                            else:
                                x = xn[s]
                                if w.new(d_done, a["sum_tag"]):
                                    g.wait_ge(d_done.sem, d_done.after(turn, a["sum_tag"]))
                            ins = nc.gpsimd.tensor_tensor(xb[s][:, :, :], x[:, :, :],
                                                          m2[:, None, :].broadcast_to((P, QT, C)), ALU.add)
                            ins.then_inc(xb_ready.sem, 1)
                        else:
                            if w.new(xhat_ready, tag):
                                g.wait_ge(xhat_ready.sem, xhat_ready.after(turn, tag))
                            settle(g)
                            nc.gpsimd.tensor_tensor(xb[s][:, :, :], xh[s][:, :, :],
                                                    m1[:, None, :].broadcast_to((P, QT, C)), ALU.mult)\
                              .then_inc(pool_step.sem, 1)
                            g.wait_ge(pool_step.sem, pool_step.after(turn, tag))
                            nc.gpsimd.tensor_tensor(xb[s][:, :, :], xb[s][:, :, :],
                                                                    m2[:, None, :].broadcast_to((P, QT, C)), ALU.add).then_inc(xb_ready.sem, 1)
                    if kind in ("project_q", "project_k"):
                        i = 0 if kind == "project_q" else 1
                        nt = a.nk if i else T
                        x32 = (q32, k32)[i][s][:, :, 0:nt]
                        if w.new(mid_ready, tag):
                            g.wait_ge(mid_ready.sem, mid_ready.after(turn, tag))
                        nc.gpsimd.tensor_tensor(part_cols(s, i, 2, nt), x32, part_cols(s, i, 1, nt), ALU.subtract).then_inc(lo_ready.sem, 1)

            body(0, "first")
            with g.Fori(1, TURNS) as turn:
                body(turn, "middle")
            body(TURNS, "last")

        @block.scalar
        def _(act_e):
            w = Seen()
            act_e.wait_ge(setup_dma, 16 * res["n_setup"])
            act_e.wait_ge(setup_g, res["n_setup_g"])

            def affine(out, in_, scale, bias):
                return nc.scalar.activation(out, in_, ACT.Identity, scale=scale, bias=bias)

            def body(turn, mode):
                w.last = {}
                for kind, s, key, a, j in steps(mode):
                    tag = (kind, s, key, j)
                    if tag in a_full.at:
                        if w.new(a_full, tag):
                            act_e.wait_ge(a_full.sem, a_full.after(turn, tag))
                        bank = slot_of("a", tag)
                    if kind == "context":
                        nc.scalar.activation(ct[s][:, :, :], bank[:, 0:FT * S2].rearrange(
                            "p (f t) -> p f t", f=FT), ACT.Copy).then_inc(a_done.sem, 1)
                    elif kind == "norm":
                        for f in range(FT):
                            ins = affine(ht[s][:, f, :], bank[:, f * T:(f + 1) * T], a["g"][:, f:f + 1], a["b"][:, f:f + 1])
                        ins.then_inc(a_done.sem, 1)
                    elif kind == "turn":
                        nc.scalar.activation(ht[s][:, :, :], bank[:, :].rearrange(
                            "p (f t) -> p f t", f=FT), ACT.Copy).then_inc(a_done.sem, 1)
                    elif kind in ("project_q", "project_k"):
                        i = 0 if kind == "project_q" else 1
                        nt = a.nk if i else T
                        if i and a.after:
                            if w.new(d_done, ("normalise", s, a.after, 1)):
                                act_e.wait_ge(d_done.sem, d_done.after(turn, ("normalise", s, a.after, 1)))
                        bias = (a.q, a.k)[i][1]
                        src = bank[:, 0:FT * nt].rearrange("p (f t) -> p f t", f=FT)
                        dst = (q32, k32)[i][s]
                        if bias is None:
                            ins = nc.scalar.activation(dst[:, :, 0:nt], src, ACT.Copy)
                        else:
                            for f in range(FT):
                                ins = nc.scalar.activation(dst[:, f, 0:nt], src[:, f, :], ACT.Identity,
                                                           bias=bias[:, f:f + 1])
                        ins.then_inc(a_done.sem, 1)
                    elif kind == "project_q3":
                        nc.scalar.activation(q3[s][:, 2 * j:2 * j + 2, :], bank[:, :].rearrange(
                            "p (f t) -> p f t", f=2), ACT.Copy).then_inc(a_done.sem, 1)
                    elif kind == "project_k3":
                        for odd in range(2):
                            r = slice(64 * odd, 64 * odd + 64)
                            ins = nc.scalar.activation(kmask3[s][r, 8 * j + odd:8 * j + 8:2, :],
                                                       bank[r, 0:4 * S2].rearrange("p (f t) -> p f t", f=4), ACT.Copy)
                        ins.then_inc(a_done.sem, 1)
                    elif kind == "scores_exp":
                        if a.cross:
                            n, rows = 2 * T, S2
                        else:
                            n, rows = (T + P if a.kind == "causal" else 2 * T), P
                        nc.scalar.activation(probs[s][0:rows, j % slots, 0:n], bank[0:rows, 0:n], ACT.Exp,
                                                              scale=a.scale).then_inc(a_done.sem, 1)
                    elif kind == "probs_v":
                        heads = a.exp_units()[a.sum_units()[j][-1]]
                        per = 8 if a.d == D else 4
                        if (heads[-1] + 1) % per == 0:
                            n = heads[-1] // per
                            ot = (kind, s, key, n)
                            if w.new(o_full, ot):
                                act_e.wait_ge(o_full.sem, o_full.after(turn, ot))
                            nc.scalar.activation(ot_raw[s][:, 512 * n:512 * n + 512],
                                                                  slot_of("o", ot)[:, :], ACT.Copy).then_inc(o_done.sem, 1)
                    elif kind == "ff_in":
                        for f in range(2):
                            b = a["b"][:, 2 * j + f:2 * j + f + 1]
                            src = bank[:, f * T:(f + 1) * T]
                            if act == "relu":
                                ins = nc.scalar.activation(ffh[s][:, 2 * j + f, :], src, ACT.Relu, bias=b)
                            else:
                                if f == 0 and j >= 2:
                                    if w.new(ff_ready, ("ff_mid", s, key, j - 2)):
                                        act_e.wait_ge(ff_ready.sem, ff_ready.after(turn, ("ff_mid", s, key, j - 2)))
                                nc.scalar.activation(g32[s][:, j % 2, 0, f, :], src, ACT.Identity, bias=b)
                                ins = nc.scalar.activation(g32[s][:, j % 2, 1, f, :], src, ACT.Square, bias=b)
                        ins.then_inc(a_done.sem, 1)
                    elif kind == "ff_mid" and act == "gelu":
                        if w.new(poly_ready, ("ff_in", s, key, j)):
                            act_e.wait_ge(poly_ready.sem, poly_ready.after(turn, ("ff_in", s, key, j)))
                        nc.scalar.activation(g32[s][:, j % 2, 1, :, :], g32[s][:, j % 2, 1, :, :],
                                                               ACT.Tanh, scale=GELU_C).then_inc(tanh_ready.sem, 1)

            body(0, "first")
            with act_e.Fori(1, TURNS) as turn:
                body(turn, "middle")
            body(TURNS, "last")

        @block.vector
        def _(dve):
            w = Seen()
            dve.wait_ge(setup_dma, 16 * res["n_setup"])
            dve.wait_ge(setup_g, res["n_setup_g"])
            v = nc.vector
            k = 0
            for ins in res["dve_setup"](v):
                k += 1
                ins.then_inc(setup_v, 1)
            assert k == res["n_setup_v"]
            dve.wait_ge(setup_v, k)

            def body(turn, mode):
                w.last = {}
                for kind, s, key, a, j in steps(mode):
                    tag = (kind, s, key, j)
                    if kind == "stats":
                        if a["src"] == "x_in":
                            dve.wait_ge(loaded[s], per_load * turn + per_load)
                        x = x_in[s] if a["src"] == "x_in" else xn[s]
                        for t in range(QT):
                            ins = v.bn_stats(moments[s][:, t, :], x[:, t, :])
                        ins.then_inc(dve_step.sem, 1)
                        dve.wait_ge(dve_step.sem, dve_step.after(turn, tag + (0,)))
                        settle(dve)
                        for t in range(QT):
                            ins = v.bn_aggr(meanvar[s][:, t, :], moments[s][:, t, :])
                        ins.then_inc(moments_ready.sem, 1)
                    elif kind in ("norm", "final"):
                        if w.new(moments_ready, ("stats", s, key, 0)):
                            dve.wait_ge(moments_ready.sem, moments_ready.after(turn, ("stats", s, key, 0)))
                        if w.new(rstd_ready, ("stats", s, key, 0)):
                            dve.wait_ge(rstd_ready.sem, rstd_ready.after(turn, ("stats", s, key, 0)))
                        x = x_in[s] if a["src"] == "x_in" else xn[s]
                        for t in range(QT):
                            ins = v.tensor_scalar(xh[s][:, t, :], x[:, t, :], meanvar[s][:, t, 0:1], rstd[s][:, t:t + 1],
                                                  ALU.subtract, ALU.mult)
                        ins.then_inc(xhat_ready.sem, 1)
                    elif kind == "mask":
                        dve.wait_ge(loaded[s], per_load * turn + per_load)
                        v.tensor_scalar(m_rows[s][:, :, :], m_in[s][:, :, :], 0.0, -BIG,
                                                          ALU.not_equal, ALU.mult).then_inc(mask_ready.sem, 1)
                        if w.new(d_full, tag):
                            dve.wait_ge(d_full.sem, d_full.after(turn, tag))
                        v.tensor_copy(m_cols[s][:, :], slot_of("d", tag)[0:S2, 0:T // 2].bitcast(BF16)).then_inc(d_done.sem, 1)
                    elif kind in ("project_q", "project_k"):
                        i = 0 if kind == "project_q" else 1
                        nt = a.nk if i else T
                        x32 = (q32, k32)[i][s][:, :, 0:nt]
                        pt = [part_cols(s, i, n, nt) for n in range(PARTS)]
                        if w.new(a_done, tag):
                            dve.wait_ge(a_done.sem, a_done.after(turn, tag))
                        v.tensor_copy(pt[0], x32).then_inc(hi_ready.sem, 1)
                        if w.new(hi_ready, tag):
                            dve.wait_ge(hi_ready.sem, hi_ready.after(turn, tag))
                        v.tensor_tensor(x32, x32, pt[0], ALU.subtract).then_inc(rest_ready.sem, 1)
                        if w.new(rest_ready, tag):
                            dve.wait_ge(rest_ready.sem, rest_ready.after(turn, tag))
                        v.tensor_copy(pt[1], x32).then_inc(mid_ready.sem, 1)
                    elif kind == "project_v":
                        if w.new(d_full, tag):
                            dve.wait_ge(d_full.sem, d_full.after(turn, tag))
                        bank = slot_of("d", tag)
                        kt, rows = (1, S2) if a.cross else (QT, P)
                        src = bank[0:rows, 0:kt * C].rearrange("p (k h d) -> p k h d", k=kt, d=D)
                        dst = v_aug[s][0:rows, 0:kt, :, 0:D]
                        if a.v_bias is None:
                            ins = v.tensor_copy(dst, src)
                        else:
                            for t in range(kt):
                                ins = v.tensor_tensor(dst[:, t], src[:, t],
                                                      a.v_bias[0:rows, :].rearrange("p (h d) -> p h d", d=D), ALU.add)
                        ins.then_inc(d_done.sem, 1)
                    elif kind == "project_v3":
                        if w.new(d_full, tag):
                            dve.wait_ge(d_full.sem, d_full.after(turn, tag))
                        v.tensor_copy(v3[s][:, 512 * j:512 * j + 512], slot_of("d", tag)[0:S2, :]).then_inc(d_done.sem, 1)
                    elif kind == "scores_max":
                        t, heads, nk = a.max_jobs()[j]
                        if w.new(d_full, tag):
                            dve.wait_ge(d_full.sem, d_full.after(turn, tag))
                        bank = slot_of("d", tag)
                        first, apart = (stack_place(heads[0]), FT) if a.d == D else (heads[0], 1)
                        v.tensor_reduce(mx[s][:, t, first:first + apart * len(heads) - apart + 1:apart],
                                                         bank[:, 0:len(heads) * nk].rearrange("p (h k) -> p h k", k=nk),
                                                         AX_X, ALU.max).then_inc(d_done.sem, 1)
                    elif kind == "negate_max":
                        lim = 2.0 ** 90 if a.masked == "each" else 3.0e38
                        if w.new(d_done, ("scores_max", s, key, len(a.max_jobs()) - 1)):
                            dve.wait_ge(d_done.sem, d_done.after(turn, ("scores_max", s, key, len(a.max_jobs()) - 1)))
                        pt = nm_parts[s]
                        v.tensor_scalar(nmf[s][:, :, :], mx[s][:, :, :], -1.0, lim, ALU.mult, ALU.min).then_inc(dve_step.sem, 1)
                        dve.wait_ge(dve_step.sem, dve_step.after(turn, tag + (0,)))
                        v.tensor_copy(pt[:, :, 0, :], nmf[s][:, :, :]).then_inc(dve_step.sem, 1)
                        dve.wait_ge(dve_step.sem, dve_step.after(turn, tag + (1,)))
                        v.tensor_tensor(nmf[s][:, :, :], nmf[s][:, :, :], pt[:, :, 0, :], ALU.subtract).then_inc(dve_step.sem, 1)
                        dve.wait_ge(dve_step.sem, dve_step.after(turn, tag + (2,)))
                        v.tensor_copy(pt[:, :, 1, :], nmf[s][:, :, :]).then_inc(dve_step.sem, 1)
                        dve.wait_ge(dve_step.sem, dve_step.after(turn, tag + (3,)))
                        v.tensor_tensor(pt[:, :, 2, :], nmf[s][:, :, :], pt[:, :, 1, :], ALU.subtract).then_inc(negmax_ready.sem, 1)
                        if w.new(d_full, tag):
                            dve.wait_ge(d_full.sem, d_full.after(turn, tag))
                        v.tensor_copy(nm_t[s][0:PARTS * H, :],
                                                       slot_of("d", tag)[0:PARTS * H, 0:T // 2].bitcast(BF16)).then_inc(d_done.sem, 1)
                    elif kind == "probs_v":
                        if tag in den_full[s].at:
                            if w.new(den_full[s], tag):
                                dve.wait_ge(den_full[s].sem, den_full[s].after(turn, tag))
                            v.reciprocal(rden[s][0:H, :], den_bank[s][0:H, :]).then_inc(den_done[s].sem, 1)
                    elif kind == "denominators":
                        if w.new(d_full, tag):
                            dve.wait_ge(d_full.sem, d_full.after(turn, tag))
                        v.reciprocal(rden[s][:, :], slot_of("d", tag)[:, 0:T]).then_inc(d_done.sem, 1)
                    elif kind == "normalise":
                        if w.new(o_done, ("probs_v", s, key, j)):
                            dve.wait_ge(o_done.sem, o_done.after(turn, ("probs_v", s, key, j)))
                        if w.new(d_full, tag):
                            dve.wait_ge(d_full.sem, d_full.after(turn, tag))
                        v.tensor_tensor(ot_n[s][:, 2 * j:2 * j + 2, :], otr[s][:, 2 * j:2 * j + 2, :],
                                        slot_of("d", tag)[:, :].rearrange("p (g t) -> p g t", g=2),
                                        ALU.mult).then_inc(d_done.sem, 1)
                    elif kind == "normalise3":
                        if w.new(o_done, ("probs_v", s, key, j)):
                            dve.wait_ge(o_done.sem, o_done.after(turn, ("probs_v", s, key, j)))
                        if w.new(d_full, tag):
                            dve.wait_ge(d_full.sem, d_full.after(turn, tag))
                        v.tensor_tensor(ot_n3[s][:, 2 * j:2 * j + 2, :],
                                                         ot_raw[s][:, 512 * j:512 * j + 512].rearrange("p (g t) -> p g t", g=2),
                                                         slot_of("d", tag)[:, :].rearrange("p (g t) -> p g t", g=2),
                                                         ALU.mult).then_inc(d_done.sem, 1)
                    elif kind in ("project_out", "ff_out"):
                        if w.new(d_full, tag):
                            dve.wait_ge(d_full.sem, d_full.after(turn, tag))
                        bank = slot_of("d", tag)[:, :].rearrange("p (t c) -> p t c", t=QT)
                        half = kind == "ff_out" and act == "gelu"
                        if kind == "project_out" and a.res == "x_in":
                            other = x_in[s]
                        else:
                            other = xb[s]
                            if w.new(xb_ready, res["xb_for"][s, kind, key]):
                                dve.wait_ge(xb_ready.sem, xb_ready.after(turn, res["xb_for"][s, kind, key]))
                        if not (wide or res["final_ln"]):
                            if w.new(stored[s], stored[s].tags[0]):
                                dve.wait_ge(stored[s].sem, stored[s].after(turn, stored[s].tags[0]))
                        if half:
                            ins = v.scalar_tensor_tensor(xn[s][:, :, :], bank, 0.5, other[:, :, :], ALU.mult, ALU.add)
                        else:
                            ins = v.tensor_tensor(xn[s][:, :, :], bank, other[:, :, :], ALU.add)
                        ins.then_inc(d_done.sem, 1)
                        if w.new(d_done, tag):
                            dve.wait_ge(d_done.sem, d_done.after(turn, tag))
                    elif kind == "ff_in" and act == "gelu":
                        if w.new(a_done, tag):
                            dve.wait_ge(a_done.sem, a_done.after(turn, tag))
                        x, sq = g32[s][:, j % 2, 0], g32[s][:, j % 2, 1]
                        v.tensor_scalar(sq, sq, GELU_A, 1.0, ALU.mult, ALU.add).then_inc(dve_step.sem, 1)
                        dve.wait_ge(dve_step.sem, dve_step.after(turn, tag + (0,)))
                        v.tensor_tensor(sq, sq, x, ALU.mult).then_inc(poly_ready.sem, 1)
                    elif kind == "ff_mid" and act == "gelu":
                        if w.new(tanh_ready, tag):
                            dve.wait_ge(tanh_ready.sem, tanh_ready.after(turn, tag))
                        v.scalar_tensor_tensor(ffh[s][:, 2 * j:2 * j + 2, :], g32[s][:, j % 2, 1], 1.0,
                                                               g32[s][:, j % 2, 0], ALU.add, ALU.mult).then_inc(ff_ready.sem, 1)

            body(0, "first")
            with dve.Fori(1, TURNS) as turn:
                body(turn, "middle")
            body(TURNS, "last")

        @block.tensor
        def _(pe):
            w = Seen()
            pe.wait_ge(setup_dma, 16 * res["n_setup"])
            pe.wait_ge(setup_g, res["n_setup_g"])
            pe.wait_ge(setup_v, res["n_setup_v"])
            ident, identb = res["ident"], res["identb"]
            sel_gather, sel_head = res["sel_gather"], res["sel_head"]

            def mm(out, lhsT, rhs, first):
                return nc.tensor.matmul(out, lhsT, rhs, start=first, stop=True, skip_group_check=True)

            def body(turn, mode):
                w.last = {}

                def take(r, tag):
                    n = full[r].at[tag]
                    if n < len(rings[r]):
                        if w.new(done[r]):
                            pe.wait_ge(done[r].sem, done[r].before(turn))
                    else:
                        if w.new(done[r], full[r].tags[n - len(rings[r])]):
                            pe.wait_ge(done[r].sem, done[r].after(turn, full[r].tags[n - len(rings[r])]))
                    return slot_of(r, tag)

                for kind, s, key, a, j in steps(mode):
                    tag = (kind, s, key, j)
                    if kind == "context":
                        pe.wait_ge(loaded[s], per_load * turn + per_load)
                        bank = take("a", tag)
                        for f in range(FT):
                            ins = nc.tensor.transpose(bank[:, f * S2:(f + 1) * S2], c_in[s][:, f * P:(f + 1) * P],
                                                      ident[0:S2, 0:S2])
                        ins.then_inc(a_full.sem, 1)
                    elif kind in ("norm", "turn"):
                        if kind == "norm":
                            if w.new(xhat_ready, tag):
                                pe.wait_ge(xhat_ready.sem, xhat_ready.after(turn, tag))
                            x = xh[s]
                        else:
                            pe.wait_ge(loaded[s], per_load * turn + per_load)
                            x = x_in[s]
                        bank = take("a", tag)
                        for f in range(FT):
                            for t in range(QT):
                                ins = nc.tensor.transpose(bank[:, f * T + t * P:f * T + (t + 1) * P],
                                                          x[:, t, f * P:(f + 1) * P], ident[:, :])
                        ins.then_inc(a_full.sem, 1)
                    elif kind == "mask":
                        if w.new(mask_ready, tag):
                            pe.wait_ge(mask_ready.sem, mask_ready.after(turn, tag))
                        bank = take("d", tag)
                        for t in range(QT):
                            ins = nc.tensor.transpose(bank[0:S2, t * P // 2:(t + 1) * P // 2].bitcast(BF16),
                                                      m_rows[s][:, t, :], identb[:, :])
                        ins.then_inc(d_full.sem, 1)
                    elif kind in ("project_q", "project_k", "project_q3", "project_k3", "ff_in"):
                        if kind == "ff_in":
                            wt, x, xt, nt, n, fs = a["w"], ht[s], a["x_tag"], T, 2, (2 * j, 2 * j + 2)
                        elif kind in ("project_q", "project_q3"):
                            wt, x, xt, nt, n = a.q[0], ht[s], a.q[2], T, 2
                            fs = (2 * j, 2 * j + 2) if kind == "project_q3" else (0, FT)
                        else:
                            src = "c" if a.cross else "h"
                            wt, x, nt, xt = a.k[0], (ct if a.cross else ht)[s], a.nk, a.k[2]
                            fs = (4 * j, 4 * j + 4) if kind == "project_k3" else (0, FT)
                        if w.new(a_done, (xt[0], s) + xt[1:]):
                            pe.wait_ge(a_done.sem, a_done.after(turn, (xt[0], s) + xt[1:]))
                        bank = take("a", tag)
                        for m, f in enumerate(range(*fs)):
                            for c in range(FT):
                                ins = mm(bank[:, m * nt:(m + 1) * nt], wt[:, c, f * P:(f + 1) * P], x[:, c, 0:nt], c == 0)
                        ins.then_inc(a_full.sem, 1)
                    elif kind in ("project_v", "project_v3"):
                        xt = a.v[2]
                        if w.new(a_done, (xt[0], s) + xt[1:]):
                            pe.wait_ge(a_done.sem, a_done.after(turn, (xt[0], s) + xt[1:]))
                        bank = take("d", tag)
                        if kind == "project_v3":
                            for c in range(FT):
                                ins = mm(bank[0:S2, :], ct[s][:, c, :], a.v[0][:, c, 512 * j:512 * j + 512], c == 0)
                        else:
                            kt, rows = (1, S2) if a.cross else (QT, P)
                            x = (ct if a.cross else ht)[s]
                            for t in range(kt):
                                for c in range(FT):
                                    ins = mm(bank[0:rows, t * C:(t + 1) * C], x[:, c, t * rows:(t + 1) * rows],
                                             a.v[0][:, c, :], c == 0)
                        ins.then_inc(d_full.sem, 1)
                    elif kind == "scores_max":
                        t, heads, nk = a.max_jobs()[j]
                        if j == 0 and a.d == D:
                            if w.new(stacks["project_q", s], ("project_q", s, key, 0)):
                                pe.wait_ge(stacks["project_q", s].sem, stacks["project_q", s].after(turn, ("project_q", s, key, 0)))
                            if w.new(stacks["project_k", s], ("project_k", s, key, 0)):
                                pe.wait_ge(stacks["project_k", s].sem, stacks["project_k", s].after(turn, ("project_k", s, key, 0)))
                        elif j == 0:
                            if w.new(a_done, ("project_k3", s, key, FT3 // 4 - 1)):
                                pe.wait_ge(a_done.sem, a_done.after(turn, ("project_k3", s, key, FT3 // 4 - 1)))
                            if w.new(a_done, ("project_q3", s, key, FT3 // 2 - 1)):
                                pe.wait_ge(a_done.sem, a_done.after(turn, ("project_q3", s, key, FT3 // 2 - 1)))
                        bank = take("d", tag)
                        if a.d == D:
                            for n, h in enumerate(heads):
                                ins = mm(bank[:, n * nk:(n + 1) * nk], qs[s][0:KS, stack_place(h), t * P:(t + 1) * P],
                                         ks[s][a.nk][0:KS, stack_place(h), 0:nk], n == 0)
                        else:
                            for n in range(0, len(heads), 2):
                                h = heads[n]
                                ins = mm(bank[:, n * nk:(n + 2) * nk], q3[s][:, h // 2, t * P:(t + 1) * P],
                                         kmask3[s][:, h:h + 2, :], n == 0)
                        n = len(heads)
                        whole = bank[:, 0:n * nk].rearrange("p (h k) -> p h k", k=nk)
                        if a.kind == "causal":
                            ins = mm(whole[:, :, nk - P:nk], identb[:, :],
                                     res["causal_rows"][:, None, :].broadcast_to((P, n, P)), False)
                        elif a.masked == "all":
                            ins = mm(whole, identb[:, :], res["mask_rows"][:, t, None, :].broadcast_to((P, n, nk)), False)
                        elif a.masked == "each":
                            if j == 0:
                                if w.new(mask_ready, ("mask", s, "mask", 0)):
                                    pe.wait_ge(mask_ready.sem, mask_ready.after(turn, ("mask", s, "mask", 0)))
                            ins = mm(whole, identb[:, :], m_rows[s][:, t, None, :].broadcast_to((P, n, nk)), False)
                        ins.then_inc(d_full.sem, 1)
                    elif kind == "negate_max":
                        if w.new(negmax_ready, tag):
                            pe.wait_ge(negmax_ready.sem, negmax_ready.after(turn, tag))
                        bank = take("d", tag)
                        settle(pe)
                        for t in range(QT):
                            ins = nc.tensor.transpose(bank[0:PARTS * H, t * P // 2:(t + 1) * P // 2].bitcast(BF16),
                                                      nm_parts[s][:, t, :, :].rearrange("p a h -> p (a h)"), identb[:, :])
                        ins.then_inc(d_full.sem, 1)
                    elif kind == "scores_exp":
                        if j == 0 and a.d == D:
                            if w.new(nm_rows[s], ("negate_max", s, key, 0)):
                                pe.wait_ge(nm_rows[s].sem, nm_rows[s].after(turn, ("negate_max", s, key, 0)))
                            if ("project_k", s, key, 0) in ones_rows[s].at:
                                if w.new(ones_rows[s], ("project_k", s, key, 0)):
                                    pe.wait_ge(ones_rows[s].sem, ones_rows[s].after(turn, ("project_k", s, key, 0)))
                        if j == 0:
                            if a.d != D:
                                if w.new(d_done, ("negate_max", s, key, 0)):
                                    pe.wait_ge(d_done.sem, d_done.after(turn, ("negate_max", s, key, 0)))
                            if a.masked == "each":
                                if w.new(d_done, ("mask", s, "mask", 0)):
                                    pe.wait_ge(d_done.sem, d_done.after(turn, ("mask", s, "mask", 0)))
                        bank = take("a", tag)
                        heads = a.exp_units()[j]
                        at, kq = stack_place(heads[0]), slice(0, KS + PARTS)
                        if a.cross:
                            for n, h in enumerate(heads):
                                out = bank[0:S2, n * T:(n + 1) * T]
                                if a.d == D:
                                    ins = mm(out, ks[s][a.nk][kq, stack_place(h), :], qs[s][kq, stack_place(h), :], n == 0)
                                else:
                                    mm(out, kmask3[s][:, h, :], q3[s][:, h // 2, :], n == 0)
                            if a.d != D:
                                for n, h in enumerate(heads):
                                    ins = mm(bank[0:S2, n * T:(n + 1) * T], res["sel"][:, h, 0:S2], nm_t[s][:, :], False)
                            if a.masked == "each":
                                ins = mm(bank[0:S2, :].rearrange("p (h t) -> p h t", h=2), identb[0:S2, 0:S2],
                                         m_cols[s][:, None, :].broadcast_to((S2, 2, T)), False)
                        elif a.kind == "causal":
                            mm(bank[:, 0:T], ks[s][a.nk][kq, at, 0:P], qs[s][kq, at, :], True)
                            mm(bank[:, T:T + P], ks[s][a.nk][kq, at, P:T], qs[s][kq, at, P:T], False)
                            ins = mm(bank[:, :].rearrange("p (k t) -> p k t", k=2)[:, :, 0:P], identb[:, :],
                                     res["causal_cols"][:, None, :].broadcast_to((P, 2, P)), False)
                        else:
                            for t in range(QT):
                                mm(bank[:, t * T:(t + 1) * T], ks[s][a.nk][kq, at, t * P:(t + 1) * P], qs[s][kq, at, :], t == 0)
                            ins = mm(bank[:, :], identb[:, :], res["mask_cols"][:, :, :].rearrange("p k t -> p (k t)"), False)
                        ins.then_inc(a_full.sem, 1)
                    elif kind == "probs_v":
                        taken = a.sum_units()[j]
                        if w.new(a_done, ("scores_exp", s, key, taken[-1])):
                            pe.wait_ge(a_done.sem, a_done.after(turn, ("scores_exp", s, key, taken[-1])))
                        if j == 0:
                            vt = "project_v" if a.d == D else "project_v3"
                            if w.new(d_done, (vt, s, key, 0 if a.d == D else 1)):
                                pe.wait_ge(d_done.sem, d_done.after(turn, (vt, s, key, 0 if a.d == D else 1)))
                        if a.d == D:
                            first = j * HG
                            ot = (kind, s, key, first // 8)
                            if first % 8 == 0:
                                take("o", ot)
                            half = slot_of("o", ot)[:, (j % 2) * T:(j % 2) * T + T]
                            for t in range(1 if a.cross else QT):
                                for n in range(HG):
                                    h, keys = first + n, S2 if a.cross else P
                                    unit, at = (taken[n // 2], n % 2) if a.cross else (taken[n], t)
                                    since = P if a.kind == "causal" and t else 0
                                    ins = mm(half[32 * n:32 * n + 32, since:T], v_aug[s][0:keys, t, h, :],
                                             probs[s][0:keys, unit % slots, at * T:at * T + T - since], t == 0)
                            if first % 8 == HG:
                                ins.then_inc(o_full.sem, 1)
                        else:
                            for n, h in enumerate(a.exp_units()[j]):
                                pr = probs[s][:, j % slots, :]
                                ot = (kind, s, key, h // 4)
                                if h % 4 == 0:
                                    take("o", ot)
                                if h == 0:
                                    take(f"den{s}", (kind, s, key, H // 2 - 1))
                                ins = mm(den_bank[s], res["onehot"][0:S2, 31 - h:63 - h], pr[0:S2, n * T:(n + 1) * T], h == 0)
                                if h == H - 1:
                                    ins.then_inc(den_full[s].sem, 1)
                                half = (h // 2) % 2
                                out = slot_of("o", ot)[64 * (h % 2):64 * (h % 2) + 64, half * T:(half + 1) * T]
                                ins = mm(out, v3[s][:, h * D3:(h + 1) * D3], pr[0:S2, n * T:(n + 1) * T], True)
                                if h % 4 == 3:
                                    ins.then_inc(o_full.sem, 1)
                    elif kind == "denominators":
                        if w.new(o_done, ("probs_v", s, key, 1)):
                            pe.wait_ge(o_done.sem, o_done.after(turn, ("probs_v", s, key, 1)))
                        bank = take("d", tag)
                        for n in range(G):
                            ins = mm(bank[32 * n:32 * n + 32, 0:T], sel_gather[:, :], otr[s][:, n, :], True)
                        ins.then_inc(d_full.sem, 1)
                    elif kind == "normalise":
                        if w.new(d_done, ("denominators", s, key, 0)):
                            pe.wait_ge(d_done.sem, d_done.after(turn, ("denominators", s, key, 0)))
                        bank = take("d", tag)
                        for n in range(2):
                            ins = mm(bank[:, n * T:(n + 1) * T], sel_head[:, 2 * j + n, :], rden[s][:, :], n == 0)
                        ins.then_inc(d_full.sem, 1)
                    elif kind == "normalise3":
                        if j == 0:
                            if w.new(den_done[s], ("probs_v", s, key, H // 2 - 1)):
                                pe.wait_ge(den_done[s].sem, den_done[s].after(turn, ("probs_v", s, key, H // 2 - 1)))
                        bank = take("d", tag)
                        for n in range(2):
                            ins = mm(bank[:, n * T:(n + 1) * T], res["sel_pair"][:, 2 * j + n, :], rden[s][0:H, :], n == 0)
                        ins.then_inc(d_full.sem, 1)
                    elif kind in ("project_out", "ff_out"):
                        if kind == "ff_out":
                            wt, x, n = a["w"], ffh[s], 8
                            if act == "gelu":
                                if w.new(ff_ready, ("ff_mid", s, key, 3)):
                                    pe.wait_ge(ff_ready.sem, ff_ready.after(turn, ("ff_mid", s, key, 3)))
                            else:
                                if w.new(a_done, ("ff_in", s, key, 3)):
                                    pe.wait_ge(a_done.sem, a_done.after(turn, ("ff_in", s, key, 3)))
                        else:
                            wt, n = a.o, (G if a.d == D else FT3)
                            x = ot_n[s] if a.d == D else ot_n3[s]
                            if w.new(d_done, (("normalise", s, key, 1) if a.d == D else ("normalise3", s, key, 3))):
                                pe.wait_ge(d_done.sem, d_done.after(turn, (("normalise", s, key, 1) if a.d == D else ("normalise3", s, key, 3))))
                        bank = take("d", tag)
                        for t in range(QT):
                            for c in range(n):
                                ins = mm(bank[:, t * C:(t + 1) * C], x[:, c, t * P:(t + 1) * P], wt[:, c, :], c == 0)
                        ins.then_inc(d_full.sem, 1)

            body(0, "first")
            with pe.Fori(1, TURNS) as turn:
                body(turn, "middle")
            body(TURNS, "last")


def build(nc, ins, out):
    x1 = nc.dram_tensor("between_0_1", (NB, T, C), F32).ap()
    x2 = nc.dram_tensor("between_1_2", (NB, T, C), F32).ap()
    scratch = nc.dram_tensor("parts", (PAIR, 2, SLOTS, P, FT * T), BF16).ap()

    ones = nc.dram_tensor("ones", (PARTS, H * T), BF16).ap()

    def rows(t, turn, s):
        v = t.rearrange("(i s) (q p) c -> i s p q c", s=PAIR, p=P)
        return v[turn, s]

    def context(turn, s):
        return ins["ctx_1024"].rearrange("(i s) t c -> i s t c", s=PAIR)[turn, s]

    def common(ctx, name, want):
        def sb(n, shape, dt=F32):
            return ctx.enter_context(nc.sbuf_tensor(f"{name}_{n}", shape, dt))
        r = {"scratch": scratch, "ones": ones, "zero": [], "weight_loads": [], "sums": [], "sb": sb, "name": name}
        r["ident"] = sb("ident", [P, P])
        r["identb"] = sb("identb", [P, P], BF16)
        r["sel_gather"], r["sel_head"] = sb("sel_gather", [P, 32]), sb("sel_head", [P, G, P])
        r["half"] = sb("half", [P, QT])
        r["zero"].append((r["half"][:, :], -0.5))
        return r

    def weight(r, n, src, width=None):
        k, m = src.shape
        t = r["sb"](n, [P, k // P, m])
        r["weight_loads"].append((t[:, :, :], src.rearrange("(c p) n -> p c n", p=P)))
        return t

    def padded(r, n, src):
        t = r["sb"](n, [P, G, C])
        v = src.rearrange("(g j d) n -> j d g n", j=HG, d=D)
        for j in range(HG):
            r["weight_loads"].append((t[32 * j:32 * j + D, :, :], v[j]))
        r["padded"].append(t)
        return t

    def column(r, n, src):
        k = src.shape[0] // P
        t = r["sb"](n, [P, k])
        r["weight_loads"].append((t[:, :], src.rearrange("(c p) -> p c", p=P)))
        return t

    def spread(r, n, src):
        t = r["sb"](n, [P, C])
        r["weight_loads"].append((t[:, :], src.partition_broadcast(P)))
        return t

    def prepare(r, name):
        with ExitStack() as c:
            zeroed = c.enter_context(nc.semaphore(f"{name}_zeroed"))
            made = c.enter_context(nc.semaphore(f"{name}_made"))
            block = c.enter_context(nc.Block())

            @block.gpsimd
            def _(g):
                n = 0
                for t in [r["ident"], r["identb"], r["sel_gather"], r["sel_head"]] + r["padded"] + r["selectors"]:
                    nc.gpsimd.memset(t[tuple(slice(None) for _ in t.shape)], 0.0).then_inc(zeroed, 1)
                    n += 1
                g.wait_ge(zeroed, n)
                k = 0

                def select(v, op, fill, base, pattern, mult):
                    nonlocal k
                    nc.gpsimd.affine_select(out=v, in_=v, compare_op=op, fill=fill, base=base, pattern=pattern,
                                            channel_multiplier=mult).then_inc(made, 1)
                    k += 1
                    g.wait_ge(made, k)

                for t in (r["ident"], r["identb"]):
                    select(t[:, :], ALU.not_equal, 1.0, 0, [[-1, P]], 1)
                select(r["sel_gather"][:, :].rearrange("p (n j) -> p n j", j=HG), ALU.not_equal, 1.0, -D,
                       [[0, 32 // HG], [-32, HG]], 1)
                select(r["sel_head"][:, :, :].rearrange("p g (j d) -> p g j d", j=HG), ALU.not_equal, 1.0, 0,
                       [[-32, G], [-1, HG], [0, 32]], 1)
                if "causal_rows" in r:
                    select(r["causal_rows"][:, :], ALU.is_ge, -BIG, 0, [[-1, P]], 1)
                    select(r["causal_cols"][:, :], ALU.is_ge, -BIG, 0, [[1, P]], -1)
                if "onehot" in r:
                    for part in range(PARTS):
                        select(r["sel"][:, :, :], ALU.not_equal, 1.0, -H * part, [[-1, H], [0, P]], 1)
                    nc.gpsimd.memset(r["onehot"][:, 31:32], 1.0).then_inc(made, 1)
                    k += 1
                    select(r["sel_pair"][:, :, :].rearrange("p a (b d) -> p a b d", b=2), ALU.not_equal, 1.0, 0,
                           [[-2, FT3], [-1, 2], [0, D3]], 1)
                g.wait_ge(made, k)

    def xb_tags(streams):
        last, found = {}, {}
        for s in range(PAIR):
            for kind, _, key, a, j in streams[s]:
                if kind in ("norm", "turn", "final") and a.get("xb"):
                    last[s] = (kind, s, key, j)
                if kind in ("project_out", "ff_out"):
                    found[s, kind, key] = last.get(s)
        return found

    with ExitStack() as ctx:
        r = common(ctx, "l0", None)
        r["padded"], sb = [], r["sb"]
        r["causal_rows"], r["causal_cols"] = sb("causal_rows", [P, P], BF16), sb("causal_cols", [P, P], BF16)
        r["selectors"] = [r["causal_rows"], r["causal_cols"]]
        i = {k[len("L0_xattn_"):]: v for k, v in ins.items() if k.startswith("L0_")}
        w_q0, w_k0, w_q, w_k, w_v = (weight(r, n, i[m]) for n, m in (("w_q0", "q0"), ("w_k0", "k0"), ("wq", "Wq"),
                                                                     ("wk", "Wk"), ("wv", "Wv")))
        w_v0 = weight(r, "w_v0", i["W_attn"][:, 2 * C:3 * C])
        w_ao, w_co = padded(r, "w_ao", i["W_aproj"]), padded(r, "w_co", i["Wcproj"])
        w_fc, w_mp = weight(r, "w_fc", i["W_fc"]), weight(r, "w_mp", i["W_mproj"])
        b_attn = i["b_attn"]
        bq0, bk0 = column(r, "bq0", i["bq0"]), column(r, "bk0", i["bk0"])
        bv0 = spread(r, "bv0", b_attn[2 * C:3 * C])
        bq, bk, bv = column(r, "bq", i["bq"]), column(r, "bk", i["bk"]), spread(r, "bv", i["bv"])
        b_ao, b_co, b_mp = (spread(r, n, i[m]) for n, m in (("b_ao", "b_aproj"), ("b_co", "bcproj"), ("b_mp", "b_mproj")))
        b_fc = column(r, "b_fc", i["b_fc"])
        g1, b1, g2, b2 = (column(r, n, i[n]) for n in ("ln1_g", "ln1_b", "ln2_g", "ln2_b"))
        prepare(r, "l0p")
        streams = []
        for s in range(PAIR):
            h0, h1, c = ("norm", "ln0", 0), ("norm", "ln1", 0), ("context", "ctx", 0)
            own = Att("own", "causal", (w_q0, bq0, h0), (w_k0, bk0, h0), (w_v0, None, h0), w_ao, v_bias=bv0)
            other = Att("other", "cross", (w_q, bq, h1), (w_k, bk, c), (w_v, None, c), w_co, v_bias=bv, after="own")
            n0 = dict(src="x_in", eps=1e-5, g=g1, b=b1, xb=("add", "x_in", None, b_ao))
            n1 = dict(src="xn", eps=1e-5, g=g1, b=b1, xb=("add", "xn", None, b_co), sum_tag=("project_out", s, "own", 0))
            n2 = dict(src="xn", eps=1e-5, g=g2, b=b2, xb=("add", "xn", None, b_mp), sum_tag=("project_out", s, "other", 0))
            u = [("context", s, "ctx", None, 0), ("stats", s, "ln0", n0, 0), ("norm", s, "ln0", n0, 0)]
            u += att_units(s, own, other) + [("stats", s, "ln1", n1, 0), ("norm", s, "ln1", n1, 0)]
            u += att_units(s, other) + [("stats", s, "ln2", n2, 0), ("norm", s, "ln2", n2, 0)]
            f = dict(w=w_fc, b=b_fc, x_tag=("norm", "ln2", 0))
            for j in range(5):
                if j < 4:
                    u.append(("ff_in", s, "ff", f, j))
                if j:
                    u.append(("ff_mid", s, "ff", f, j - 1))
            u += [("ff_out", s, "ff", dict(w=w_mp), 0), ("store", s, "x", None, 0)]
            streams.append(u)
        r.update(wide=False, loads=2, final_ln=False, x=lambda t, s: rows(ins["x"], t, s), ctx=context,
                 out=lambda t, s: rows(x1, t, s), prefetch_at=("project_v", "own"), n_setup=len(r["weight_loads"]),
                 x_readers=lambda s, c: [(c["xhat"], ("norm", s, "ln0", 0)), (c["xb"], ("norm", s, "ln0", 0)),
                                         (c["a"], ("context", s, "ctx", 0))],
                 n_setup_g=len(r["zero"]) + 4 * PAIR, n_setup_v=0, dve_setup=lambda v: [],
                 xb_for=xb_tags(streams), late_from="ff_inff")
        run_pass(nc, "l0", streams, r, "gelu")

    with ExitStack() as ctx:
        r = common(ctx, "l1", None)
        r["padded"], sb = [], r["sb"]
        r["selectors"] = []
        i = {k[len("L1_xattn_"):]: v for k, v in ins.items() if k.startswith("L1_")}
        wt = {n: weight(r, n, i[n + "_w"]) for n in ("q", "k", "v", "cq", "ck", "cv")}
        w_o, w_co = padded(r, "w_o", i["o_w"]), padded(r, "w_co", i["co_w"])
        w_1, w_2 = weight(r, "w_1", i["lin1_w"]), weight(r, "w_2", i["lin2_w"])
        col = {n: column(r, "c_" + n, i[n]) for n in ("q_b", "k_b", "cq_b", "ck_b", "lin1_b", "ln1_g", "ln1_b", "ln2_g", "ln2_b")}
        spr = {n: spread(r, "s_" + n, i[n]) for n in ("v_b", "cv_b", "o_b", "co_b", "lin2_b", "ln1_g", "ln1_b", "ln2_g",
                                                      "ln2_b", "ln3_g", "ln3_b")}
        r["sums"] = [(spr["ln1_b"][:, :], spr["ln1_b"][:, :], spr["co_b"][:, :]),
                     (spr["ln2_b"][:, :], spr["ln2_b"][:, :], spr["lin2_b"][:, :])]
        mask_i, mask_j = sb("mask_i", [P, QT, T], I32), sb("mask_j", [P, QT, T], I32)
        r["mask_rows"], r["mask_cols"] = sb("mask_rows", [P, QT, T], BF16), sb("mask_cols", [P, QT, T], BF16)
        m = ins["mask_SxS_ik1"]
        r["weight_loads"].append((mask_i[:, :, :], m.rearrange("(q p) k -> p q k", p=P)))
        r["weight_loads"].append((mask_j[:, :, :], ins["mask_by_key"].rearrange("(k p) q -> p k q", p=P)))
        prepare(r, "l1p")

        def masks(v):
            return [v.tensor_scalar(r["mask_rows"][:, :, :], mask_i[:, :, :], 0.0, -BIG, ALU.not_equal, ALU.mult),
                    v.tensor_scalar(r["mask_cols"][:, :, :], mask_j[:, :, :], 0.0, -BIG, ALU.not_equal, ALU.mult)]

        streams = []
        for s in range(PAIR):
            h0, h1, c = ("turn", "in", 0), ("norm", "ln1", 0), ("context", "ctx", 0)
            own = Att("own", "self", (wt["q"], col["q_b"], h0), (wt["k"], col["k_b"], h0), (wt["v"], None, h0), w_o,
                      masked="all", v_bias=spr["v_b"])
            other = Att("other", "cross", (wt["cq"], col["cq_b"], h1), (wt["ck"], col["ck_b"], c), (wt["cv"], None, c),
                        w_co, v_bias=spr["cv_b"], after="own")
            n1 = dict(src="xn", eps=1e-5, g=col["ln1_g"], b=col["ln1_b"], xb=("scale", None, spr["ln1_g"], spr["ln1_b"]))
            n2 = dict(src="xn", eps=1e-5, g=col["ln2_g"], b=col["ln2_b"], xb=("scale", None, spr["ln2_g"], spr["ln2_b"]))
            n3 = dict(src="xn", eps=1e-5, xb=("scale", None, spr["ln3_g"], spr["ln3_b"]))
            u = [("context", s, "ctx", None, 0), ("turn", s, "in", dict(xb=("add", "x_in", None, spr["o_b"])), 0)]
            u += att_units(s, own, other) + [("stats", s, "ln1", n1, 0), ("norm", s, "ln1", n1, 0)]
            u += att_units(s, other) + [("stats", s, "ln2", n2, 0), ("norm", s, "ln2", n2, 0)]
            u += [("ff_in", s, "ff", dict(w=w_1, b=col["lin1_b"], x_tag=("norm", "ln2", 0)), j) for j in range(4)]
            u += [("ff_out", s, "ff", dict(w=w_2), 0), ("stats", s, "ln3", n3, 0), ("final", s, "ln3", n3, 0),
                  ("store", s, "x", None, 0)]
            streams.append(u)
        r.update(wide=False, loads=2, final_ln=True, x=lambda t, s: rows(x1, t, s), ctx=context,
                 out=lambda t, s: rows(x2, t, s), prefetch_at=("project_v", "own"), n_setup=len(r["weight_loads"]),
                 x_readers=lambda s, c: [(c["xb"], ("turn", s, "in", 0)), (c["a"], ("turn", s, "in", 0)),
                                         (c["a"], ("context", s, "ctx", 0))],
                 n_setup_g=len(r["zero"]) + 4 * PAIR + 2, n_setup_v=2, dve_setup=masks,
                 xb_for=xb_tags(streams), late_from="ff_inff")
        run_pass(nc, "l1", streams, r, "relu")

    with ExitStack() as ctx:
        r = common(ctx, "l2", None)
        r["padded"], sb = [], r["sb"]
        r["onehot"], r["sel_pair"] = sb("onehot", [P, 63]), sb("sel_pair", [H, FT3, P])
        r["sel"] = sb("sel", [P, H, P], BF16)
        r["selectors"] = [r["onehot"], r["sel_pair"], r["sel"]]
        i = {k[3:]: v for k, v in ins.items() if k.startswith(("L2_", "L3_"))}
        w2 = {n: weight(r, "2" + n, ins["L2_xattn_w" + n]) for n in "qkv"}
        w2o = padded(r, "2o", ins["L2_xattn_wo"])
        w3 = {n: weight(r, "3" + n, ins["L3_xattn_w_" + n]) for n in ("q", "k", "v", "fc")}
        g2, b2 = column(r, "g2", ins["L2_xattn_gamma"]), column(r, "b2", ins["L2_xattn_beta"])
        g2s, b2s = spread(r, "g2s", ins["L2_xattn_gamma"]), spread(r, "b2s", ins["L2_xattn_beta"])
        g3s, b3s = spread(r, "g3s", ins["L3_xattn_ln_gamma"]), spread(r, "b3s", ins["L3_xattn_ln_beta"])
        prepare(r, "l2p")
        streams = []
        for s in range(PAIR):
            h0, h1, c = ("turn", "in", 0), ("norm", "ln2", 0), ("context", "ctx", 0)
            a2 = Att("two", "cross", (w2["q"], None, h0), (w2["k"], None, c), (w2["v"], None, c), w2o, masked="each",
                     res="x_in", slots=3)
            a3 = Att("three", "cross", (w3["q"], None, h1), (w3["k"], None, c), (w3["v"], None, c), w3["fc"], d=D3, slots=3)
            n2 = dict(src="xn", eps=1e-5, g=g2, b=b2, xb=("scale", None, g2s, b2s))
            n3 = dict(src="xn", eps=1e-6, xb=("scale", None, g3s, b3s))
            u = [("context", s, "ctx", None, 0), ("turn", s, "in", {}, 0), ("mask", s, "mask", None, 0)]
            u += att_units(s, a2, a3) + [("stats", s, "ln2", n2, 0), ("norm", s, "ln2", n2, 0)]
            u += att_units(s, a3) + [("stats", s, "ln3", n3, 0), ("final", s, "ln3", n3, 0), ("store", s, "x", None, 0)]
            streams.append(u)
        mask = ins["mask_BxSxS2_bk1"].rearrange("(i s) (q p) k -> i s p q k", s=PAIR, p=P)
        r.update(wide=True, loads=3, final_ln=True, x=lambda t, s: rows(x2, t, s), ctx=context,
                 mask=lambda t, s: mask[t, s], out=lambda t, s: rows(out, t, s), prefetch_at=("project_out", "two"),
                 n_setup=len(r["weight_loads"]),
                 x_readers=lambda s, c: [(c["d"], ("project_out", s, "two", 0)), (c["a"], ("turn", s, "in", 0)),
                                         (c["a"], ("context", s, "ctx", 0)), (c["mask"], ("mask", s, "mask", 0))],
                 n_setup_g=len(r["zero"]) + 5 * PAIR, n_setup_v=0, dve_setup=lambda v: [],
                 xb_for=xb_tags(streams), late_from="project_outthree")
        run_pass(nc, "l2", streams, r, None)


def kernel(**inputs):
    import numpy as _np
    import concourse.bacc as _bacc
    from concourse import mybir as _mybir
    from concourse.bass_utils import run_bass_kernel_spmd as _run

    nc = _bacc.Bacc("TRN2", target_bir_lowering=False, num_devices=1)
    arrays, aps = {}, {}
    inputs["mask_by_key"] = _np.asarray(inputs["mask_SxS_ik1"]).T
    for part, name in enumerate(("q0", "k0")):
        inputs[f"L0_xattn_{name}"] = _np.asarray(inputs["L0_xattn_W_attn"])[:, part * C:(part + 1) * C]
        inputs[f"L0_xattn_b{name}"] = _np.asarray(inputs["L0_xattn_b_attn"])[part * C:(part + 1) * C]
    for name in ("L0_xattn_q0", "L0_xattn_k0", "L0_xattn_bq0", "L0_xattn_bk0", "L0_xattn_Wq", "L0_xattn_Wk", "L0_xattn_bq",
                 "L0_xattn_bk", "L1_xattn_q_w", "L1_xattn_k_w", "L1_xattn_cq_w", "L1_xattn_ck_w", "L1_xattn_q_b",
                 "L1_xattn_k_b", "L1_xattn_cq_b", "L1_xattn_ck_b", "L2_xattn_wq", "L2_xattn_wk"):
        a = _np.asarray(inputs[name])
        inputs[name] = a.reshape(*a.shape[:-1], FT, H // FT, D).swapaxes(-1, -2).reshape(a.shape)
    for name, a in inputs.items():
        a = _np.ascontiguousarray(a)
        arrays[f"in_{name}"] = a
        aps[name] = nc.dram_tensor(f"in_{name}", a.shape, _mybir.dt.from_np(a.dtype), kind="ExternalInput").ap()
    out = nc.dram_tensor("out_0", (NB, T, C), F32, kind="ExternalOutput").ap()
    build(nc, aps, out)
    r = _run(nc, [arrays], core_ids=[0])
    return r.results[0]["out_0"]
```
